# Optimizing a Trainium2 kernel written in Bass

```python
import numpy as np
import jax
import jax.numpy as jnp

def _softmax(x, axis=-1):
    return jax.nn.softmax(x, axis=axis)

def _gelu(x):
    return jax.nn.gelu(x, approximate=True)

def _silu(x):
    return jax.nn.silu(x)

def _sigmoid(x):
    return jax.nn.sigmoid(x)

def _layernorm(x, axis=-1, eps=1e-05):
    m = jnp.mean(x, axis=axis, keepdims=True)
    v = jnp.var(x, axis=axis, keepdims=True)
    return (x - m) / jnp.sqrt(v + eps)

def _scatter_add(tgt, idx, src, axis=0):
    return tgt.at[idx].add(src)

def _segment_sum(src, seg, n):
    return jax.ops.segment_sum(src, seg, n)
kernel_name = 'mk_pixart_resid_d2_seqx_r4_76b3ec'

def setup_inputs(seed: int=0):
    np.random.seed(seed)
    _w = jnp.asarray

    def _rec_inputs():
        import jax
        import jax.numpy as jnp
        _rk = jax.random.key(seed)
        x = 7.22e-05 + 1 * jax.random.normal(jax.random.fold_in(_rk, 1), (1, 2048, 256), jnp.float32)
        _lenS = 2048 - jax.random.randint(jax.random.fold_in(_rk, 7), (1,), 0, max(1, 2048 // 4) + 1, jnp.int32)
        _lenS2 = 1601 - jax.random.randint(jax.random.fold_in(_rk, 8), (1,), 0, max(1, 1601 // 4) + 1, jnp.int32)
        _ctx_1024P = jax.random.normal(jax.random.fold_in(_rk, 11), (1, 16, 256), jnp.float32)
        _ctx_1024c = jax.random.dirichlet(jax.random.fold_in(_rk, 511), 0.3 * jnp.ones((16,), jnp.float32), (1, 1601))
        _ctx_1024t = jnp.einsum('bsk,bkd->bsd', _ctx_1024c, _ctx_1024P)
        _ctx_1024t = _ctx_1024t * jax.lax.rsqrt(jnp.mean(jnp.square(_ctx_1024t)) + 1e-12) * 0.953939
        ctx_1024 = 4.13588e-05 + 0.999923 * (_ctx_1024t + 0.3 * jax.random.normal(jax.random.fold_in(_rk, 611), (1, 1601, 256), jnp.float32))
        condB_tau = jax.random.uniform(jax.random.fold_in(_rk, 12), (1,), jnp.float32, 0.0, 1.45372)
        fside_BxS2_0 = 0.0088954 + 1.00633 * jax.random.normal(jax.random.fold_in(_rk, 13), (1, 1601), jnp.float32)
        condB_pt = jax.random.uniform(jax.random.fold_in(_rk, 15), (1,), jnp.float32, 0.0, 226.919)
        return (x, ctx_1024, condB_tau, fside_BxS2_0, condB_pt, _lenS2)
    x, ctx_1024, condB_tau, fside_BxS2_0, condB_pt, _lenS2 = _rec_inputs()

    def _L0_xcond_setup():
        import jax, jax.numpy as jnp
        import numpy as np
        D_MODEL = 256
        N_HEADS = 16
        key = jax.random.key(seed)
        ks = jax.random.split(key, 16)
        B, L, S, D = (4, 512, 512, D_MODEL)
        inp = {'q': jax.random.normal(ks[0], (B, L, D), jnp.float32), 'k': jax.random.normal(ks[1], (B, S, D), jnp.float32), 'v': jax.random.normal(ks[2], (B, S, D), jnp.float32), 'tau': jax.random.uniform(ks[3], (B, 1), jnp.float32, 0.5, 1.5), 'delta': jax.random.normal(ks[4], (B, S), jnp.float32)}
        s = 1.0 / np.sqrt(D)
        inp['Wq'] = jax.random.normal(ks[5], (D, D), jnp.float32) * s
        inp['bq'] = jnp.zeros((D,), jnp.float32)
        inp['Wk'] = jax.random.normal(ks[6], (D, D), jnp.float32) * s
        inp['bk'] = jnp.zeros((D,), jnp.float32)
        inp['Wv'] = jax.random.normal(ks[7], (D, D), jnp.float32) * s
        inp['bv'] = jnp.zeros((D,), jnp.float32)
        inp['Wo'] = jax.random.normal(ks[8], (D, D), jnp.float32) * s
        inp['bo'] = jnp.zeros((D,), jnp.float32)
        return inp
    _L0_xcond_all = _L0_xcond_setup()
    _L0_xcond_in = {k: v for k, v in _L0_xcond_all.items() if k in ('Wq', 'bq', 'Wk', 'bk', 'Wv', 'bv', 'Wo', 'bo')}
    del _L0_xcond_all

    def _L0_ffn_setup():
        import jax, jax.numpy as jnp
        import numpy as np
        B, S, D, E = (2, 512, 256, 8)
        key = jax.random.key(seed)
        ks = jax.random.split(key, 5)
        x = jax.random.normal(ks[0], (B, S, D), dtype=jnp.float32)
        router_w = jax.random.normal(ks[1], (E, D), dtype=jnp.float32) * 0.02
        router_b = jnp.zeros((E,), dtype=jnp.float32)
        expert_w = jax.random.normal(ks[2], (E, D, D), dtype=jnp.float32) * 0.02
        expert_b = jnp.zeros((E, D), dtype=jnp.float32)
        return {'x': x, 'router_w': router_w, 'router_b': router_b, 'expert_w': expert_w, 'expert_b': expert_b}
    _L0_ffn_all = _L0_ffn_setup()
    _L0_ffn_in = {k: v for k, v in _L0_ffn_all.items() if k in ('router_w', 'router_b', 'expert_w', 'expert_b')}
    del _L0_ffn_all

    def _L1_xcond_setup():
        import jax, jax.numpy as jnp
        import numpy as np
        N, L, H, Q = (64, 258, 256, 64)
        WINDOW = 16.0
        DEV_POW = 128.0
        key = jax.random.key(seed)
        k1, k2, k3, k4, k5, k6 = jax.random.split(key, 6)
        encoder_outputs = jax.random.normal(k1, (N, L, H), dtype=jnp.float32)
        decoder_h_t = jax.random.normal(k2, (N, Q, H), dtype=jnp.float32)
        src_len = jax.random.randint(k3, (N,), 32, L + 1).astype(jnp.int32)
        p_t = jax.random.uniform(k4, (N,), dtype=jnp.float32) * (src_len.astype(jnp.float32) - 1.0)
        W_a = jax.random.normal(k5, (H, H), dtype=jnp.float32) * (1.0 / np.sqrt(H))
        W_c = jax.random.normal(k6, (H, 2 * H), dtype=jnp.float32) * (1.0 / np.sqrt(2 * H))
        return {'encoder_outputs': encoder_outputs, 'decoder_h_t': decoder_h_t, 'src_len': src_len, 'p_t': p_t, 'W_a': W_a, 'W_c': W_c}
    _L1_xcond_all = _L1_xcond_setup()
    _L1_xcond_in = {k: v for k, v in _L1_xcond_all.items() if k in ('W_a', 'W_c')}
    del _L1_xcond_all

    def _L1_ffn_setup():
        import jax, jax.numpy as jnp
        import numpy as np
        B, T, D = (8, 1024, 256)
        NUM_SLOTS = 64
        TOP_K = 8
        DQ = D // 4
        DH = D // 2

        def _forward(x, slot_init, w1, b1, w2, b2, tau, Wih, Whh, bih, bhh, wq, bq, wk, bk, wv, bv, ln_g, ln_b, wvp, bvp, wo, bo):
            Bx, Tx, Dx = x.shape
            S = jnp.broadcast_to(slot_init[None], (Bx, NUM_SLOTS, Dx)).astype(x.dtype)
            slot_mean = jnp.broadcast_to(S.mean(axis=1, keepdims=True), (Bx, Tx, Dx))
            ctx = jnp.concatenate([x, slot_mean], axis=-1)
            h = jax.nn.gelu(ctx @ w1 + b1, approximate=False)
            route_logits = (h @ w2 + b2) / (jnp.abs(tau) + 0.1)
            topk_vals, topk_idx = jax.lax.top_k(route_logits, TOP_K)
            topk_w = jax.nn.softmax(topk_vals, axis=-1)
            alpha = (jax.nn.one_hot(topk_idx, NUM_SLOTS, dtype=x.dtype) * topk_w[..., None]).sum(axis=-2)
            slot_input = jnp.einsum('bts,btd->bsd', alpha, x)
            denom = alpha.sum(axis=1) + 1e-08
            si = slot_input / denom[..., None]
            gi = si @ Wih.T + bih
            gh = S @ Whh.T + bhh
            i_r, i_z, i_n = jnp.split(gi, 3, axis=-1)
            h_r, h_z, h_n = jnp.split(gh, 3, axis=-1)
            r = jax.nn.sigmoid(i_r + h_r)
            z = jax.nn.sigmoid(i_z + h_z)
            n = jnp.tanh(i_n + r * h_n)
            S_new = (1.0 - z) * n + z * S
            q = S_new @ wq + bq
            k = S_new @ wk + bk
            v = S_new @ wv + bv
            scale = DQ ** (-0.5)
            attn = jax.nn.softmax(jnp.einsum('bsq,btq->bst', q, k) * scale, axis=-1)
            S_comm = jnp.einsum('bst,btd->bsd', attn, v)
            y = S_new + S_comm
            mu = y.mean(axis=-1, keepdims=True)
            var = y.var(axis=-1, keepdims=True)
            y = (y - mu) * jax.lax.rsqrt(var + 1e-05) * ln_g + ln_b
            slot_values = y @ wvp + bvp
            out = jnp.einsum('bts,bsd->btd', alpha, slot_values)
            return out @ wo + bo
        key = jax.random.key(seed)
        ks = jax.random.split(key, 24)
        n = lambda k, shp, s=0.02: jax.random.normal(k, shp, dtype=jnp.float32) * s
        return {'x': jax.random.normal(ks[0], (B, T, D), dtype=jnp.float32), 'slot_init': n(ks[1], (NUM_SLOTS, D)), 'w1': n(ks[2], (2 * D, DH)), 'b1': jnp.zeros((DH,)), 'w2': n(ks[3], (DH, NUM_SLOTS)), 'b2': jnp.zeros((NUM_SLOTS,)), 'tau': jnp.ones((1,)), 'Wih': n(ks[4], (3 * D, D)), 'Whh': n(ks[5], (3 * D, D)), 'bih': jnp.zeros((3 * D,)), 'bhh': jnp.zeros((3 * D,)), 'wq': n(ks[6], (D, DQ)), 'bq': jnp.zeros((DQ,)), 'wk': n(ks[7], (D, DQ)), 'bk': jnp.zeros((DQ,)), 'wv': n(ks[8], (D, D)), 'bv': jnp.zeros((D,)), 'ln_g': jnp.ones((D,)), 'ln_b': jnp.zeros((D,)), 'wvp': n(ks[9], (D, D)), 'bvp': jnp.zeros((D,)), 'wo': n(ks[10], (D, D)), 'bo': jnp.zeros((D,))}
    _L1_ffn_all = _L1_ffn_setup()
    _L1_ffn_in = {k: v for k, v in _L1_ffn_all.items() if k in ('slot_init', 'w1', 'b1', 'w2', 'b2', 'tau', 'Wih', 'Whh', 'bih', 'bhh', 'wq', 'bq', 'wk', 'bk', 'wv', 'bv', 'ln_g', 'ln_b', 'wvp', 'bvp', 'wo', 'bo')}
    del _L1_ffn_all
    return {'x': x, 'ctx_1024': ctx_1024, 'condB_tau': condB_tau, 'fside_BxS2_0': fside_BxS2_0, 'condB_pt': condB_pt, '_lenS2': _lenS2, 'L0_xcond_Wq': _L0_xcond_in['Wq'], 'L0_xcond_bq': _L0_xcond_in['bq'], 'L0_xcond_Wk': _L0_xcond_in['Wk'], 'L0_xcond_bk': _L0_xcond_in['bk'], 'L0_xcond_Wv': _L0_xcond_in['Wv'], 'L0_xcond_bv': _L0_xcond_in['bv'], 'L0_xcond_Wo': _L0_xcond_in['Wo'], 'L0_xcond_bo': _L0_xcond_in['bo'], 'L0_ffn_router_w': _L0_ffn_in['router_w'], 'L0_ffn_router_b': _L0_ffn_in['router_b'], 'L0_ffn_expert_w': _L0_ffn_in['expert_w'], 'L0_ffn_expert_b': _L0_ffn_in['expert_b'], 'L1_xcond_W_a': _L1_xcond_in['W_a'], 'L1_xcond_W_c': _L1_xcond_in['W_c'], 'L1_ffn_slot_init': _L1_ffn_in['slot_init'], 'L1_ffn_w1': _L1_ffn_in['w1'], 'L1_ffn_b1': _L1_ffn_in['b1'], 'L1_ffn_w2': _L1_ffn_in['w2'], 'L1_ffn_b2': _L1_ffn_in['b2'], 'L1_ffn_tau': _L1_ffn_in['tau'], 'L1_ffn_Wih': _L1_ffn_in['Wih'], 'L1_ffn_Whh': _L1_ffn_in['Whh'], 'L1_ffn_bih': _L1_ffn_in['bih'], 'L1_ffn_bhh': _L1_ffn_in['bhh'], 'L1_ffn_wq': _L1_ffn_in['wq'], 'L1_ffn_bq': _L1_ffn_in['bq'], 'L1_ffn_wk': _L1_ffn_in['wk'], 'L1_ffn_bk': _L1_ffn_in['bk'], 'L1_ffn_wv': _L1_ffn_in['wv'], 'L1_ffn_bv': _L1_ffn_in['bv'], 'L1_ffn_ln_g': _L1_ffn_in['ln_g'], 'L1_ffn_ln_b': _L1_ffn_in['ln_b'], 'L1_ffn_wvp': _L1_ffn_in['wvp'], 'L1_ffn_bvp': _L1_ffn_in['bvp'], 'L1_ffn_wo': _L1_ffn_in['wo'], 'L1_ffn_bo': _L1_ffn_in['bo']}

def reference(x, ctx_1024, condB_tau, fside_BxS2_0, condB_pt, _lenS2, L0_xcond_Wq, L0_xcond_bq, L0_xcond_Wk, L0_xcond_bk, L0_xcond_Wv, L0_xcond_bv, L0_xcond_Wo, L0_xcond_bo, L0_ffn_router_w, L0_ffn_router_b, L0_ffn_expert_w, L0_ffn_expert_b, L1_xcond_W_a, L1_xcond_W_c, L1_ffn_slot_init, L1_ffn_w1, L1_ffn_b1, L1_ffn_w2, L1_ffn_b2, L1_ffn_tau, L1_ffn_Wih, L1_ffn_Whh, L1_ffn_bih, L1_ffn_bhh, L1_ffn_wq, L1_ffn_bq, L1_ffn_wk, L1_ffn_bk, L1_ffn_wv, L1_ffn_bv, L1_ffn_ln_g, L1_ffn_ln_b, L1_ffn_wvp, L1_ffn_bvp, L1_ffn_wo, L1_ffn_bo):
    import jax
    import jax.numpy as jnp

    def _L0_xcond_ref(q, k, v, tau, delta, Wq, bq, Wk, bk, Wv, bv, Wo, bo):
        import jax, jax.numpy as jnp
        import numpy as np
        D_MODEL = 256
        N_HEADS = 16
        B, L, D = q.shape
        S = k.shape[1]
        H = N_HEADS
        E = D // H
        qh = (q @ Wq.T + bq).reshape(B, L, H, E)
        kh = (k @ Wk.T + bk).reshape(B, S, H, E)
        vh = (v @ Wv.T + bv).reshape(B, S, H, E)
        scale = 1.0 / np.sqrt(E).astype(np.float32)
        scores = jnp.einsum('blhe,bshe->bhls', qh, kh)
        scores = scores * tau[:, None, None, :] + delta[:, None, None, :]
        a = jax.nn.softmax(scale * scores, axis=-1)
        out = jnp.einsum('bhls,bshd->blhd', a, vh).reshape(B, L, D)
        return out @ Wo.T + bo

    def _L0_ffn_ref(x, router_w, router_b, expert_w, expert_b):
        import jax, jax.numpy as jnp
        import numpy as np
        B, S, D, E = (2, 512, 256, 8)
        logits = jnp.einsum('bsd,ed->bse', x, router_w) + router_b
        probs = jax.nn.softmax(logits, axis=-1)
        weights = jnp.max(probs, axis=-1)
        top1 = jnp.argmax(probs, axis=-1)
        y_all = jnp.einsum('bsd,eod->bseo', x, expert_w) + expert_b
        y = jnp.take_along_axis(y_all, top1[:, :, None, None], axis=2)[:, :, 0, :]
        out = y * weights[:, :, None]
        return out

    def _L1_xcond_ref(encoder_outputs, decoder_h_t, src_len, p_t, W_a, W_c):
        import jax, jax.numpy as jnp
        import numpy as np
        N, L, H, Q = (64, 258, 256, 64)
        WINDOW = 16.0
        DEV_POW = 128.0
        n, l, h = encoder_outputs.shape
        idx = jnp.arange(l, dtype=jnp.float32)
        src_end = src_len.astype(jnp.float32)
        attn_start = jnp.maximum(p_t - WINDOW, 0.0)
        attn_end = jnp.minimum(p_t + WINDOW, src_end)
        mask = (idx[None, :] < attn_start[:, None]) | (idx[None, :] > attn_end[:, None])
        score = jnp.einsum('nqh,hk,nlk->nql', decoder_h_t, W_a, encoder_outputs)
        score = jnp.where(mask[:, None, :], -1000000000.0, score)
        align = jax.nn.softmax(score, axis=2)
        gauss = jnp.exp(-(idx[None, :] - p_t[:, None]) ** 2 / DEV_POW)
        align = align * gauss[:, None, :]
        context = jnp.einsum('nql,nlh->nqh', align, encoder_outputs)
        cat = jnp.concatenate([context, decoder_h_t], axis=2)
        return jnp.tanh(cat @ W_c.T)

    def _L1_ffn_ref(x, slot_init, w1, b1, w2, b2, tau, Wih, Whh, bih, bhh, wq, bq, wk, bk, wv, bv, ln_g, ln_b, wvp, bvp, wo, bo):
        import jax, jax.numpy as jnp
        import numpy as np
        B, T, D = (8, 1024, 256)
        NUM_SLOTS = 64
        TOP_K = 8
        DQ = D // 4
        DH = D // 2

        def _forward(x, slot_init, w1, b1, w2, b2, tau, Wih, Whh, bih, bhh, wq, bq, wk, bk, wv, bv, ln_g, ln_b, wvp, bvp, wo, bo):
            Bx, Tx, Dx = x.shape
            S = jnp.broadcast_to(slot_init[None], (Bx, NUM_SLOTS, Dx)).astype(x.dtype)
            slot_mean = jnp.broadcast_to(S.mean(axis=1, keepdims=True), (Bx, Tx, Dx))
            ctx = jnp.concatenate([x, slot_mean], axis=-1)
            h = jax.nn.gelu(ctx @ w1 + b1, approximate=False)
            route_logits = (h @ w2 + b2) / (jnp.abs(tau) + 0.1)
            topk_vals, topk_idx = jax.lax.top_k(route_logits, TOP_K)
            topk_w = jax.nn.softmax(topk_vals, axis=-1)
            alpha = (jax.nn.one_hot(topk_idx, NUM_SLOTS, dtype=x.dtype) * topk_w[..., None]).sum(axis=-2)
            slot_input = jnp.einsum('bts,btd->bsd', alpha, x)
            denom = alpha.sum(axis=1) + 1e-08
            si = slot_input / denom[..., None]
            gi = si @ Wih.T + bih
            gh = S @ Whh.T + bhh
            i_r, i_z, i_n = jnp.split(gi, 3, axis=-1)
            h_r, h_z, h_n = jnp.split(gh, 3, axis=-1)
            r = jax.nn.sigmoid(i_r + h_r)
            z = jax.nn.sigmoid(i_z + h_z)
            n = jnp.tanh(i_n + r * h_n)
            S_new = (1.0 - z) * n + z * S
            q = S_new @ wq + bq
            k = S_new @ wk + bk
            v = S_new @ wv + bv
            scale = DQ ** (-0.5)
            attn = jax.nn.softmax(jnp.einsum('bsq,btq->bst', q, k) * scale, axis=-1)
            S_comm = jnp.einsum('bst,btd->bsd', attn, v)
            y = S_new + S_comm
            mu = y.mean(axis=-1, keepdims=True)
            var = y.var(axis=-1, keepdims=True)
            y = (y - mu) * jax.lax.rsqrt(var + 1e-05) * ln_g + ln_b
            slot_values = y @ wvp + bvp
            out = jnp.einsum('bts,bsd->btd', alpha, slot_values)
            return out @ wo + bo
        return _forward(x, slot_init, w1, b1, w2, b2, tau, Wih, Whh, bih, bhh, wq, bq, wk, bk, wv, bv, ln_g, ln_b, wvp, bvp, wo, bo)
    x = x + _L0_xcond_ref(_layernorm(x, axis=-1), ctx_1024, ctx_1024, condB_tau[:, None], fside_BxS2_0, L0_xcond_Wq, L0_xcond_bq, L0_xcond_Wk, L0_xcond_bk, L0_xcond_Wv, L0_xcond_bv, L0_xcond_Wo, L0_xcond_bo)
    x = x + _L0_ffn_ref(_layernorm(x, axis=-1), L0_ffn_router_w, L0_ffn_router_b, L0_ffn_expert_w, L0_ffn_expert_b)
    x = x + _L1_xcond_ref(ctx_1024, _layernorm(x, axis=-1), _lenS2, condB_pt, L1_xcond_W_a, L1_xcond_W_c)
    x = x + _L1_ffn_ref(_layernorm(x, axis=-1), L1_ffn_slot_init, L1_ffn_w1, L1_ffn_b1, L1_ffn_w2, L1_ffn_b2, L1_ffn_tau, L1_ffn_Wih, L1_ffn_Whh, L1_ffn_bih, L1_ffn_bhh, L1_ffn_wq, L1_ffn_bq, L1_ffn_wk, L1_ffn_bk, L1_ffn_wv, L1_ffn_bv, L1_ffn_ln_g, L1_ffn_ln_b, L1_ffn_wvp, L1_ffn_bvp, L1_ffn_wo, L1_ffn_bo)
    return x

_drawn_inputs = setup_inputs


def setup_inputs(seed=0):
    import zlib

    import numpy as np

    out = dict(_drawn_inputs(seed))
    spreads = {'L0_xcond_bq': (0.0, 0.549),
     'L0_xcond_bk': (0.0, 2.0),
     'L0_xcond_bv': (0.0, 0.1),
     'L0_xcond_bo': (0.0, 0.1),
     'L0_ffn_router_b': (0.0, 0.1),
     'L0_ffn_expert_b': (0.0, 0.346),
     'L1_ffn_b1': (0.0, 2.0),
     'L1_ffn_b2': (0.0, 2.0),
     'L1_ffn_bih': (0.0, 0.1),
     'L1_ffn_bhh': (0.0, 0.408),
     'L1_ffn_bq': (0.0, 2.0),
     'L1_ffn_bk': (0.0, 2.0),
     'L1_ffn_bv': (0.0, 0.1),
     'L1_ffn_ln_g': (1.0, 0.6),
     'L1_ffn_ln_b': (0.0, 0.8),
     'L1_ffn_bvp': (0.0, 0.322),
     'L1_ffn_bo': (0.0, 0.1)}
    factors = {'fside_BxS2_0': 5.547,
     'L1_ffn_slot_init': 8.0,
     'L1_ffn_w1': 8.0,
     'L1_ffn_w2': 8.0,
     'L1_ffn_Whh': 8.0,
     'L1_ffn_wq': 64.0,
     'L1_ffn_wk': 64.0,
     'L1_ffn_wv': 4.385}
    for name, (base, spread) in spreads.items():
        noise = np.random.default_rng([zlib.crc32(name.encode()), seed]).standard_normal(out[name].shape)
        drawn = base * np.exp(spread * noise) if base else spread * noise
        out[name] = jnp.asarray(drawn.astype(out[name].dtype))
    for name, factor in factors.items():
        out[name] = (out[name] * factor).astype(out[name].dtype)
    return out
```

```python
from contextlib import ExitStack

import concourse.bass as bass
from concourse import mybir

F32 = mybir.dt.float32
BF16 = mybir.dt.bfloat16
I32 = mybir.dt.int32
ALU = mybir.AluOpType
ACT = mybir.ActivationFunctionType
AX = mybir.AxisListType

P = 128
T, D = 2048, 256
S = 1601
H, E = 16, 16
KT = D // P
CT = 512
NC = T // CT
TT = CT // P
HG = 4
NG = H // HG
ST = (S + P - 1) // P
LAST = S - (ST - 1) * P
NX = 8
W = 256
NS, TOPK = 64, 8
DQ, DH = 64, 128
SPLIT = 401
UNITS = TT * HG * 2
HALF_START = (0, S - 2 * SPLIT)
BIG = 1.0e9

Q_PART = (0, 0, 1, 1, 0, 2)
K_PART = (0, 1, 0, 1, 2, 0)
DELTA_ROW = 96
MAX_ROW = 99
ROWS = 101


def rows_of(st):
    return LAST if st == ST - 1 else P


def build(nc, io):
    with ExitStack() as ctx:
        def sb(name, shape, dt=F32):
            return ctx.enter_context(nc.sbuf_tensor(name, shape, dt))

        def ps(name, shape, dt=F32):
            return ctx.enter_context(nc.psum_tensor(name, shape, dt))

        def sem(name):
            return ctx.enter_context(nc.semaphore(name))

        q_parts = nc.dram_tensor("q_parts", (3, D, T + CT), BF16, kind="Internal").ap()
        k_parts = nc.dram_tensor("k_parts", (3, D, S), BF16, kind="Internal").ap()

        tokens = sb("tokens", [P, T // P, D])
        kst_raw = sb("k_stack", [P, H * S // 2 + 8])
        kst = kst_raw[:, 0:H * S // 2].bitcast(BF16).rearrange("p (h s) -> p h s", h=H)
        qst = sb("q_stack", [P, NG, HG, CT], BF16)
        v_sb = sb("v_heads", [P, ST, H, 32])
        probs_raw = sb("probs", [P, 2 * HG * CT])
        probs = probs_raw[:].rearrange("p (b h t) -> p b h t", b=2, h=HG)
        ctxT = probs_raw[:, 0:KT * S].rearrange("p (k s) -> p k s", k=KT)
        expert_w = sb("expert_w", [P, KT, NX * D])
        wqkv = expert_w[:].rearrange("p k n -> p (k n)")[:, 0:3 * KT * D]\
            .rearrange("p (w k n) -> p w k n", w=3, k=KT)
        attc = sb("attn_chunk", [P, NG, CT])
        o_raw = sb("o_unnormed", [P, CT])
        z_inv = sb("z_inv", [P, CT])
        wo_pad = sb("wo_pad", [P, NG, D])
        alphaT_raw = sb("alphaT", [P, T])
        alphaT = alphaT_raw[0:NS + 1, :]
        parts = alphaT_raw[:, 0:3 * CT].bitcast(BF16).rearrange("p (m a t) -> p m a t", m=2, a=3)
        xa = sb("xa", [P, TT, D])
        attc_flat = attc[:].rearrange("p g t -> p (g t)")
        xb = attc_flat[:, 0:TT * D].rearrange("p (t d) -> p t d", t=TT)
        xn = sb("xn", [P, TT, D + 1])
        xnT = sb("xnT", [P, KT, CT])
        work = sb("work", [P, TT, W])
        work2 = attc_flat[:, TT * D:].rearrange("p (t w) -> p t w", t=TT)
        hT = z_inv
        q32 = work[:].rearrange("p t w -> p (t w)").rearrange("p (m n) -> p m n", m=2)
        rest = work2.rearrange("p t w -> p (t w)").rearrange("p (m n) -> p m n", m=2)
        ident = sb("ident", [P, P])
        z_pick = sb("z_pick", [P, P])
        iota_w = z_inv[:, W:2 * W]
        keep = sb("keep", [P, W])
        gauss = sb("gauss", [P, W])
        neg_mask = sb("neg_mask", [P, W])
        win_f = sb("win_f", [P, 8])
        win_i = sb("win_i", [P, 2], I32)
        enc_win = o_raw[:].rearrange("p (k w) -> p k w", k=KT)
        win_k = sb("win_k", [P, KT, W])
        win_v = sb("win_v", [P, KT, D])
        wa_c = work2.rearrange("p t w -> p (t w)").rearrange("p (k n) -> p k n", k=KT * 2)
        wc = sb("wc", [P, 2 * KT, D])
        w1 = sb("w1", [P, 2 * KT, DH])
        w2 = sb("w2", [DH, NS])
        rw = sb("router_w", [P, KT, NX])
        rb = sb("router_b", [P, NX])
        rank = sb("rank", [P, NX])
        eb = sb("expert_b_tiles", [TT * NX, TT, D])
        bo0 = sb("bo0", [P, D])
        bv0 = z_inv[:, 0:D]
        b2 = sb("b2", [P, NS])
        b1 = sb("b1", [P, 1])
        hbias = sb("hbias", [P, 1])
        slotT = sb("slotT", [P, KT, NS])
        slot_mean = sb("slot_mean", [P, KT])
        qk_bias = sb("qk_bias", [P, 2, KT])
        tau = sb("tau", [P, 4])
        rtau = sb("rtau", [P, 2])
        q_flat = qst[:].rearrange("p g h t -> p (g h t)")
        delta3 = q_flat[0:H, 0:3 * S].rearrange("p (a s) -> p a s", a=3)
        delta_a = q_flat[0:H, 3 * S + 1:5 * S + 1].bitcast(F32)
        delta_b = expert_w[:].rearrange("p k n -> p (k n)")[0:H, 3 * KT * D:3 * KT * D + S]
        ones_sb = attc_flat[0:H, 0:1024].bitcast(BF16)
        mx = sb("mx", [P, 2, HG * TT])
        mxc = sb("mxc", [P, HG * TT])
        mrow = sb("mrow", [HG * TT, 2, P], BF16)
        bst = sb("bst", [P, TT, 6])
        mv = sb("mv", [P, TT, 2])
        var_e = sb("var_e", [P, TT])
        rstd = sb("rstd", [P, TT])
        neg_half = sb("neg_half", [P, TT])
        eps = sb("eps", [P, TT])
        lg8 = sb("lg8", [P, TT, NX])
        ex8 = sb("ex8", [P, TT, NX])
        hot8 = sb("hot8", [P, TT, NX])
        st4 = sb("st4", [P, 8, TT])
        gateT = sb("gateT", [TT * NX, P])
        rowsum = sb("rowsum", [P, TT])
        tail = sb("tail", [P, TT])
        neg_big = sb("neg_big", [P, 1])
        lg, lgr, elg, alpha = (work[:].rearrange("p t w -> p (t w)")[:, TT * NS * i:TT * NS * (i + 1)]
                               .rearrange("p (t n) -> p t n", t=TT) for i in range(4))
        top8 = sb("top8", [P, TT, TOPK])
        slot_acc = sb("slot_acc", [NS, D + 1])

        at = [0]

        def late(n_rows, *shape):
            n = 1
            for x in shape:
                n *= x
            a = kst_raw[0:n_rows, at[0]:at[0] + n]
            at[0] += n
            assert at[0] <= H * S // 2
            if len(shape) == 2:
                a = a.rearrange("p (a b) -> p a b", a=shape[0])
            return a

        wihT, whhT = late(P, KT, 3 * D), late(P, KT, 3 * D)
        wqs, wks = late(P, KT, DQ), late(P, KT, DQ)
        wvs, wvps, wos = late(P, KT, D), late(P, KT, D), late(P, KT, D)
        b_ih, b_hh = late(NS, 3 * D), late(NS, 3 * D)
        b_v, ln_g, ln_b, b_vp, slot0 = (late(NS, D) for _ in range(5))
        b_qk = late(DQ, 2)
        rz, gate_n, hid_n, s_new, comm, y_ln = late(NS, 2 * D), late(NS, D), late(NS, D), late(NS, D), late(NS, D), late(NS, D)
        vec = late(NS, D)
        sT = late(P, KT, NS)
        qkT = late(DQ, 2, NS)
        att_s = late(NS, NS)
        att_sT = late(NS, NS)
        svo = late(NS + 1, D)
        small = late(NS, 16)

        ps_e = [ps(f"ps_e{i}", [P, CT]) for i in range(2)]
        ps_m = ps("ps_m", [P, 4, CT])
        ps_o = ps("ps_o", [P, CT])
        ps_x = ps("ps_x", [P, CT])

        names = """ld_x ld_ctx ld_wqkv ld_const ld_cond ld_encwin ld_expert ld_delta ld_fill ld_k ld_slot ld_wac
            fills_set consts_set wqkv_free scr_stored_a scr_stored_b delta_parts window_start masks_ready
            blk_psum blk_hi blk_parts v_psum v_taken
            var_ready rstd_ready xn_ready xnT_psum xnT_ready
            win_psum win_copied hb_psum hb_ready mean_ready
            max_ready max_taken mx_ready mT_ready mrow_ready
            qk_ready exp_done pv_done o_taken z_ready z_taken att_ready
            xa_ready y_ready router_ready gate_ready gateT_psum gateT_ready gbias_ready gbias_added
            experts_ready experts_taken x2_ready
            score_ready negmax_ready rowsum_ready a_ready aT_psum aT_ready
            zed_ready tanh_ready h_psum h_ready lg_psum lg_taken negtop_ready elg_ready alpha_ready
            slot_psum alphaT_psum slot_taken alphaT_taken
            p_si p_siT_ps p_siT p_gi p_rz p_sig p_npre p_n p_snew p_snT_ps p_snT p_qkv p_qkT p_lg
            p_nmax p_exp p_attn p_attT_ps p_attT p_comm p_var p_rstd p_y p_yT_ps p_yT p_sv p_svb p_svT_ps p_svT
            p_svo p_svo_sb out_psum out_ready out_stored""".split()
        s = {n: sem(n) for n in names}
        q_loaded = [sem(f"q_loaded{g}") for g in range(NG)]
        m_loaded = [sem(f"m_loaded{g}") for g in range(NG)]
        block = ctx.enter_context(nc.Block())

        const_loads = [
            (ident[:], io["c_ident"]), (z_pick[:], io["c_zpick"]),
            (iota_w[:], io["c_iota"].partition_broadcast(P)), (rank[:], io["c_rank"].partition_broadcast(P)),
            (wc[:], io["L1_W_cT"].rearrange("(k p) n -> p k n", p=P)),
            (w1[:], io["w1"].rearrange("(k p) n -> p k n", p=P)),
            (w2[:], io["w2"]),
            (rw[:], io["router_wT"].rearrange("(k p) n -> p k n", p=P)),
            (rb[:], io["router_b"].partition_broadcast(P)),
            (bo0[:], io["L0_bo"].partition_broadcast(P)), 
            (bv0[:], io["L0_bv"].partition_broadcast(P)), (b2[:], io["b2"].partition_broadcast(P)),
            (b1[:], io["b1"].rearrange("(p a) -> p a", a=1)),
            (slotT[:], io["slot_initT"].rearrange("(k p) n -> p k n", p=P)),
        ]
        wo_loads = [(wo_pad[32 * j:32 * j + E, :, :],
                     io["L0_WoT"].rearrange("(g j e) n -> j e g n", g=NG, j=HG)[j]) for j in range(HG)]
        eb_loads = [(eb[NX * t:NX * t + NX, t, :], io["expert_b"]) for t in range(TT)]
        slot_loads = [
            (wihT, io["WihT"].rearrange("(k p) n -> p k n", p=P)), (whhT, io["WhhT"].rearrange("(k p) n -> p k n", p=P)),
            (wqs, io["wq"].rearrange("(k p) n -> p k n", p=P)), (wks, io["wk"].rearrange("(k p) n -> p k n", p=P)),
            (wvs, io["wv"].rearrange("(k p) n -> p k n", p=P)), (wvps, io["wvp"].rearrange("(k p) n -> p k n", p=P)),
            (wos, io["wo"].rearrange("(k p) n -> p k n", p=P)),
            (b_ih, io["bih"].partition_broadcast(NS)), (b_hh, io["bhh"].partition_broadcast(NS)),
            (b_v, io["bv"].partition_broadcast(NS)), (ln_g, io["ln_g"].partition_broadcast(NS)),
            (ln_b, io["ln_b"].partition_broadcast(NS)), (b_vp, io["bvp"].partition_broadcast(NS)),
            (slot0, io["slot_init"]), (svo[NS:NS + 1, :], io["L1_bo"].unsqueeze(0)), (b_qk[:, 0:1], io["bq"].rearrange("(p a) -> p a", a=1)),
            (b_qk[:, 1:2], io["bk"].rearrange("(p a) -> p a", a=1)),
        ]
        N_CONST = 16 * len(const_loads)
        N_FILL = 16 * (len(wo_loads) + len(eb_loads))
        KBLK = 2 * ((S + CT - 1) // CT)
        k_cols = [(i * CT, min(CT, S - i * CT)) for i in range((S + CT - 1) // CT)]

        def load_q(eng, g, chunk):
            for j in range(6):
                src = q_parts[Q_PART[j], HG * E * g:HG * E * (g + 1), bass.ds(chunk * CT, CT)]
                eng.dma_start(qst[16 * j:16 * j + 16, g, :, :], src.rearrange("(h e) t -> e h t", h=HG))\
                   .then_inc(q_loaded[g], 16)

        @block.sync
        def _(sp):
            sp.dma_start(ctxT, io["ctxT"].rearrange("(k p) s -> p k s", p=P)).then_inc(s["ld_ctx"], 16)
            for i, name in enumerate(("L0_WkT", "L0_WvT", "L0_WqT")):
                sp.dma_start(wqkv[:, i], io[name].rearrange("(k p) n -> p k n", p=P)).then_inc(s["ld_wqkv"], 16)
            sp.dma_start(tokens[:], io["x"].rearrange("(a p) d -> p a d", p=P)).then_inc(s["ld_x"], 16)
            for dst, src in const_loads:
                sp.dma_start(dst, src).then_inc(s["ld_const"], 16)
            sp.wait_ge(s["fills_set"], 1)
            for dst, src in wo_loads + eb_loads:
                sp.dma_start(dst, src).then_inc(s["ld_fill"], 16)
            sp.wait_ge(s["consts_set"], 1)
            for r in (MAX_ROW, MAX_ROW + 1):
                sp.dma_start(kst[r:r + 1, :, :], ones_sb[0:H, 0:S]).then_inc(s["ld_k"], 16)
            for g in range(NG):
                sp.dma_start(qst[DELTA_ROW:DELTA_ROW + 3, g, :, :], ones_sb[0:3, :]).then_inc(s["ld_k"], 16)
            for i, (at_col, n) in enumerate(k_cols):
                for m in range(KT):
                    sp.wait_ge(s["blk_parts"], KT * i + m + 1)
                    for a in range(3):
                        sp.dma_start(k_parts[a, P * m:P * m + P, at_col:at_col + n], parts[:, m, a, 0:n])\
                          .then_inc(s["scr_stored_a" if m == 0 else "scr_stored_b"], 16)
            sp.wait_ge(s["delta_parts"], 1)
            for a in range(3):
                sp.dma_start(kst[DELTA_ROW + a:DELTA_ROW + a + 1, :, :], delta3[:, a, :]).then_inc(s["ld_k"], 16)
            sp.wait_ge(s["scr_stored_a"], 48 * len(k_cols))
            sp.wait_ge(s["scr_stored_b"], 48 * len(k_cols))
            for j in range(6):
                sp.dma_start(kst[16 * j:16 * j + 16, :, :], k_parts[K_PART[j]].rearrange("(h e) s -> e h s", h=H))\
                  .then_inc(s["ld_k"], 16)
            with sp.Fori(0, NC) as c:
                for m in range(KT):
                    sp.wait_ge(s["blk_parts"], KBLK + 1 + m + KT * c)
                    for a in range(3):
                        sp.dma_start(q_parts[a, P * m:P * m + P, bass.ds(c * CT, CT)], parts[:, m, a, :])\
                          .then_inc(s["scr_stored_a" if m == 0 else "scr_stored_b"], 16)
            sp.wait_ge(s["scr_stored_a"], 48 * (len(k_cols) + NC))
            sp.wait_ge(s["scr_stored_b"], 48 * (len(k_cols) + NC))
            sp.dma_start(q_parts[:, :, T:T + CT], q_parts[:, :, 0:CT]).then_inc(s["scr_stored_a"], 16)
            sp.wait_ge(s["scr_stored_a"], 48 * (len(k_cols) + NC) + 16)
            sp.wait_ge(s["wqkv_free"], 1)
            for k in range(KT):
                sp.dma_start(expert_w[:, k, :], io["expert_wT"][k]).then_inc(s["ld_expert"], 16)
            sp.wait_ge(s["ld_k"], 16 * (2 + NG + 3 + 6))
            for g in range(3):
                load_q(sp, g, 0)
            sp.wait_ge(s["mrow_ready"], 1)

            def load_m(g):
                for a in range(2):
                    sp.dma_start(qst[MAX_ROW + a:MAX_ROW + a + 1, g, :, :], mrow[:, a, :]).then_inc(m_loaded[g], 16)

            load_m(0)
            with sp.Fori(0, NC) as c:
                for g in range(NG):
                    sp.wait_ge(s["mrow_ready"], NG * c + g + 2)
                    load_m((g + 1) % NG)
                    load_q(sp, (g + 3) % NG, c if g == 0 else c + 1)
            sp.wait_ge(s["slot_taken"], NC)
            for dst, src in slot_loads:
                sp.dma_start(dst, src).then_inc(s["ld_slot"], 16)
            out = io["out"].rearrange("(a p) d -> p a d", p=P)
            for c in range(NC):
                sp.wait_ge(s["out_ready"], c + 1)
                sp.dma_start(out[:, TT * c:TT * c + TT, :], tokens[:, TT * c:TT * c + TT, :]).then_inc(s["out_stored"], 16)
            for g in range(NG):
                sp.wait_ge(q_loaded[g], 96 * (NC + (g < 3)))
            sp.wait_ge(m_loaded[0], 32 * (NC + 1))
            sp.wait_ge(s["out_stored"], 16 * NC)

        @block.gpsimd
        def _(pool):
            pool.dma_start(tau[:, 0:1], io["condB_tau"].partition_broadcast(P)).then_inc(s["ld_cond"], 16)
            pool.dma_start(win_f[:, 0:1], io["condB_pt"].partition_broadcast(P)).then_inc(s["ld_cond"], 16)
            pool.dma_start(win_i[:, 0:1], io["lenS2"].partition_broadcast(P)).then_inc(s["ld_cond"], 16)
            pool.dma_start(rtau[:, 0:1], io["L1_tau"].partition_broadcast(P)).then_inc(s["ld_cond"], 16)
            for i, name in enumerate(("L0_bq", "L0_bk")):
                pool.dma_start(qk_bias[:, i, :], io[name].rearrange("(k p) -> p k", p=P),
                               allow_slow_non_contiguous=True).then_inc(s["ld_cond"], 16)
            pool.dma_start(delta_a, io["fside"].partition_broadcast(H)).then_inc(s["ld_delta"], 16)
            pool.memset(ones_sb, 1.0).then_inc(s["consts_set"], 1)
            pool.memset(wo_pad[:], 0.0)
            pool.memset(eb[:], 0.0).then_inc(s["fills_set"], 1)
            pool.memset(neg_half[:], -0.5)
            pool.memset(eps[:], 1e-5)
            pool.memset(neg_big[:], -BIG)
            pool.memset(v_sb[:], 1.0)
            pool.memset(xn[:, :, D:D + 1], 1.0)
            pool.memset(slot_acc[:], 0.0).then_inc(s["consts_set"], 1)
            pool.wait_ge(s["window_start"], 1)
            w0 = pool.value_load(win_i[0:1, 1:2], min_val=0, max_val=S - W)
            pool.dma_start(enc_win[:], io["ctxT"].rearrange("(k p) s -> p k s", p=P)[:, :, bass.ds(w0, W)])\
                .then_inc(s["ld_encwin"], 16)

            def rsqrt(n):
                pool.wait_ge(s["var_ready"], n)
                pool.tensor_tensor(var_e[:], mv[:, :, 1], eps[:], ALU.add)
                pool.drain()
                pool.tensor_tensor(rstd[:], var_e[:], neg_half[:], ALU.pow).then_inc(s["rstd_ready"], 1)

            with pool.Fori(0, NC) as c:
                rsqrt(c + 1)
            pool.wait_ge(s["blk_parts"], KBLK + KT * NC)
            pool.dma_start(wa_c[:, 0:KT, :], io["L1_W_aT"].rearrange("(k p) n -> p k n", p=P)).then_inc(s["ld_wac"], 16)
            pool.wait_ge(s["ld_const"], N_CONST)
            pool.wait_ge(s["wqkv_free"], 1)
            pool.tensor_tensor(tokens[:], tokens[:], bo0[:].unsqueeze(1).broadcast_to((P, T // P, D)), ALU.add)\
                .then_inc(s["xa_ready"], 1)
            with pool.Fori(0, NC) as c:
                for i in range(3):
                    rsqrt(NC + 3 * c + i + 1)
            pool.wait_ge(s["p_var"], 1)
            pool.tensor_scalar(small[:, 9:10], small[:, 8:9], 1e-5, None, ALU.add)
            pool.drain()
            pool.tensor_tensor(small[:, 10:11], small[:, 9:10], neg_half[0:NS, 0:1], ALU.pow).then_inc(s["p_rstd"], 1)

        @block.scalar
        def _(act):
            def block_split(b, m, n, which):
                act.wait_ge(s["blk_psum"], b + 1)
                act.activation(q32[:, m, 0:n], ps_e[m][:, 0:n], ACT.Identity,
                               bias=qk_bias[:, which, m:m + 1], scale=tau[:, 2:3] if which == 0 else 1.0)
                act.activation(parts[:, m, 0, 0:n], ps_e[m][:, 0:n], ACT.Identity,
                               bias=qk_bias[:, which, m:m + 1], scale=tau[:, 2:3] if which == 0 else 1.0)\
                   .then_inc(s["blk_hi"], 1)

            def reuse_parts(m, stored, done):
                act.wait_ge(s["scr_stored_a" if m == 0 else "scr_stored_b"], stored)
                act.wait_ge(s["blk_parts"], done)

            act.wait_ge(s["masks_ready"], 1)
            for i, (_, n) in enumerate(k_cols):
                for m in range(KT):
                    if i:
                        reuse_parts(m, 48 * i, KT * (i - 1) + m + 1)
                    block_split(KT * i + m, m, n, 1)
            act.wait_ge(s["masks_ready"], 2)
            act.activation(gauss[:], iota_w[:], ACT.Exp, scale=-1.0 / 128.0)

            def copy_xnT(n):
                act.wait_ge(s["xnT_psum"], n)
                act.copy(xnT[:], ps_m[:, 2:4, :]).then_inc(s["xnT_ready"], 1)

            with act.Fori(0, NC) as c:
                copy_xnT(c + 1)
                for m in range(KT):
                    reuse_parts(m, 48 * len(k_cols) + 48 * c, KBLK - 2 + m + 1 + KT * c)
                    block_split(KBLK + m + KT * c, m, CT, 0)
            act.wait_ge(s["win_psum"], 1)
            act.copy(win_k[:], ps_m[:, 0:2, 0:W])
            act.copy(win_v[:], ps_m[:, 2:4, 0:D]).then_inc(s["win_copied"], 1)

            with act.Fori(0, NC) as c:
                for g in range(NG):
                    for st in range(ST):
                        k = ST * g + st
                        n = rows_of(st)
                        if k >= 2:
                            act.wait_ge(s["pv_done"], NG * ST * c + k - 1)
                        for h in range(HG):
                            act.wait_ge(s["qk_ready"], NG * ST * HG * c + HG * k + h + 1)
                            act.activation(probs[0:n, k % 2, h, :], ps_e[h % 2][0:n, :], ACT.Exp)\
                               .then_inc(s["exp_done"], 1)
                copy_xnT(NC + 3 * c + 1)
                act.wait_ge(s["router_ready"], 2 * c + 2)
                act.activation(ex8[:], lg8[:], ACT.Exp).then_inc(s["elg_ready"], 1)
                act.wait_ge(s["gateT_psum"], c + 1)
                act.copy(gateT[:], ps_x[0:TT * NX, 0:P]).then_inc(s["gateT_ready"], 1)
                copy_xnT(NC + 3 * c + 2)
                act.wait_ge(s["negmax_ready"], c + 1)
                act.activation(tail[:], st4[:, 0, :], ACT.Exp, bias=neg_big[:, 0:1])
                for t in range(TT):
                    last = act.activation(work2[:, t, :], work[:, t, :], ACT.Exp, bias=st4[:, 0, t:t + 1],
                                          accum_out=rowsum[:, t:t + 1])
                last.then_inc(s["rowsum_ready"], 1)
                act.wait_ge(s["aT_psum"], c + 1)
                act.copy(work2[:].rearrange("p (k a) w -> p k (a w)", k=KT), ps_m[:, 0:2, :]).then_inc(s["aT_ready"], 1)
                act.wait_ge(s["zed_ready"], c + 1)
                act.activation(work[:].rearrange("p (k a) w -> p k (a w)", k=2), ps_m[:, 2:4, :], ACT.Tanh)\
                   .then_inc(s["tanh_ready"], 1)
                copy_xnT(NC + 3 * c + 3)
                act.wait_ge(s["h_psum"], c + 1)
                act.activation(hT[:], ps_e[0][:], ACT.Gelu, bias=hbias[:, 0:1]).then_inc(s["h_ready"], 1)
                act.wait_ge(s["negtop_ready"], c + 1)
                for t in range(TT):
                    last = act.activation(elg[:, t, :], lg[:, t, :], ACT.Exp, bias=st4[:, 1, t:t + 1])
                last.then_inc(s["elg_ready"], 1)
                act.wait_ge(s["alphaT_psum"], c + 1)
                act.copy(alphaT[0:NS, bass.ds(c * CT, CT)], ps_o[0:NS, :]).then_inc(s["alphaT_taken"], 1)
            act.wait_ge(s["p_rz"], 1)
            act.activation(rz, rz, ACT.Sigmoid).then_inc(s["p_sig"], 1)
            act.wait_ge(s["p_npre"], 1)
            act.activation(gate_n, gate_n, ACT.Tanh).then_inc(s["p_n"], 1)
            act.wait_ge(s["p_nmax"], 1)
            act.activation(att_s, ps_x[0:NS, 0:NS], ACT.Exp, bias=small[:, 2:3], scale=DQ ** -0.5,
                           accum_out=small[:, 3:4]).then_inc(s["p_exp"], 1)

        @block.tensor
        def _(pe):
            pe.wait_ge(s["ld_ctx"], 16)
            pe.wait_ge(s["ld_wqkv"], 48)
            for i, (col, n) in enumerate(k_cols):
                for m in range(KT):
                    if i:
                        pe.wait_ge(s["blk_hi"], KT * (i - 1) + m + 1)
                    for k in range(KT):
                        mm = pe.matmul(ps_e[m][:, 0:n], wqkv[:, 0, k, P * m:P * m + P], ctxT[:, k, col:col + n],
                                       start=(k == 0), stop=(k == KT - 1))
                    mm.then_inc(s["blk_psum"], 1)
            for st in range(ST):
                n = rows_of(st)
                if st >= 2:
                    pe.wait_ge(s["v_taken"], st - 1)
                for k in range(KT):
                    mm = pe.matmul(ps_m[0:n, st % 2, 0:D], ctxT[:, k, P * st:P * st + n], wqkv[:, 1, k, :],
                                   start=(k == 0), stop=(k == KT - 1))
                mm.then_inc(s["v_psum"], 1)
            pe.wait_ge(s["ld_const"], N_CONST)
            pe.wait_ge(s["mean_ready"], 1)
            for k in range(KT):
                mm = pe.matmul(ps_x[:, 0:1], w1[:, KT + k, :], slot_mean[:, k:k + 1], start=(k == 0), stop=(k == KT - 1))
            mm.then_inc(s["hb_psum"], 1)

            def transposes(n, bank=2):
                pe.wait_ge(s["xn_ready"], n)
                for k in range(KT):
                    for t in range(TT):
                        mm = pe.transpose(ps_m[:, bank + k, P * t:P * t + P], xn[:, t, P * k:P * k + P], ident[:])
                mm.then_inc(s["xnT_psum"], 1)
                pe.wait_ge(s["xnT_ready"], n)

            with pe.Fori(0, NC) as c:
                transposes(c + 1)
                for m in range(KT):
                    pe.wait_ge(s["blk_hi"], KBLK - 2 + m + 1 + KT * c)
                    for k in range(KT):
                        mm = pe.matmul(ps_e[m][:, :], wqkv[:, 2, k, P * m:P * m + P], xnT[:, k, :],
                                       start=(k == 0), stop=(k == KT - 1))
                    mm.then_inc(s["blk_psum"], 1)
            pe.wait_ge(s["ld_encwin"], 16)
            pe.wait_ge(s["ld_wac"], 16)
            pe.wait_ge(s["v_taken"], ST)
            for m in range(KT):
                for k in range(KT):
                    pe.matmul(ps_m[:, m, 0:W], wa_c[:, k, P * m:P * m + P], enc_win[:, k, :],
                              start=(k == 0), stop=(k == KT - 1))
            for m in range(KT):
                for k in range(KT):
                    mm = pe.matmul(ps_m[:, 2 + m, 0:D], enc_win[:, k, P * m:P * m + P], wc[:, k, :],
                                   start=(k == 0), stop=(k == KT - 1))
            mm.then_inc(s["win_psum"], 1)
            pe.wait_ge(s["win_copied"], 1)
            pe.wait_ge(s["hb_ready"], 1)
            pe.wait_ge(s["blk_hi"], KBLK + KT * NC)

            def max_unit(u, g, n1, first=False):
                t, h, half = u // (2 * HG), (u // 2) % HG, u % 2
                if not (first and u < 2):
                    pe.wait_ge(s["max_taken"], UNITS * n1 + u - 1)
                for i in range(2):
                    col = HALF_START[half] + SPLIT * i
                    mm = pe.matmul(ps_m[:, 2 * half + i, 0:SPLIT], qst[0:MAX_ROW, g, h, P * t:P * t + P],
                                   kst[0:MAX_ROW, HG * g + h, col:col + SPLIT], start=True, stop=True)
                mm.then_inc(s["max_ready"], 1)

            def max_rows(n1):
                pe.wait_ge(s["mx_ready"], n1 + 1)
                pe.transpose(ps_x[0:HG * TT, 0:P], mxc[:], ident[:]).then_inc(s["mT_ready"], 1)

            pe.wait_ge(s["ld_fill"], N_FILL)
            pe.wait_ge(s["ld_expert"], 32)
            pe.wait_ge(s["ld_k"], 16 * (2 + NG + 3 + 6))
            pe.wait_ge(q_loaded[0], 96)
            for u in range(UNITS):
                max_unit(u, 0, 0, first=True)
            max_rows(0)

            def pv(c, g, st):
                k = ST * g + st
                n = rows_of(st)
                if st == 0 and g:
                    pe.wait_ge(s["o_taken"], NG * c + g)
                pe.wait_ge(s["exp_done"], NG * ST * HG * c + HG * (k + 1))
                for h in range(HG):
                    mm = pe.matmul(ps_o[32 * h:32 * h + 32, :], v_sb[0:n, st, HG * g + h, :], probs[0:n, k % 2, h, :],
                                   start=(st == 0), stop=(st == ST - 1))
                mm.then_inc(s["pv_done"], 1)

            def spread_z(c, g):
                pe.wait_ge(s["o_taken"], NG * c + g + 1)
                pe.wait_ge(s["mrow_ready"], NG * c + g + 2)
                pe.matmul(ps_x[:, :], z_pick[:], o_raw[:], start=True, stop=True).then_inc(s["z_ready"], 1)

            def step(c, g):
                g1 = (g + 1) % NG
                n1 = NG * c + g + 1
                pe.wait_ge(m_loaded[g], 32 * (c + 1))
                u = 0
                for st in range(ST):
                    n = rows_of(st)
                    for h in range(HG):
                        e = HG * (ST * g + st) + h
                        if e >= 2:
                            pe.wait_ge(s["exp_done"], NG * ST * HG * c + e - 1)
                        pe.matmul(ps_e[h % 2][0:n, :], kst[0:ROWS, HG * g + h, P * st:P * st + n],
                                  qst[0:ROWS, g, h, :], start=True, stop=True).then_inc(s["qk_ready"], 1)
                        if h and u < UNITS:
                            if u == 0:
                                pe.wait_ge(q_loaded[g1], 96 * (c + 1 + (g1 == 0)))
                            max_unit(u, g1, n1)
                            u += 1
                    if st:
                        pv(c, g, st - 1)
                    elif g:
                        pv(c, g - 1, ST - 1)
                    if st == 2 and g:
                        spread_z(c, g - 1)
                assert u == UNITS
                if g:
                    pe.wait_ge(s["z_taken"], NG * c + g)
                max_rows(n1)

            with pe.Fori(0, NC) as c:
                for g in range(NG):
                    step(c, g)
                pv(c, NG - 1, ST - 1)
                spread_z(c, NG - 1)
                pe.wait_ge(s["att_ready"], NG * (c + 1))
                pe.wait_ge(s["max_taken"], UNITS * (NG * c + NG + 1))
                for t in range(TT):
                    for g in range(NG):
                        mm = pe.matmul(ps_m[:, t // 2, D * (t % 2):D * (t % 2) + D], attc[:, g, P * t:P * t + P],
                                       wo_pad[:, g, :], start=(g == 0), stop=(g == NG - 1))
                mm.then_inc(s["y_ready"], 1)
                transposes(NC + 3 * c + 1)
                for t in range(TT):
                    for k in range(KT):
                        mm = pe.matmul(ps_x[:, NX * t:NX * t + NX], xnT[:, k, P * t:P * t + P], rw[:, k, :],
                                       start=(k == 0), stop=(k == KT - 1))
                mm.then_inc(s["router_ready"], 1)
                for t in range(TT):
                    for j in range(4):
                        if t:
                            pe.wait_ge(s["experts_taken"], 16 * c + 4 * (t - 1) + j + 1)
                        for k in range(KT):
                            mm = pe.matmul(ps_m[:, j, :], xnT[:, k, P * t:P * t + P], expert_w[:, k, CT * j:CT * j + CT],
                                           start=(k == 0), stop=(k == KT - 1))
                        mm.then_inc(s["experts_ready"], 1)
                    if t == 0:
                        pe.wait_ge(s["gate_ready"], c + 1)
                        pe.transpose(ps_x[0:TT * NX, 0:P], hot8[:].rearrange("p t e -> p (t e)"), ident[:])\
                          .then_inc(s["gateT_psum"], 1)
                        pe.wait_ge(s["gateT_ready"], c + 1)
                        for tt in range(TT):
                            mm = pe.matmul(ps_e[tt // 2][:, D * (tt % 2):D * (tt % 2) + D], gateT[:], eb[:, tt, :],
                                           start=True, stop=True)
                        mm.then_inc(s["gbias_ready"], 1)
                pe.wait_ge(s["x2_ready"], c + 1)
                transposes(NC + 3 * c + 2)
                for t in range(TT):
                    for k in range(KT):
                        mm = pe.matmul(ps_m[:, t // 2, W * (t % 2):W * (t % 2) + W], xnT[:, k, P * t:P * t + P],
                                       win_k[:, k, :], start=(k == 0), stop=(k == KT - 1))
                mm.then_inc(s["score_ready"], 1)
                pe.wait_ge(s["a_ready"], c + 1)
                for k in range(KT):
                    for t in range(TT):
                        mm = pe.transpose(ps_m[:, k, P * t:P * t + P], work[:, t, P * k:P * k + P], ident[:])
                mm.then_inc(s["aT_psum"], 1)
                aT = work2[:].rearrange("p (k a) w -> p k (a w)", k=KT)
                pe.wait_ge(s["aT_ready"], c + 1)
                for t in range(TT):
                    o = ps_m[:, 2 + t // 2, D * (t % 2):D * (t % 2) + D]
                    for k in range(KT):
                        pe.matmul(o, aT[:, k, P * t:P * t + P], win_v[:, k, :], start=(k == 0), stop=False)
                    for k in range(KT):
                        mm = pe.matmul(o, xnT[:, k, P * t:P * t + P], wc[:, KT + k, :], start=False, stop=(k == KT - 1))
                mm.then_inc(s["zed_ready"], 1)
                transposes(NC + 3 * c + 3)
                for k in range(KT):
                    mm = pe.matmul(ps_e[0][:, :], w1[:, k, :], xnT[:, k, :], start=(k == 0), stop=(k == KT - 1))
                mm.then_inc(s["h_psum"], 1)
                pe.wait_ge(s["h_ready"], c + 1)
                for t in range(TT):
                    mm = pe.matmul(ps_x[:, NS * t:NS * t + NS], hT[:, P * t:P * t + P], w2[:], start=True, stop=True)
                mm.then_inc(s["lg_psum"], 1)
                pe.wait_ge(s["alpha_ready"], c + 1)
                for t in range(TT):
                    mm = pe.matmul(ps_e[1][0:NS, 0:D + 1], alpha[:, t, :], xn[:, t, :], start=(t == 0), stop=(t == TT - 1))
                mm.then_inc(s["slot_psum"], 1)
                for t in range(TT):
                    mm = pe.transpose(ps_o[0:NS, P * t:P * t + P], alpha[:, t, :], ident[:])
                mm.then_inc(s["alphaT_psum"], 1)
                pe.wait_ge(s["slot_taken"], c + 1)
                pe.wait_ge(s["alphaT_taken"], c + 1)

            def transpose_slots(src, ready, done):
                pe.wait_ge(s[ready], 1)
                for k in range(KT):
                    mm = pe.transpose(ps_x[:, NS * k:NS * k + NS], src[:, P * k:P * k + P], ident[0:NS, 0:NS])
                mm.then_inc(s[done], 1)

            def product(out, lhsT, rhs, first=True, last=True):
                for k in range(KT):
                    mm = pe.matmul(out, lhsT[:, k, :], rhs[:, k, :], start=(first and k == 0), stop=(last and k == KT - 1))
                return mm

            transpose_slots(vec, "p_si", "p_siT_ps")
            pe.wait_ge(s["ld_slot"], 16 * len(slot_loads))
            pe.wait_ge(s["p_siT"], 1)
            product(ps_m[0:NS, 0, :], sT, wihT[:, :, 0:2 * D], last=False)
            product(ps_m[0:NS, 0, :], slotT, whhT[:, :, 0:2 * D], first=False)
            product(ps_m[0:NS, 1, 0:D], sT, wihT[:, :, 2 * D:3 * D])
            product(ps_m[0:NS, 2, 0:D], slotT, whhT[:, :, 2 * D:3 * D]).then_inc(s["p_gi"], 1)
            transpose_slots(s_new, "p_snew", "p_snT_ps")
            pe.wait_ge(s["p_snT"], 1)
            product(ps_e[0][0:DQ, 0:NS], wqs, sT)
            product(ps_e[1][0:DQ, 0:NS], wks, sT)
            product(ps_m[0:NS, 3, 0:D], sT, wvs).then_inc(s["p_qkv"], 1)
            pe.wait_ge(s["p_qkT"], 1)
            pe.matmul(ps_x[0:NS, 0:NS], qkT[:, 0, :], qkT[:, 1, :], start=True, stop=True).then_inc(s["p_lg"], 1)
            pe.wait_ge(s["p_attn"], 1)
            pe.transpose(ps_x[0:NS, P:P + NS], att_s, ident[0:NS, 0:NS]).then_inc(s["p_attT_ps"], 1)
            pe.wait_ge(s["p_attT"], 1)
            pe.matmul(ps_m[0:NS, 0, 0:D], att_sT, comm, start=True, stop=True).then_inc(s["p_comm"], 1)
            transpose_slots(y_ln, "p_y", "p_yT_ps")
            pe.wait_ge(s["p_yT"], 1)
            product(ps_m[0:NS, 1, 0:D], sT, wvps).then_inc(s["p_sv"], 1)
            transpose_slots(vec, "p_svb", "p_svT_ps")
            pe.wait_ge(s["p_svT"], 1)
            product(ps_m[0:NS, 2, 0:D], sT, wos).then_inc(s["p_svo"], 1)
            pe.wait_ge(s["p_svo_sb"], 1)
            for c in range(NC):
                if c >= 2:
                    pe.wait_ge(s["out_ready"], c - 1)
                for t in range(TT):
                    mm = pe.matmul(ps_m[:, 2 * (c % 2) + t // 2, D * (t % 2):D * (t % 2) + D],
                                   alphaT[:, CT * c + P * t:CT * c + P * t + P], svo, start=True, stop=True)
                mm.then_inc(s["out_psum"], 1)

        @block.vector
        def _(dve):
            dve.wait_ge(s["ld_cond"], 96)
            dve.wait_ge(s["ld_const"], N_CONST)
            scale = E ** -0.5
            dve.tensor_scalar(tau[:, 2:3], tau[:, 0:1], scale, None, ALU.mult)
            dve.tensor_scalar(win_f[:, 2:3], win_f[:, 0:1], -float(W // 2), 0.0, ALU.add, ALU.max)
            dve.tensor_copy(win_f[:, 4:5], win_i[:, 0:1])
            dve.tensor_scalar(rtau[:, 1:2], rtau[:, 0:1], -1.0, None, ALU.mult)
            dve.drain()
            dve.tensor_scalar(qk_bias[:, 0, :], qk_bias[:, 0, :], tau[:, 2:3], None, ALU.mult)
            dve.tensor_scalar(win_f[:, 3:4], win_f[:, 2:3], float(S - W), None, ALU.min)
            dve.tensor_scalar(win_f[:, 5:6], win_f[:, 0:1], -16.0, 0.0, ALU.add, ALU.max)
            dve.tensor_scalar(win_f[:, 6:7], win_f[:, 0:1], 16.0, win_f[:, 4:5], ALU.add, ALU.min)
            dve.tensor_tensor(rtau[:, 0:1], rtau[:, 0:1], rtau[:, 1:2], ALU.max)
            dve.drain()
            dve.tensor_copy(win_i[:, 1:2], win_f[:, 3:4]).then_inc(s["masks_ready"], 1)
            dve.tensor_scalar(rtau[:, 0:1], rtau[:, 0:1], 0.1, None, ALU.add)
            dve.drain()
            dve.tensor_copy(win_f[:, 7:8], win_i[:, 1:2]).then_inc(s["window_start"], 1)
            dve.reciprocal(rtau[:, 1:2], rtau[:, 0:1])
            dve.drain()
            dve.tensor_scalar(iota_w[:], iota_w[:], win_f[:, 7:8], None, ALU.add)
            dve.drain()
            dve.tensor_scalar(keep[:], iota_w[:], win_f[:, 5:6], None, ALU.is_ge)
            dve.tensor_scalar(gauss[:], iota_w[:], win_f[:, 6:7], None, ALU.is_le)
            dve.tensor_scalar(iota_w[:], iota_w[:], win_f[:, 0:1], None, ALU.subtract)
            dve.drain()
            dve.tensor_tensor(keep[:], keep[:], gauss[:], ALU.mult)
            dve.drain()
            dve.tensor_scalar(neg_mask[:], keep[:], -1.0, BIG, ALU.add, ALU.mult)
            dve.tensor_tensor(iota_w[:], iota_w[:], iota_w[:], ALU.mult).then_inc(s["masks_ready"], 1)
            dve.tensor_reduce(slot_mean[:], slotT[:], AX.X, ALU.add)
            dve.drain()
            dve.tensor_scalar(slot_mean[:], slot_mean[:], 1.0 / NS, None, ALU.mult).then_inc(s["mean_ready"], 1)
            dve.wait_ge(s["ld_delta"], 16)
            dve.tensor_scalar(delta_a, delta_a, scale, None, ALU.mult)
            dve.drain()
            dve.tensor_copy(delta3[:, 0, :], delta_a)
            dve.drain()
            dve.tensor_tensor(delta_b, delta_a, delta3[:, 0, :], ALU.subtract)
            dve.drain()
            dve.tensor_copy(delta3[:, 1, :], delta_b)
            dve.drain()
            dve.tensor_tensor(delta3[:, 2, :], delta_b, delta3[:, 1, :], ALU.subtract).then_inc(s["delta_parts"], 1)

            def split(b, m, n):
                dve.wait_ge(s["blk_hi"], b + 1)
                dve.tensor_tensor(rest[:, m, 0:n], q32[:, m, 0:n], parts[:, m, 0, 0:n], ALU.subtract)
                dve.drain()
                dve.tensor_copy(parts[:, m, 1, 0:n], rest[:, m, 0:n])
                dve.drain()
                dve.tensor_tensor(parts[:, m, 2, 0:n], rest[:, m, 0:n], parts[:, m, 1, 0:n], ALU.subtract)\
                   .then_inc(s["blk_parts"], 1)

            for i, (_, n) in enumerate(k_cols):
                for m in range(KT):
                    split(KT * i + m, m, n)
            dve.wait_ge(s["consts_set"], 2)
            for st in range(ST):
                n = rows_of(st)
                dve.wait_ge(s["v_psum"], st + 1)
                dve.tensor_tensor(v_sb[0:n, st, :, 0:E], ps_m[0:n, st % 2, 0:D].rearrange("p (h e) -> p h e", h=H),
                                  bv0[0:n, :].rearrange("p (h e) -> p h e", h=H), ALU.add).then_inc(s["v_taken"], 1)
            dve.wait_ge(s["hb_psum"], 1)
            dve.tensor_tensor(hbias[:], ps_x[:, 0:1], b1[:], ALU.add).then_inc(s["hb_ready"], 1)

            def layernorm(src, n):
                dve.drain()
                for t in range(TT):
                    dve.bn_stats(bst[:, t, :], src(t))
                dve.drain()
                for t in range(TT):
                    last = dve.bn_aggr(mv[:, t, :], bst[:, t, :])
                last.then_inc(s["var_ready"], 1)
                dve.wait_ge(s["rstd_ready"], n)
                for t in range(TT):
                    last = dve.tensor_scalar(xn[:, t, 0:D], src(t), mv[:, t, 0:1], rstd[:, t:t + 1], ALU.subtract, ALU.mult)
                last.then_inc(s["xn_ready"], 1)

            dve.wait_ge(s["ld_x"], 16)
            with dve.Fori(0, NC) as c:
                dve.drain()
                for t in range(TT):
                    dve.bn_stats(bst[:, t, :], tokens[:, bass.ds(c * TT + t, 1), :])
                dve.drain()
                for t in range(TT):
                    last = dve.bn_aggr(mv[:, t, :], bst[:, t, :])
                last.then_inc(s["var_ready"], 1)
                dve.wait_ge(s["rstd_ready"], c + 1)
                for t in range(TT):
                    last = dve.tensor_scalar(xn[:, t:t + 1, 0:D], tokens[:, bass.ds(c * TT + t, 1), :], mv[:, t, 0:1],
                                             rstd[:, t:t + 1], ALU.subtract, ALU.mult)
                last.then_inc(s["xn_ready"], 1)
                for m in range(KT):
                    split(KBLK + m + KT * c, m, CT)
            dve.tensor_copy(st4[:, 7, 0:1], rtau[:, 1:2]).then_inc(s["wqkv_free"], 1)

            def take_max(u, n1):
                t, h, half = u // (2 * HG), (u // 2) % HG, u % 2
                dve.wait_ge(s["max_ready"], UNITS * n1 + u + 1)
                col = TT * h + t
                dve.tensor_reduce(mx[:, half, col:col + 1], ps_m[:, 2 * half:2 * half + 2, 0:SPLIT], AX.XY, ALU.max)\
                   .then_inc(s["max_taken"], 1)

            def max_out(g, n1):
                dve.tensor_tensor(mxc[:], mx[:, 0, :], mx[:, 1, :], ALU.max).then_inc(s["mx_ready"], 1)
                dve.wait_ge(s["mT_ready"], n1 + 1)
                dve.tensor_scalar(mrow[:, 0, :], ps_x[0:HG * TT, 0:P], -1.0, None, ALU.mult)
                dve.drain()
                dve.scalar_tensor_tensor(out=mrow[:, 1, :], in0=ps_x[0:HG * TT, 0:P], scalar=-1.0, in1=mrow[:, 0, :],
                                         op0=ALU.mult, op1=ALU.subtract).then_inc(s["mrow_ready"], 1)

            def take_o(c, g):
                dve.wait_ge(s["pv_done"], NG * ST * c + ST * (g + 1))
                dve.tensor_copy(o_raw[:], ps_o[:]).then_inc(s["o_taken"], 1)

            def normalise(c, g):
                dve.wait_ge(s["z_ready"], NG * c + g + 1)
                dve.reciprocal(z_inv[:], ps_x[:]).then_inc(s["z_taken"], 1)
                dve.drain()
                dve.tensor_tensor(attc[:, g, :], o_raw[:], z_inv[:], ALU.mult).then_inc(s["att_ready"], 1)

            for u in range(UNITS):
                take_max(u, 0)
            dve.drain()
            max_out(0, 0)

            dve.wait_ge(s["xa_ready"], 1)
            with dve.Fori(0, NC) as c:
                for g in range(NG):
                    n1 = NG * c + g + 1
                    for u in range(UNITS):
                        take_max(u, n1)
                        if u == 3 and g:
                            take_o(c, g - 1)
                        if u == 8 and g:
                            normalise(c, g - 1)
                    dve.drain()
                    dve.wait_ge(m_loaded[g], 32 * (c + 1))
                    max_out((g + 1) % NG, n1)
                take_o(c, NG - 1)
                normalise(c, NG - 1)

                dve.wait_ge(s["y_ready"], c + 1)
                dve.tensor_tensor(xa[:], tokens[:, bass.ds(c * TT, TT), :],
                                  ps_m[:, 0:2, :].rearrange("p b (a d) -> p (b a) d", a=2), ALU.add)
                layernorm(lambda t: xa[:, t, :], NC + 3 * c + 1)
                dve.wait_ge(s["router_ready"], 2 * c + 1)
                dve.tensor_tensor(lg8[:], ps_x[:, 0:TT * NX].rearrange("p (t e) -> p t e", t=TT),
                                  rb[:].unsqueeze(1).broadcast_to((P, TT, NX)), ALU.add)
                dve.drain()
                dve.tensor_reduce(st4[:, 2, :], lg8[:], AX.X, ALU.max)
                dve.drain()
                top = st4[:, 2, :].unsqueeze(2).broadcast_to((P, TT, NX))
                dve.tensor_tensor(hot8[:], lg8[:], top, ALU.is_equal)
                dve.drain()
                dve.tensor_tensor(lg8[:], lg8[:], top, ALU.subtract).then_inc(s["router_ready"], 1)
                dve.tensor_tensor(hot8[:], hot8[:], rank[:].unsqueeze(1).broadcast_to((P, TT, NX)), ALU.mult)
                dve.drain()
                dve.tensor_reduce(st4[:, 3, :], hot8[:], AX.X, ALU.max)
                dve.drain()
                dve.tensor_tensor(hot8[:], hot8[:], st4[:, 3, :].unsqueeze(2).broadcast_to((P, TT, NX)), ALU.is_equal)
                dve.wait_ge(s["elg_ready"], 2 * c + 1)
                dve.tensor_reduce(st4[:, 4, :], ex8[:], AX.X, ALU.add)
                dve.drain()
                dve.reciprocal(st4[:, 5, :], st4[:, 4, :])
                dve.drain()
                dve.tensor_tensor(hot8[:], hot8[:], st4[:, 5, :].unsqueeze(2).broadcast_to((P, TT, NX)), ALU.mult)\
                   .then_inc(s["gate_ready"], 1)
                for t in range(TT):
                    for e in range(NX):
                        dve.drain()
                        if e % 2 == 0:
                            dve.wait_ge(s["experts_ready"], 16 * c + 4 * t + e // 2 + 1)
                        last = dve.scalar_tensor_tensor(out=xb[:, t, :], in0=ps_m[:, e // 2, D * (e % 2):D * (e % 2) + D],
                                                        scalar=hot8[:, t, e:e + 1], in1=(xb if e else xa)[:, t, :],
                                                        op0=ALU.mult, op1=ALU.add)
                        if e % 2:
                            last.then_inc(s["experts_taken"], 1)
                dve.drain()
                dve.wait_ge(s["gbias_ready"], c + 1)
                for i in range(2):
                    dst = xb[:, 2 * i:2 * i + 2, :].rearrange("p a d -> p (a d)")
                    last = dve.tensor_tensor(dst, dst, ps_e[i][:, :], ALU.add)
                last.then_inc(s["x2_ready"], 1)
                layernorm(lambda t: xb[:, t, :], NC + 3 * c + 2)
                dve.wait_ge(s["score_ready"], c + 1)
                work_h = work[:].rearrange("p (b a) w -> p b a w", b=2)
                dve.tensor_tensor(work_h, ps_m[:, 0:2, :].rearrange("p b (a w) -> p b a w", a=2),
                                  keep[:].unsqueeze(1).unsqueeze(1).broadcast_to((P, 2, 2, W)), ALU.mult)
                dve.drain()
                dve.tensor_tensor(work[:], work[:], neg_mask[:].unsqueeze(1).broadcast_to((P, TT, W)), ALU.add)
                dve.drain()
                dve.tensor_reduce(st4[:, 6, :], work[:], AX.X, ALU.max)
                dve.drain()
                dve.tensor_scalar(st4[:, 0, :], st4[:, 6, :], -BIG, -1.0, ALU.max, ALU.mult).then_inc(s["negmax_ready"], 1)
                dve.wait_ge(s["rowsum_ready"], c + 1)
                dve.scalar_tensor_tensor(out=rowsum[:], in0=tail[:], scalar=float(S - W), in1=rowsum[:],
                                         op0=ALU.mult, op1=ALU.add)
                dve.drain()
                dve.reciprocal(st4[:, 6, :], rowsum[:])
                dve.drain()
                for t in range(TT):
                    last = dve.scalar_tensor_tensor(out=work[:, t, :], in0=work2[:, t, :], scalar=st4[:, 6, t:t + 1],
                                                    in1=gauss[:], op0=ALU.mult, op1=ALU.mult)
                last.then_inc(s["a_ready"], 1)
                dve.wait_ge(s["tanh_ready"], c + 1)
                dve.tensor_tensor(xa[:], xb[:], work[:], ALU.add)
                layernorm(lambda t: xa[:, t, :], NC + 3 * c + 3)
                dve.tensor_copy(tokens[:, bass.ds(c * TT, TT), :], xa[:])
                dve.wait_ge(s["lg_psum"], c + 1)
                dve.tensor_tensor(lg[:], ps_x[:, 0:TT * NS].rearrange("p (t n) -> p t n", t=TT),
                                  b2[:].unsqueeze(1).broadcast_to((P, TT, NS)), ALU.add)
                dve.drain()
                dve.tensor_scalar(lg[:], lg[:], rtau[:, 1:2], None, ALU.mult)
                dve.drain()
                for t in range(TT):
                    dve.max(top8[:, t, :], lg[:, t, :])
                dve.drain()
                dve.tensor_scalar(st4[:, 1, :], top8[:, :, 0], -1.0, None, ALU.mult).then_inc(s["negtop_ready"], 1)
                for t in range(TT):
                    dve.match_replace(lgr[:, t, :], top8[:, t, :], lg[:, t, :], -3.0e38)
                dve.drain()
                dve.tensor_tensor(lgr[:], lg[:], lgr[:], ALU.not_equal)
                dve.drain()
                dve.wait_ge(s["elg_ready"], 2 * c + 2)
                dve.tensor_tensor(elg[:], elg[:], lgr[:], ALU.mult)
                dve.drain()
                dve.tensor_reduce(st4[:, 4, :], elg[:], AX.X, ALU.add)
                dve.drain()
                dve.reciprocal(st4[:, 5, :], st4[:, 4, :])
                dve.drain()
                dve.tensor_tensor(alpha[:], elg[:], st4[:, 5, :].unsqueeze(2).broadcast_to((P, TT, NS)), ALU.mult)\
                   .then_inc(s["alpha_ready"], 1)
                dve.wait_ge(s["slot_psum"], c + 1)
                dve.tensor_tensor(slot_acc[:], slot_acc[:], ps_e[1][0:NS, 0:D + 1], ALU.add).then_inc(s["slot_taken"], 1)
                dve.drain()

            dve.memset(alphaT_raw[NS:NS + 1, :], 1.0)
            dve.wait_ge(s["ld_slot"], 16 * len(slot_loads))
            dve.tensor_scalar(small[:, 0:1], slot_acc[:, D:D + 1], 1e-8, None, ALU.add)
            dve.drain()
            dve.reciprocal(small[:, 1:2], small[:, 0:1])
            dve.drain()
            dve.tensor_scalar(vec, slot_acc[:, 0:D], small[:, 1:2], None, ALU.mult).then_inc(s["p_si"], 1)
            dve.tensor_tensor(b_ih[:, 0:2 * D], b_ih[:, 0:2 * D], b_hh[:, 0:2 * D], ALU.add)

            def copy_T(ready, done):
                dve.wait_ge(s[ready], 1)
                dve.tensor_copy(sT, ps_x[:, 0:KT * NS].rearrange("p (k n) -> p k n", k=KT)).then_inc(s[done], 1)

            copy_T("p_siT_ps", "p_siT")
            dve.wait_ge(s["p_gi"], 1)
            dve.tensor_tensor(rz, ps_m[0:NS, 0, :], b_ih[:, 0:2 * D], ALU.add).then_inc(s["p_rz"], 1)
            dve.tensor_tensor(gate_n, ps_m[0:NS, 1, 0:D], b_ih[:, 2 * D:3 * D], ALU.add)
            dve.tensor_tensor(hid_n, ps_m[0:NS, 2, 0:D], b_hh[:, 2 * D:3 * D], ALU.add)
            dve.wait_ge(s["p_sig"], 1)
            dve.drain()
            dve.tensor_tensor(hid_n, hid_n, rz[:, 0:D], ALU.mult)
            dve.drain()
            dve.tensor_tensor(gate_n, gate_n, hid_n, ALU.add).then_inc(s["p_npre"], 1)
            dve.wait_ge(s["p_n"], 1)
            dve.tensor_tensor(s_new, slot0, gate_n, ALU.subtract)
            dve.drain()
            dve.tensor_tensor(s_new, s_new, rz[:, D:2 * D], ALU.mult)
            dve.drain()
            dve.tensor_tensor(s_new, s_new, gate_n, ALU.add).then_inc(s["p_snew"], 1)
            copy_T("p_snT_ps", "p_snT")
            dve.wait_ge(s["p_qkv"], 1)
            for i in range(2):
                dve.tensor_scalar(qkT[:, i, :], ps_e[i][0:DQ, 0:NS], b_qk[:, i:i + 1], None, ALU.add)
            dve.tensor_tensor(comm, ps_m[0:NS, 3, 0:D], b_v, ALU.add).then_inc(s["p_qkT"], 1)
            dve.wait_ge(s["p_lg"], 1)
            dve.tensor_reduce(small[:, 4:5], ps_x[0:NS, 0:NS], AX.X, ALU.max)
            dve.drain()
            dve.tensor_scalar(small[:, 2:3], small[:, 4:5], -(DQ ** -0.5), None, ALU.mult).then_inc(s["p_nmax"], 1)
            dve.wait_ge(s["p_exp"], 1)
            dve.reciprocal(small[:, 5:6], small[:, 3:4])
            dve.drain()
            dve.tensor_scalar(att_s, att_s, small[:, 5:6], None, ALU.mult).then_inc(s["p_attn"], 1)
            dve.wait_ge(s["p_attT_ps"], 1)
            dve.tensor_copy(att_sT, ps_x[0:NS, P:P + NS]).then_inc(s["p_attT"], 1)
            dve.wait_ge(s["p_comm"], 1)
            dve.tensor_tensor(y_ln, s_new, ps_m[0:NS, 0, 0:D], ALU.add)
            dve.drain()
            dve.bn_stats(bst[0:NS, 0, :], y_ln)
            dve.drain()
            dve.bn_aggr(small[:, 7:9], bst[0:NS, 0, :]).then_inc(s["p_var"], 1)
            dve.wait_ge(s["p_rstd"], 1)
            dve.tensor_scalar(y_ln, y_ln, small[:, 7:8], small[:, 10:11], ALU.subtract, ALU.mult)
            dve.drain()
            dve.tensor_tensor(y_ln, y_ln, ln_g, ALU.mult)
            dve.drain()
            dve.tensor_tensor(y_ln, y_ln, ln_b, ALU.add).then_inc(s["p_y"], 1)
            copy_T("p_yT_ps", "p_yT")
            dve.wait_ge(s["p_sv"], 1)
            dve.tensor_tensor(vec, ps_m[0:NS, 1, 0:D], b_vp, ALU.add).then_inc(s["p_svb"], 1)
            copy_T("p_svT_ps", "p_svT")
            dve.wait_ge(s["p_svo"], 1)
            dve.tensor_copy(svo[0:NS, :], ps_m[0:NS, 2, 0:D]).then_inc(s["p_svo_sb"], 1)
            for c in range(NC):
                dve.wait_ge(s["out_psum"], c + 1)
                tok = tokens[:, TT * c:TT * c + TT, :].rearrange("p (b a) d -> p b (a d)", b=2)
                dve.tensor_tensor(tok, tok, ps_m[:, 2 * (c % 2):2 * (c % 2) + 2, :], ALU.add).then_inc(s["out_ready"], 1)


def kernel(**inputs):
    import numpy as np
    import concourse.bacc as bacc
    from concourse import mybir as _mybir
    from concourse.bass_utils import run_bass_kernel_spmd

    x = {k: np.asarray(v) for k, v in inputs.items()}
    z_pick = np.zeros((P, P), np.float32)
    for h in range(HG):
        z_pick[32 * h + E, 32 * h:32 * h + 32] = 1.0
    arrays = {
        "x": x["x"][0], "ctxT": x["ctx_1024"][0].T, "condB_tau": x["condB_tau"], "fside": x["fside_BxS2_0"][0],
        "condB_pt": x["condB_pt"], "lenS2": x["_lenS2"],
        "L0_WqT": x["L0_xcond_Wq"].T, "L0_WkT": x["L0_xcond_Wk"].T, "L0_WvT": x["L0_xcond_Wv"].T,
        "L0_WoT": x["L0_xcond_Wo"].T, "L0_bq": x["L0_xcond_bq"], "L0_bk": x["L0_xcond_bk"],
        "L0_bv": x["L0_xcond_bv"], "L0_bo": x["L0_xcond_bo"],
        "router_wT": x["L0_ffn_router_w"].T, "router_b": x["L0_ffn_router_b"],
        "expert_wT": x["L0_ffn_expert_w"].transpose(2, 0, 1).reshape(KT, P, NX * D), "expert_b": x["L0_ffn_expert_b"],
        "L1_W_aT": x["L1_xcond_W_a"].T, "L1_W_cT": x["L1_xcond_W_c"].T,
        "slot_init": x["L1_ffn_slot_init"], "slot_initT": x["L1_ffn_slot_init"].T,
        "w1": x["L1_ffn_w1"], "b1": x["L1_ffn_b1"], "w2": x["L1_ffn_w2"], "b2": x["L1_ffn_b2"],
        "L1_tau": x["L1_ffn_tau"], "WihT": x["L1_ffn_Wih"].T, "WhhT": x["L1_ffn_Whh"].T,
        "bih": x["L1_ffn_bih"], "bhh": x["L1_ffn_bhh"], "wq": x["L1_ffn_wq"], "bq": x["L1_ffn_bq"],
        "wk": x["L1_ffn_wk"], "bk": x["L1_ffn_bk"], "wv": x["L1_ffn_wv"], "bv": x["L1_ffn_bv"],
        "ln_g": x["L1_ffn_ln_g"], "ln_b": x["L1_ffn_ln_b"], "wvp": x["L1_ffn_wvp"], "bvp": x["L1_ffn_bvp"],
        "wo": x["L1_ffn_wo"], "L1_bo": x["L1_ffn_bo"],
        "c_ident": np.eye(P, dtype=np.float32), "c_zpick": z_pick,
        "c_iota": np.arange(W, dtype=np.float32), "c_rank": np.arange(NX, 0, -1).astype(np.float32),
    }
    arrays = {k: np.ascontiguousarray(a) for k, a in arrays.items()}
    nc = bacc.Bacc("TRN2", target_bir_lowering=False, num_devices=1)
    io = {k: nc.dram_tensor(f"in_{k}", a.shape, _mybir.dt.from_np(a.dtype), kind="ExternalInput").ap() for k, a in arrays.items()}
    io["out"] = nc.dram_tensor("out_0", (T, D), _mybir.dt.float32, kind="ExternalOutput").ap()
    build(nc, io)
    r = run_bass_kernel_spmd(nc, [{f"in_{k}": a for k, a in arrays.items()}], core_ids=[0])
    return r.results[0]["out_0"].reshape(1, T, D)
```

```python
from contextlib import ExitStack

import concourse.bass as bass
from concourse import mybir

F32 = mybir.dt.float32
BF16 = mybir.dt.bfloat16
I32 = mybir.dt.int32
ALU = mybir.AluOpType
ACT = mybir.ActivationFunctionType
AX = mybir.AxisListType

P = 128
T, D = 2048, 256
S = 1601
H, E = 16, 16
KT = D // P
CT = 512
NC = T // CT
TT = CT // P
HG = 4
NG = H // HG
ST = (S + P - 1) // P
LAST = S - (ST - 1) * P
NX = 8
NE = 2 * TT * NX // 4
W = 256
NS, TOPK = 64, 8
DQ, DH = 64, 128
QUARTERS = 4
SPLIT = (S + QUARTERS - 1) // QUARTERS
QUARTER_START = [min(q * SPLIT, S - SPLIT) for q in range(QUARTERS)]
UNITS = TT * HG * QUARTERS
SLOTS = NG * ST
LEAD = 14
SHIFT = 1
BIG = 1.0e9

Q_PART = (0, 0, 1, 1, 0, 2)
K_PART = (0, 1, 0, 1, 2, 0)
DELTA_ROW = 96
MAX_ROW = 99
ROWS = 101


JOBS = (["y0", "y1", "t1a", "t1b", "router"] + [f"e{i}" for i in range(4)] + ["gateT"] + [f"e{i}" for i in range(4, 8)]
        + ["gb0", "gb1"] + [f"e{i}" for i in range(8, 16)]
        + ["t2a", "t2b", "score0", "score1", "aTa", "aTb", "z0", "z1", "t3a", "t3b", "h", "logits", "slots", "alphaT"])
JOB = {name: i for i, name in enumerate(JOBS)}
USES = len(JOBS) // 2
assert len(JOBS) % 2 == 0


def need(eng, sem, value):
    if not (isinstance(value, int) and value <= 0):
        eng.wait_ge(sem, value)


def units_of(k):
    per = NG * UNITS
    return [divmod(UNITS + LEAD + v, UNITS) for v in range(per * k // SLOTS, per * (k + 1) // SLOTS)]


def max_end(k):
    return next((j for j, u in units_of(k % SLOTS) if u == UNITS - 1), None)


def rows_of(st):
    return LAST if st == ST - 1 else P


def build(nc, io):
    with ExitStack() as ctx:
        def sb(name, shape, dt=F32):
            return ctx.enter_context(nc.sbuf_tensor(name, shape, dt))

        def ps(name, shape, dt=F32):
            return ctx.enter_context(nc.psum_tensor(name, shape, dt))

        def sem(name):
            return ctx.enter_context(nc.semaphore(name))

        q_parts = nc.dram_tensor("q_parts", (3, D, T + CT), BF16, kind="Internal").ap()
        k_parts = nc.dram_tensor("k_parts", (3, D, S), BF16, kind="Internal").ap()
        x3_dram = nc.dram_tensor("x3", (T, D), F32, kind="Internal").ap().rearrange("(a p) d -> p a d", p=P)
        x_dram = io["x"].rearrange("(a p) d -> p a d", p=P)

        xres = sb("xres", [P, TT, D])
        kst_raw = sb("k_stack", [P, H * S // 2 + 8])
        kst = kst_raw[:, 0:H * S // 2].bitcast(BF16).rearrange("p (h s) -> p h s", h=H)
        qst = sb("q_stack", [P, NG, HG, CT], BF16)
        v_sb = sb("v_heads", [P, ST, H, 32])
        probs_raw = sb("probs", [P, 2 * HG * CT])
        probs = probs_raw[:].rearrange("p (b h t) -> p b h t", b=2, h=HG)
        ctxT = probs_raw[:, 0:KT * S].rearrange("p (k s) -> p k s", k=KT)
        expert_w = sb("expert_w", [P, KT, NX * D])
        wqkv = expert_w[:].rearrange("p k n -> p (k n)")[:, 0:3 * KT * D]\
            .rearrange("p (w k n) -> p w k n", w=3, k=KT)
        attc = sb("attn_chunk", [P, NG, CT])
        o_raw = sb("o_unnormed", [P, CT])
        z_sb = sb("z_sb", [P, CT])
        wo_pad = sb("wo_pad", [P, NG, D])
        alphaT_raw = sb("alphaT", [P, T])
        alphaT = alphaT_raw[0:NS + 1, :]
        parts = alphaT_raw[:, 0:3 * CT].bitcast(BF16).rearrange("p (m a t) -> p m a t", m=2, a=3)
        xa = sb("xa", [P, TT, D])
        attc_flat = attc[:].rearrange("p g t -> p (g t)")
        xb = sb("xb", [P, TT, D])
        xn = sb("xn", [P, TT, D + 1])
        xnT = sb("xnT", [P, KT, CT])
        work = sb("work", [P, TT, W])
        work2 = sb("work2", [P, TT, W])
        hT = sb("hT", [P, CT])
        q32 = work[:].rearrange("p t w -> p (t w)").rearrange("p (m n) -> p m n", m=2)
        rest = work2[:].rearrange("p t w -> p (t w)").rearrange("p (m n) -> p m n", m=2)
        ident = sb("ident", [P, P])
        z_pick = sb("z_pick", [P, HG])
        z_inv = sb("z_inv", [P, TT * HG])
        one = sb("one", [P, 1])
        iota_w = z_sb[:, W:2 * W]
        keep = sb("keep", [P, W])
        gauss = sb("gauss", [P, W])
        neg_mask = sb("neg_mask", [P, W])
        win_f = sb("win_f", [P, 8])
        win_i = sb("win_i", [P, 2], I32)
        enc_win = o_raw[:].rearrange("p (k w) -> p k w", k=KT)
        win_k = sb("win_k", [P, KT, W])
        win_v = sb("win_v", [P, KT, D])
        wa_c = work2[:].rearrange("p t w -> p (t w)").rearrange("p (k n) -> p k n", k=KT * 2)
        wc = sb("wc", [P, 2 * KT, D])
        w1 = sb("w1", [P, 2 * KT, DH])
        w2 = sb("w2", [DH, NS])
        rw = sb("router_w", [P, KT, NX])
        rb = sb("router_b", [P, NX])
        rank = sb("rank", [P, NX])
        eb = sb("expert_b_tiles", [TT * NX, TT, D])
        bo0 = sb("bo0", [P, D])
        bv0 = z_sb[:, 0:D]
        b2 = sb("b2", [P, NS])
        b1 = sb("b1", [P, 1])
        hbias = sb("hbias", [P, 1])
        slotT = sb("slotT", [P, KT, NS])
        slot_mean = sb("slot_mean", [P, KT])
        qk_bias = sb("qk_bias", [P, 2, KT])
        tau = sb("tau", [P, 4])
        rtau = sb("rtau", [P, 2])
        q_flat = qst[:].rearrange("p g h t -> p (g h t)")
        delta3 = q_flat[0:H, 0:3 * S].rearrange("p (a s) -> p a s", a=3)
        delta_a = q_flat[0:H, 3 * S + 1:5 * S + 1].bitcast(F32)
        delta_b = expert_w[:].rearrange("p k n -> p (k n)")[0:H, 3 * KT * D:3 * KT * D + S]
        aT = work2[:].rearrange("p (k a) w -> p k (a w)", k=KT)
        ones_sb = attc_flat[0:H, 0:1024].bitcast(BF16)
        mx = sb("mx", [P, QUARTERS, HG * TT])
        mxc = sb("mxc", [P, HG * TT])
        mrow = sb("mrow", [HG * TT, 2, P], BF16)
        bst = sb("bst", [P, TT, 6])
        mv = sb("mv", [P, TT, 2])
        var_e = sb("var_e", [P, TT])
        rstd = sb("rstd", [P, TT])
        neg_half = sb("neg_half", [P, TT])
        eps = sb("eps", [P, TT])
        lg8 = sb("lg8", [P, TT, NX])
        ex8 = sb("ex8", [P, TT, NX])
        hot8 = sb("hot8", [P, TT, NX])
        st4 = sb("st4", [P, 8, TT])
        gateT = sb("gateT", [TT * NX, P])
        rowsum = sb("rowsum", [P, TT])
        tail = sb("tail", [P, TT])
        neg_big = sb("neg_big", [P, 1])
        lg, lgr, elg, alpha = (work[:].rearrange("p t w -> p (t w)")[:, TT * NS * i:TT * NS * (i + 1)]
                               .rearrange("p (t n) -> p t n", t=TT) for i in range(4))
        top8 = sb("top8", [P, TT, TOPK])
        slot_acc = sb("slot_acc", [NS, D + 1])

        at = [0]

        def late(n_rows, *shape):
            n = 1
            for x in shape:
                n *= x
            a = kst_raw[0:n_rows, at[0]:at[0] + n]
            at[0] += n
            assert at[0] <= H * S // 2
            if len(shape) == 2:
                a = a.rearrange("p (a b) -> p a b", a=shape[0])
            return a

        wihT, whhT = late(P, KT, 3 * D), late(P, KT, 3 * D)
        wqs, wks = late(P, KT, DQ), late(P, KT, DQ)
        wvs, wvps, wos = late(P, KT, D), late(P, KT, D), late(P, KT, D)
        b_ih, b_hh = late(NS, 3 * D), late(NS, 3 * D)
        b_v, ln_g, ln_b, b_vp, slot0 = (late(NS, D) for _ in range(5))
        b_qk = late(DQ, 2)
        rz, gate_n, hid_n, s_new, comm, y_ln = late(NS, 2 * D), late(NS, D), late(NS, D), late(NS, D), late(NS, D), late(NS, D)
        vec = late(NS, D)
        sT = late(P, KT, NS)
        qkT = late(DQ, 2, NS)
        att_s = late(NS, NS)
        att_sT = late(NS, NS)
        svo = late(NS + 1, D)
        small = late(NS, 16)
        x_end = probs_raw[:].rearrange("p (a d) -> p a d", d=D)

        ps_e = [ps(f"ps_e{i}", [P, CT]) for i in range(2)]
        ps_m = ps("ps_m", [P, 4, CT])
        ps_o = ps("ps_o", [P, CT])
        ps_x = ps("ps_x", [P, CT])

        names = """ld_ctx ld_wqkv ld_const ld_cond ld_encwin ld_expert ld_delta ld_fill ld_k ld_slot ld_wac
            x_loaded x3_stored x_end_loaded
            fills_set consts_set scr_stored_a scr_stored_b delta_parts window_start masks_ready
            blk_psum blk_hi blk_parts v_psum v_taken
            var_ready rstd_ready xn_ready xnT_psum xnT_ready
            win_psum win_copied hb_psum hb_ready mean_ready
            max_ready max_taken mx_ready mT_ready mrow_ready
            qk_ready exp_done pv_done o_taken z_cols z_inverted z_repeated z_ready att_ready
            xres_ready lg8_ready ex8_ready gate_ready negmax_ready rowsum_ready a_ready x3_ready
            lg_ready elg_ready alpha_ready
            p_si p_siT_ps p_siT p_gi p_rz p_sig p_npre p_n p_snew p_snT_ps p_snT p_qkv p_qkT p_lg
            p_nmax p_exp p_attn p_attT_ps p_attT p_comm p_var p_rstd p_y p_yT_ps p_yT p_sv p_svb p_svT_ps p_svT
            p_svo p_svo_sb out_psum out_ready out_stored""".split()
        s = {n: sem(n) for n in names}
        q_loaded = [sem(f"q_loaded{g}") for g in range(NG)]
        m_loaded = [sem(f"m_loaded{g}") for g in range(NG)]
        x_start = [sem(f"x_start{i}") for i in range(2)]
        bank_filled = [sem(f"bank_filled{b}") for b in range(2)]
        bank_taken = [sem(f"bank_taken{b}") for b in range(2)]

        def bank(job):
            return ps_m[:, 2 + JOB[job] % 2, :]

        def bank_free(eng, job, c):
            need(eng, bank_taken[JOB[job] % 2], USES * c + JOB[job] // 2)

        def filled(mm, job):
            mm.then_inc(bank_filled[JOB[job] % 2], 1)

        def wait_filled(eng, job, c):
            eng.wait_ge(bank_filled[JOB[job] % 2], USES * c + JOB[job] // 2 + 1)

        def taken(ins, job):
            ins.then_inc(bank_taken[JOB[job] % 2], 1)

        def wait_taken(eng, job, c):
            eng.wait_ge(bank_taken[JOB[job] % 2], USES * c + JOB[job] // 2 + 1)
        block = ctx.enter_context(nc.Block())

        const_loads = [
            (ident[:], io["c_ident"]), (z_pick[:], io["c_zpick"]),
            (iota_w[:], io["c_iota"].partition_broadcast(P)), (rank[:], io["c_rank"].partition_broadcast(P)),
            (wc[:], io["L1_W_cT"].rearrange("(k p) n -> p k n", p=P)),
            (w1[:], io["w1"].rearrange("(k p) n -> p k n", p=P)),
            (w2[:], io["w2"]),
            (rw[:], io["router_wT"].rearrange("(k p) n -> p k n", p=P)),
            (rb[:], io["router_b"].partition_broadcast(P)),
            (bo0[:], io["L0_bo"].partition_broadcast(P)), 
            (bv0[:], io["L0_bv"].partition_broadcast(P)), (b2[:], io["b2"].partition_broadcast(P)),
            (b1[:], io["b1"].rearrange("(p a) -> p a", a=1)),
            (slotT[:], io["slot_initT"].rearrange("(k p) n -> p k n", p=P)),
        ]
        wo_loads = [(wo_pad[32 * j:32 * j + E, :, :],
                     io["L0_WoT"].rearrange("(g j e) n -> j e g n", g=NG, j=HG)[j]) for j in range(HG)]
        eb_loads = [(eb[NX * t:NX * t + NX, t, :], io["expert_b"]) for t in range(TT)]
        slot_loads = [
            (wihT, io["WihT"].rearrange("(k p) n -> p k n", p=P)), (whhT, io["WhhT"].rearrange("(k p) n -> p k n", p=P)),
            (wqs, io["wq"].rearrange("(k p) n -> p k n", p=P)), (wks, io["wk"].rearrange("(k p) n -> p k n", p=P)),
            (wvs, io["wv"].rearrange("(k p) n -> p k n", p=P)), (wvps, io["wvp"].rearrange("(k p) n -> p k n", p=P)),
            (wos, io["wo"].rearrange("(k p) n -> p k n", p=P)),
            (b_ih, io["bih"].partition_broadcast(NS)), (b_hh, io["bhh"].partition_broadcast(NS)),
            (b_v, io["bv"].partition_broadcast(NS)), (ln_g, io["ln_g"].partition_broadcast(NS)),
            (ln_b, io["ln_b"].partition_broadcast(NS)), (b_vp, io["bvp"].partition_broadcast(NS)),
            (slot0, io["slot_init"]), (svo[NS:NS + 1, :], io["L1_bo"].unsqueeze(0)), (b_qk[:, 0:1], io["bq"].rearrange("(p a) -> p a", a=1)),
            (b_qk[:, 1:2], io["bk"].rearrange("(p a) -> p a", a=1)),
        ]
        N_CONST = 16 * len(const_loads)
        N_FILL = 16 * (len(wo_loads) + len(eb_loads))
        KBLK = 2 * ((S + CT - 1) // CT)
        k_cols = [(i * CT, min(CT, S - i * CT)) for i in range((S + CT - 1) // CT)]

        def load_q(eng, g, chunk):
            for j in range(6):
                src = q_parts[Q_PART[j], HG * E * g:HG * E * (g + 1), bass.ds(chunk * CT, CT)]
                eng.dma_start(qst[16 * j:16 * j + 16, g, :, :], src.rearrange("(h e) t -> e h t", h=HG))\
                   .then_inc(q_loaded[g], 16)

        @block.sync
        def _(sp):
            sp.dma_start(ctxT, io["ctxT"].rearrange("(k p) s -> p k s", p=P)).then_inc(s["ld_ctx"], 16)
            for i, name in enumerate(("L0_WkT", "L0_WvT", "L0_WqT")):
                sp.dma_start(wqkv[:, i], io[name].rearrange("(k p) n -> p k n", p=P)).then_inc(s["ld_wqkv"], 16)
            for c in range(2):
                sp.dma_start((xa, xb)[c][:], x_dram[:, TT * c:TT * c + TT, :]).then_inc(x_start[c], 16)
            for dst, src in const_loads:
                sp.dma_start(dst, src).then_inc(s["ld_const"], 16)
            sp.wait_ge(s["fills_set"], 1)
            for dst, src in wo_loads + eb_loads:
                sp.dma_start(dst, src).then_inc(s["ld_fill"], 16)
            sp.wait_ge(s["consts_set"], 1)
            for r in (MAX_ROW, MAX_ROW + 1):
                sp.dma_start(kst[r:r + 1, :, :], ones_sb[0:H, 0:S]).then_inc(s["ld_k"], 16)
            for g in range(NG):
                sp.dma_start(qst[DELTA_ROW:DELTA_ROW + 3, g, :, :], ones_sb[0:3, :]).then_inc(s["ld_k"], 16)
            for i, (at_col, n) in enumerate(k_cols):
                for m in range(KT):
                    sp.wait_ge(s["blk_parts"], KT * i + m + 1)
                    for a in range(3):
                        sp.dma_start(k_parts[a, P * m:P * m + P, at_col:at_col + n], parts[:, m, a, 0:n])\
                          .then_inc(s["scr_stored_a" if m == 0 else "scr_stored_b"], 16)
            sp.wait_ge(s["delta_parts"], 1)
            for a in range(3):
                sp.dma_start(kst[DELTA_ROW + a:DELTA_ROW + a + 1, :, :], delta3[:, a, :]).then_inc(s["ld_k"], 16)
            sp.wait_ge(s["scr_stored_a"], 48 * len(k_cols))
            sp.wait_ge(s["scr_stored_b"], 48 * len(k_cols))
            for j in range(6):
                sp.dma_start(kst[16 * j:16 * j + 16, :, :], k_parts[K_PART[j]].rearrange("(h e) s -> e h s", h=H))\
                  .then_inc(s["ld_k"], 16)
            with sp.Fori(0, NC) as c:
                for m in range(KT):
                    sp.wait_ge(s["blk_parts"], KBLK + 1 + m + KT * c)
                    for a in range(3):
                        sp.dma_start(q_parts[a, P * m:P * m + P, bass.ds(c * CT, CT)], parts[:, m, a, :])\
                          .then_inc(s["scr_stored_a" if m == 0 else "scr_stored_b"], 16)
            sp.wait_ge(s["scr_stored_a"], 48 * (len(k_cols) + NC))
            sp.wait_ge(s["scr_stored_b"], 48 * (len(k_cols) + NC))
            sp.dma_start(q_parts[:, :, T:T + CT], q_parts[:, :, 0:CT]).then_inc(s["scr_stored_a"], 16)
            sp.wait_ge(s["ld_k"], 16 * (2 + NG + 3 + 6))
            for g in range(3):
                load_q(sp, g, 0)
            sp.wait_ge(s["scr_stored_a"], 48 * (len(k_cols) + NC) + 16)
            sp.wait_ge(s["blk_psum"], KBLK + KT * NC)
            for k in range(KT):
                sp.dma_start(expert_w[:, k, :], io["expert_wT"][k]).then_inc(s["ld_expert"], 16)
            sp.wait_ge(s["mrow_ready"], 1)

            def load_m(g):
                for a in range(2):
                    sp.dma_start(qst[MAX_ROW + a:MAX_ROW + a + 1, g, :, :], mrow[:, a, :]).then_inc(m_loaded[g], 16)

            def store_x3(c):
                sp.wait_ge(s["x3_ready"], c + 1)
                sp.dma_start(x3_dram[:, bass.ds(c * TT, TT), :], xres[:]).then_inc(s["x3_stored"], 16)

            def chunk_loads(c, behind):
                for g in range(NG):
                    sp.wait_ge(s["mrow_ready"], NG * c + g + 2)
                    load_m((g + 1) % NG)
                    load_q(sp, (g + 3) % NG, c if g == 0 else c + 1)
                    if g == NG - 1:
                        if behind:
                            store_x3(c - 1)
                            sp.wait_ge(s["x3_stored"], 16 * c)
                        sp.dma_start(xres[:], x_dram[:, bass.ds(c * TT, TT), :]).then_inc(s["x_loaded"], 16)

            load_m(0)
            chunk_loads(0, False)
            with sp.Fori(1, NC) as c:
                chunk_loads(c, True)
            store_x3(NC - 1)
            for dst, src in slot_loads:
                sp.dma_start(dst, src).then_inc(s["ld_slot"], 16)
            sp.wait_ge(s["x3_stored"], 16 * NC)
            sp.dma_start(x_end, x3_dram).then_inc(s["x_end_loaded"], 16)
            out = io["out"].rearrange("(a p) d -> p a d", p=P)
            for c in range(NC):
                sp.wait_ge(s["out_ready"], c + 1)
                sp.dma_start(out[:, TT * c:TT * c + TT, :], x_end[:, TT * c:TT * c + TT, :]).then_inc(s["out_stored"], 16)
            for g in range(NG):
                sp.wait_ge(q_loaded[g], 96 * (NC + (g < 3)))
            sp.wait_ge(m_loaded[0], 32 * (NC + 1))
            sp.wait_ge(s["out_stored"], 16 * NC)

        LN_SLOTS = (7, 28, 37)

        @block.gpsimd
        def _(pool):
            pool.dma_start(tau[:, 0:1], io["condB_tau"].partition_broadcast(P)).then_inc(s["ld_cond"], 16)
            pool.dma_start(win_f[:, 0:1], io["condB_pt"].partition_broadcast(P)).then_inc(s["ld_cond"], 16)
            pool.dma_start(win_i[:, 0:1], io["lenS2"].partition_broadcast(P)).then_inc(s["ld_cond"], 16)
            pool.dma_start(rtau[:, 0:1], io["L1_tau"].partition_broadcast(P)).then_inc(s["ld_cond"], 16)
            for i, name in enumerate(("L0_bq", "L0_bk")):
                pool.dma_start(qk_bias[:, i, :], io[name].rearrange("(k p) -> p k", p=P),
                               allow_slow_non_contiguous=True).then_inc(s["ld_cond"], 16)
            pool.dma_start(delta_a, io["fside"].partition_broadcast(H)).then_inc(s["ld_delta"], 16)
            pool.memset(ones_sb, 1.0).then_inc(s["consts_set"], 1)
            pool.memset(wo_pad[:], 0.0)
            pool.memset(eb[:], 0.0).then_inc(s["fills_set"], 1)
            pool.memset(neg_half[:], -0.5)
            pool.memset(eps[:], 1e-5)
            pool.memset(one[:], 1.0)
            pool.memset(neg_big[:], -BIG)
            pool.memset(v_sb[:], 1.0)
            pool.memset(xn[:, :, D:D + 1], 1.0)
            pool.memset(slot_acc[:], 0.0).then_inc(s["consts_set"], 1)
            pool.wait_ge(s["window_start"], 1)
            w0 = pool.value_load(win_i[0:1, 1:2], min_val=0, max_val=S - W)
            pool.dma_start(enc_win[:], io["ctxT"].rearrange("(k p) s -> p k s", p=P)[:, :, bass.ds(w0, W)])\
                .then_inc(s["ld_encwin"], 16)

            def rsqrt(n):
                pool.wait_ge(s["var_ready"], n)
                pool.tensor_tensor(var_e[:], mv[:, :, 1], eps[:], ALU.add)
                pool.drain()
                pool.tensor_tensor(rstd[:], var_e[:], neg_half[:], ALU.pow).then_inc(s["rstd_ready"], 1)

            with pool.Fori(0, NC) as c:
                rsqrt(c + 1)
            pool.wait_ge(s["blk_parts"], KBLK + KT * NC)
            pool.dma_start(wa_c[:, 0:KT, :], io["L1_W_aT"].rearrange("(k p) n -> p k n", p=P)).then_inc(s["ld_wac"], 16)
            pool.wait_ge(s["ld_const"], N_CONST)

            def repeat_z(c, g):
                pool.wait_ge(s["z_inverted"], NG * c + g + 1)
                z_wide = z_inv[:].unsqueeze(2).broadcast_to((P, TT * HG, 32))
                pool.tensor_tensor(z_sb[:].rearrange("p (a e) -> p a e", e=32), z_wide,
                                   one[:].unsqueeze(2).broadcast_to((P, TT * HG, 32)), ALU.mult)\
                    .then_inc(s["z_repeated"], 1)

            def behind(c, k):
                if k == 4:
                    pool.wait_ge(s["x_loaded"], 16 * (c + 1))
                    pool.tensor_tensor(xres[:], xres[:], bo0[:].unsqueeze(1).broadcast_to((P, TT, D)), ALU.add)\
                        .then_inc(s["xres_ready"], 1)
                if k in LN_SLOTS:
                    i = LN_SLOTS.index(k)
                    rsqrt(NC + 3 * c + i + 1)
                    pool.drain()
                    for t in range(TT):
                        last = pool.tensor_scalar(xn[:, t, 0:D], (xa, xb, xres)[i][:, t, :], mv[:, t, 0:1],
                                                  rstd[:, t:t + 1], ALU.subtract, ALU.mult)
                    last.then_inc(s["xn_ready"], 1)

            def chunk(c, first):
                for k in range(SLOTS):
                    g, st = k // ST, k % ST
                    if st == 3 and (g or not first):
                        repeat_z(c, g - 1)
                    if not first:
                        behind(c - 1, k - SHIFT)

            chunk(0, True)
            with pool.Fori(1, NC) as c:
                chunk(c, False)
            repeat_z(NC, -1)
            for k in range(SLOTS):
                behind(NC - 1, k)
            pool.wait_ge(s["p_var"], 1)
            pool.tensor_scalar(small[:, 9:10], small[:, 8:9], 1e-5, None, ALU.add)
            pool.drain()
            pool.tensor_tensor(small[:, 10:11], small[:, 9:10], neg_half[0:NS, 0:1], ALU.pow).then_inc(s["p_rstd"], 1)

        @block.scalar
        def _(act):
            def block_split(b, m, n, which):
                act.wait_ge(s["blk_psum"], b + 1)
                act.activation(q32[:, m, 0:n], ps_e[m][:, 0:n], ACT.Identity,
                               bias=qk_bias[:, which, m:m + 1], scale=tau[:, 2:3] if which == 0 else 1.0)
                act.activation(parts[:, m, 0, 0:n], ps_e[m][:, 0:n], ACT.Identity,
                               bias=qk_bias[:, which, m:m + 1], scale=tau[:, 2:3] if which == 0 else 1.0)\
                   .then_inc(s["blk_hi"], 1)

            def reuse_parts(m, stored, done):
                act.wait_ge(s["scr_stored_a" if m == 0 else "scr_stored_b"], stored)
                act.wait_ge(s["blk_parts"], done)

            act.wait_ge(s["masks_ready"], 1)
            for i, (_, n) in enumerate(k_cols):
                for m in range(KT):
                    if i:
                        reuse_parts(m, 48 * i, KT * (i - 1) + m + 1)
                    block_split(KT * i + m, m, n, 1)
            act.wait_ge(s["masks_ready"], 2)
            act.activation(gauss[:], iota_w[:], ACT.Exp, scale=-1.0 / 128.0)

            def copy_xnT(n):
                act.wait_ge(s["xnT_psum"], n)
                act.copy(xnT[:], ps_m[:, 2:4, :]).then_inc(s["xnT_ready"], 1)

            for c in range(NC):
                copy_xnT(c + 1)
                if c + 2 < NC:
                    act.dma_start((xa, xb)[c % 2][:], x_dram[:, TT * (c + 2):TT * (c + 3), :]).then_inc(x_start[c % 2], 16)
                for m in range(KT):
                    reuse_parts(m, 48 * len(k_cols) + 48 * c, KBLK - 2 + m + 1 + KT * c)
                    block_split(KBLK + m + KT * c, m, CT, 0)
            act.wait_ge(s["win_psum"], 1)
            act.copy(win_k[:], ps_m[:, 0:2, 0:W])
            act.copy(win_v[:], ps_m[:, 2:4, 0:D]).then_inc(s["win_copied"], 1)

            def exps(c, k):
                n = rows_of(k % ST)
                need(act, s["pv_done"], SLOTS * c + k - 1)
                for h in range(HG):
                    act.wait_ge(s["qk_ready"], SLOTS * HG * c + HG * k + h + 1)
                    act.activation(probs[0:n, k % 2, h, :], ps_e[h % 2][0:n, :], ACT.Exp).then_inc(s["exp_done"], 1)

            def take_o(c, g):
                act.wait_ge(s["pv_done"], SLOTS * c + ST * (g + 1))
                need(act, s["att_ready"], NG * c + g)
                act.copy(o_raw[:], ps_o[:]).then_inc(s["o_taken"], 1)

            def take_xnT(names, c):
                for k, name in enumerate(names):
                    wait_filled(act, name, c)
                    taken(act.copy(xnT[:, k, :], bank(name)), name)

            def behind(c, k):
                if k == 9:
                    take_xnT(("t1a", "t1b"), c)
                if k == 11:
                    act.wait_ge(s["lg8_ready"], c + 1)
                    act.activation(ex8[:], lg8[:], ACT.Exp).then_inc(s["ex8_ready"], 1)
                if k == 15:
                    wait_filled(act, "gateT", c)
                    taken(act.copy(gateT[:], bank("gateT")[0:TT * NX, 0:P]), "gateT")
                if k == 30:
                    take_xnT(("t2a", "t2b"), c)
                if k == 32:
                    act.wait_ge(s["negmax_ready"], c + 1)
                    act.activation(tail[:], st4[:, 0, :], ACT.Exp, bias=neg_big[:, 0:1])
                    for t in range(TT):
                        last = act.activation(work2[:, t, :], work[:, t, :], ACT.Exp, bias=st4[:, 0, t:t + 1],
                                              accum_out=rowsum[:, t:t + 1])
                    last.then_inc(s["rowsum_ready"], 1)
                if k == 34:
                    for kk, name in enumerate(("aTa", "aTb")):
                        wait_filled(act, name, c)
                        taken(act.copy(aT[:, kk, :], bank(name)), name)
                if k in (35, 36):
                    name = f"z{k - 35}"
                    wait_filled(act, name, c)
                    taken(act.activation(work[:, 2 * (k - 35):2 * (k - 35) + 2, :].rearrange("p a w -> p (a w)"),
                                         bank(name), ACT.Tanh), name)
                if k == 39:
                    take_xnT(("t3a", "t3b"), c)
                if k == 40:
                    wait_filled(act, "h", c)
                    taken(act.activation(hT[:], bank("h"), ACT.Gelu, bias=hbias[:, 0:1]), "h")
                if k == 42:
                    act.wait_ge(s["lg_ready"], c + 1)
                    for t in range(TT):
                        last = act.activation(elg[:, t, :], lg[:, t, :], ACT.Exp, bias=st4[:, 1, t:t + 1])
                    last.then_inc(s["elg_ready"], 1)
                if k == 44:
                    wait_filled(act, "alphaT", c)
                    taken(act.copy(alphaT[0:NS, bass.ds(c * CT, CT)], bank("alphaT")[0:NS, :]), "alphaT")

            def chunk(c, first):
                for k in range(SLOTS):
                    g, st = k // ST, k % ST
                    if st == 1 and (g or not first):
                        take_o(c, g - 1)
                    exps(c, k)
                    if not first:
                        behind(c - 1, k - SHIFT)

            chunk(0, True)
            with act.Fori(1, NC) as c:
                chunk(c, False)
            take_o(NC, -1)
            for k in range(SLOTS):
                behind(NC - 1, k)
            act.wait_ge(s["p_rz"], 1)
            act.activation(rz, rz, ACT.Sigmoid).then_inc(s["p_sig"], 1)
            act.wait_ge(s["p_npre"], 1)
            act.activation(gate_n, gate_n, ACT.Tanh).then_inc(s["p_n"], 1)
            act.wait_ge(s["p_nmax"], 1)
            act.activation(att_s, ps_x[0:NS, 0:NS], ACT.Exp, bias=small[:, 2:3], scale=DQ ** -0.5,
                           accum_out=small[:, 3:4]).then_inc(s["p_exp"], 1)

        @block.tensor
        def _(pe):
            pe.wait_ge(s["ld_ctx"], 16)
            pe.wait_ge(s["ld_wqkv"], 48)
            for i, (col, n) in enumerate(k_cols):
                for m in range(KT):
                    if i:
                        pe.wait_ge(s["blk_hi"], KT * (i - 1) + m + 1)
                    for k in range(KT):
                        mm = pe.matmul(ps_e[m][:, 0:n], wqkv[:, 0, k, P * m:P * m + P], ctxT[:, k, col:col + n],
                                       start=(k == 0), stop=(k == KT - 1))
                    mm.then_inc(s["blk_psum"], 1)
            for st in range(ST):
                n = rows_of(st)
                if st >= 2:
                    pe.wait_ge(s["v_taken"], st - 1)
                for k in range(KT):
                    mm = pe.matmul(ps_m[0:n, st % 2, 0:D], ctxT[:, k, P * st:P * st + n], wqkv[:, 1, k, :],
                                   start=(k == 0), stop=(k == KT - 1))
                mm.then_inc(s["v_psum"], 1)
            pe.wait_ge(s["ld_const"], N_CONST)
            pe.wait_ge(s["mean_ready"], 1)
            for k in range(KT):
                mm = pe.matmul(ps_x[:, 0:1], w1[:, KT + k, :], slot_mean[:, k:k + 1], start=(k == 0), stop=(k == KT - 1))
            mm.then_inc(s["hb_psum"], 1)

            def transposes(n, bank=2):
                pe.wait_ge(s["xn_ready"], n)
                for k in range(KT):
                    for t in range(TT):
                        mm = pe.transpose(ps_m[:, bank + k, P * t:P * t + P], xn[:, t, P * k:P * k + P], ident[:])
                mm.then_inc(s["xnT_psum"], 1)
                pe.wait_ge(s["xnT_ready"], n)

            with pe.Fori(0, NC) as c:
                transposes(c + 1)
                for m in range(KT):
                    pe.wait_ge(s["blk_hi"], KBLK - 2 + m + 1 + KT * c)
                    for k in range(KT):
                        mm = pe.matmul(ps_e[m][:, :], wqkv[:, 2, k, P * m:P * m + P], xnT[:, k, :],
                                       start=(k == 0), stop=(k == KT - 1))
                    mm.then_inc(s["blk_psum"], 1)
            pe.wait_ge(s["ld_encwin"], 16)
            pe.wait_ge(s["ld_wac"], 16)
            pe.wait_ge(s["v_taken"], ST)
            for m in range(KT):
                for k in range(KT):
                    pe.matmul(ps_m[:, m, 0:W], wa_c[:, k, P * m:P * m + P], enc_win[:, k, :],
                              start=(k == 0), stop=(k == KT - 1))
            for m in range(KT):
                for k in range(KT):
                    mm = pe.matmul(ps_m[:, 2 + m, 0:D], enc_win[:, k, P * m:P * m + P], wc[:, k, :],
                                   start=(k == 0), stop=(k == KT - 1))
            mm.then_inc(s["win_psum"], 1)
            pe.wait_ge(s["win_copied"], 1)
            pe.wait_ge(s["hb_ready"], 1)
            pe.wait_ge(s["blk_hi"], KBLK + KT * NC)

            def max_unit(u, c, j):
                g, n1 = j % NG, NG * c + j
                t, h, q = u // (QUARTERS * HG), (u // QUARTERS) % HG, u % QUARTERS
                if u == 0:
                    pe.wait_ge(q_loaded[j % NG], 96 * (c + j // NG + 1))
                need(pe, s["max_taken"], UNITS * n1 + u - 1)
                pe.matmul(ps_m[:, u % 2, 0:SPLIT], qst[0:MAX_ROW, g, h, P * t:P * t + P],
                          kst[0:MAX_ROW, HG * g + h, QUARTER_START[q]:QUARTER_START[q] + SPLIT],
                          start=True, stop=True).then_inc(s["max_ready"], 1)

            def max_rows(n1):
                need(pe, s["att_ready"], n1 - 1)
                pe.wait_ge(s["mx_ready"], n1 + 1)
                pe.transpose(ps_x[0:HG * TT, 0:P], mxc[:], ident[:]).then_inc(s["mT_ready"], 1)

            pe.wait_ge(s["ld_k"], 16 * (2 + NG + 3 + 6))
            for v in range(UNITS + LEAD):
                max_unit(v % UNITS, 0, v // UNITS)
            max_rows(0)
            pe.wait_ge(s["ld_fill"], N_FILL)
            pe.wait_ge(s["ld_expert"], 32)

            def pv(c, k, half):
                cols = slice(CT // 2 * half, CT // 2 * (half + 1))
                g, st = k // ST % NG, k % ST
                n = rows_of(st)
                if half == 0:
                    if st == 0:
                        need(pe, s["o_taken"], NG * c + g)
                    pe.wait_ge(s["exp_done"], HG * (SLOTS * c + k + 1))
                for h in range(HG):
                    mm = pe.matmul(ps_o[32 * h:32 * h + 32, cols], v_sb[0:n, st, HG * g + h, :],
                                   probs[0:n, k % 2, h, cols], start=(st == 0 and half == 0),
                                   stop=(st == ST - 1 and half == 1))
                if half == 1:
                    mm.then_inc(s["pv_done"], 1)

            def z_columns(c, g):
                pe.wait_ge(s["o_taken"], NG * c + g + 1)
                pe.wait_ge(s["mrow_ready"], NG * c + g + 2)
                for t in range(TT):
                    mm = pe.matmul(ps_x[:, HG * t:HG * t + HG], o_raw[:, P * t:P * t + P], z_pick[:],
                                   start=True, stop=True)
                mm.then_inc(s["z_cols"], 1)

            def spread_z(c, g):
                pe.wait_ge(s["z_repeated"], NG * c + g + 1)
                for t in range(TT):
                    mm = pe.matmul(ps_x[:, P * t:P * t + P], z_sb[:, P * t:P * t + P], ident[:], start=True, stop=True)
                mm.then_inc(s["z_ready"], 1)

            def to_xnT(names, n, c):
                pe.wait_ge(s["xn_ready"], n)
                for k, name in enumerate(names):
                    bank_free(pe, name, c)
                    for t in range(TT):
                        mm = pe.transpose(bank(name)[:, P * t:P * t + P], xn[:, t, P * k:P * k + P], ident[:])
                    filled(mm, name)

            def xnT_there(names, c):
                for name in names:
                    wait_taken(pe, name, c)

            def experts(i, c):
                name, t, j = f"e{i}", i // 4, i % 4
                bank_free(pe, name, c)
                for k in range(KT):
                    mm = pe.matmul(bank(name), xnT[:, k, P * t:P * t + P], expert_w[:, k, CT * j:CT * j + CT],
                                   start=(k == 0), stop=(k == KT - 1))
                filled(mm, name)

            def behind(c, k):
                if k in (5, 6):
                    name = f"y{k - 5}"
                    pe.wait_ge(s["att_ready"], NG * (c + 1))
                    bank_free(pe, name, c)
                    for t in range(2):
                        tok = P * (2 * (k - 5) + t)
                        for g in range(NG):
                            mm = pe.matmul(bank(name)[:, D * t:D * t + D], attc[:, g, tok:tok + P], wo_pad[:, g, :],
                                           start=(g == 0), stop=(g == NG - 1))
                    filled(mm, name)
                if k == 9:
                    to_xnT(("t1a", "t1b"), NC + 3 * c + 1, c)
                if k == 10:
                    xnT_there(("t1a", "t1b"), c)
                    bank_free(pe, "router", c)
                    for t in range(TT):
                        for kk in range(KT):
                            mm = pe.matmul(bank("router")[:, NX * t:NX * t + NX], xnT[:, kk, P * t:P * t + P],
                                           rw[:, kk, :], start=(kk == 0), stop=(kk == KT - 1))
                    filled(mm, "router")
                if k == 15:
                    pe.wait_ge(s["gate_ready"], c + 1)
                    bank_free(pe, "gateT", c)
                    filled(pe.transpose(bank("gateT")[0:TT * NX, 0:P], hot8[:].rearrange("p t e -> p (t e)"), ident[:]),
                           "gateT")
                if 11 <= k < 19:
                    experts(k - 11, c)
                if k == 19:
                    wait_taken(pe, "gateT", c)
                    for i in range(2):
                        bank_free(pe, f"gb{i}", c)
                        for t in range(2):
                            mm = pe.matmul(bank(f"gb{i}")[:, D * t:D * t + D], gateT[:], eb[:, 2 * i + t, :],
                                           start=True, stop=True)
                        filled(mm, f"gb{i}")
                if 20 <= k < 28:
                    experts(k - 12, c)
                if k == 30:
                    to_xnT(("t2a", "t2b"), NC + 3 * c + 2, c)
                if k == 31:
                    xnT_there(("t2a", "t2b"), c)
                    for i in range(2):
                        name = f"score{i}"
                        bank_free(pe, name, c)
                        for t in range(2):
                            for kk in range(KT):
                                tok = P * (2 * i + t)
                                mm = pe.matmul(bank(name)[:, W * t:W * t + W], xnT[:, kk, tok:tok + P], win_k[:, kk, :],
                                               start=(kk == 0), stop=(kk == KT - 1))
                        filled(mm, name)
                if k == 34:
                    pe.wait_ge(s["a_ready"], c + 1)
                    for kk, name in enumerate(("aTa", "aTb")):
                        bank_free(pe, name, c)
                        for t in range(TT):
                            mm = pe.transpose(bank(name)[:, P * t:P * t + P], work[:, t, P * kk:P * kk + P], ident[:])
                        filled(mm, name)
                if k in (35, 36):
                    xnT_there(("aTa", "aTb"), c)
                    name = f"z{k - 35}"
                    bank_free(pe, name, c)
                    for t in range(2):
                        tok = P * (2 * (k - 35) + t)
                        o = bank(name)[:, D * t:D * t + D]
                        for kk in range(KT):
                            pe.matmul(o, aT[:, kk, tok:tok + P], win_v[:, kk, :], start=(kk == 0), stop=False)
                        for kk in range(KT):
                            mm = pe.matmul(o, xnT[:, kk, tok:tok + P], wc[:, KT + kk, :], start=False, stop=(kk == KT - 1))
                    filled(mm, name)
                if k == 39:
                    to_xnT(("t3a", "t3b"), NC + 3 * c + 3, c)
                if k == 40:
                    xnT_there(("t3a", "t3b"), c)
                    bank_free(pe, "h", c)
                    for kk in range(KT):
                        mm = pe.matmul(bank("h"), w1[:, kk, :], xnT[:, kk, :], start=(kk == 0), stop=(kk == KT - 1))
                    filled(mm, "h")
                if k == 41:
                    wait_taken(pe, "h", c)
                    bank_free(pe, "logits", c)
                    for t in range(TT):
                        mm = pe.matmul(bank("logits")[:, NS * t:NS * t + NS], hT[:, P * t:P * t + P], w2[:],
                                       start=True, stop=True)
                    filled(mm, "logits")
                if k == 44:
                    pe.wait_ge(s["alpha_ready"], c + 1)
                    bank_free(pe, "slots", c)
                    bank_free(pe, "alphaT", c)
                    for t in range(TT):
                        mm = pe.matmul(bank("slots")[0:NS, 0:D + 1], alpha[:, t, :], xn[:, t, :],
                                       start=(t == 0), stop=(t == TT - 1))
                    filled(mm, "slots")
                    for t in range(TT):
                        mm = pe.transpose(bank("alphaT")[0:NS, P * t:P * t + P], alpha[:, t, :], ident[:])
                    filled(mm, "alphaT")

            def chunk(c, first):
                for k in range(SLOTS):
                    g, st = k // ST, k % ST
                    n = rows_of(st)
                    if st == 0:
                        pe.wait_ge(m_loaded[g], 32 * (c + 1))
                    units = units_of(k)
                    for h in range(HG):
                        if h == 2:
                            if not first:
                                behind(c - 1, k - SHIFT)
                            if k or not first:
                                pv(c, k - 1, 0)
                        need(pe, s["exp_done"], HG * SLOTS * c + HG * k + h - 1)
                        pe.matmul(ps_e[h % 2][0:n, :], kst[0:ROWS, HG * g + h, P * st:P * st + n],
                                  qst[0:ROWS, g, h, :], start=True, stop=True).then_inc(s["qk_ready"], 1)
                        for j, u in units[h:h + 1]:
                            max_unit(u, c, j)
                    if k or not first:
                        pv(c, k - 1, 1)
                    for j, u in units[HG:]:
                        max_unit(u, c, j)
                    if st == 2 and (g or not first):
                        z_columns(c, g - 1)
                    if st == 4 and (g or not first):
                        spread_z(c, g - 1)
                    if max_end(k - 1) is not None:
                        max_rows(NG * c + max_end(k - 1))

            chunk(0, True)
            with pe.Fori(1, NC) as c:
                chunk(c, False)
            for half in range(2):
                pv(NC, -1, half)
            z_columns(NC, -1)
            spread_z(NC, -1)
            for k in range(SLOTS):
                behind(NC - 1, k)
            for name in ("slots", "alphaT"):
                wait_taken(pe, name, NC - 1)

            def transpose_slots(src, ready, done):
                pe.wait_ge(s[ready], 1)
                for k in range(KT):
                    mm = pe.transpose(ps_x[:, NS * k:NS * k + NS], src[:, P * k:P * k + P], ident[0:NS, 0:NS])
                mm.then_inc(s[done], 1)

            def product(out, lhsT, rhs, first=True, last=True):
                for k in range(KT):
                    mm = pe.matmul(out, lhsT[:, k, :], rhs[:, k, :], start=(first and k == 0), stop=(last and k == KT - 1))
                return mm

            transpose_slots(vec, "p_si", "p_siT_ps")
            pe.wait_ge(s["ld_slot"], 16 * len(slot_loads))
            pe.wait_ge(s["p_siT"], 1)
            product(ps_m[0:NS, 0, :], sT, wihT[:, :, 0:2 * D], last=False)
            product(ps_m[0:NS, 0, :], slotT, whhT[:, :, 0:2 * D], first=False)
            product(ps_m[0:NS, 1, 0:D], sT, wihT[:, :, 2 * D:3 * D])
            product(ps_m[0:NS, 2, 0:D], slotT, whhT[:, :, 2 * D:3 * D]).then_inc(s["p_gi"], 1)
            transpose_slots(s_new, "p_snew", "p_snT_ps")
            pe.wait_ge(s["p_snT"], 1)
            product(ps_e[0][0:DQ, 0:NS], wqs, sT)
            product(ps_e[1][0:DQ, 0:NS], wks, sT)
            product(ps_m[0:NS, 3, 0:D], sT, wvs).then_inc(s["p_qkv"], 1)
            pe.wait_ge(s["p_qkT"], 1)
            pe.matmul(ps_x[0:NS, 0:NS], qkT[:, 0, :], qkT[:, 1, :], start=True, stop=True).then_inc(s["p_lg"], 1)
            pe.wait_ge(s["p_attn"], 1)
            pe.transpose(ps_x[0:NS, P:P + NS], att_s, ident[0:NS, 0:NS]).then_inc(s["p_attT_ps"], 1)
            pe.wait_ge(s["p_attT"], 1)
            pe.matmul(ps_m[0:NS, 0, 0:D], att_sT, comm, start=True, stop=True).then_inc(s["p_comm"], 1)
            transpose_slots(y_ln, "p_y", "p_yT_ps")
            pe.wait_ge(s["p_yT"], 1)
            product(ps_m[0:NS, 1, 0:D], sT, wvps).then_inc(s["p_sv"], 1)
            transpose_slots(vec, "p_svb", "p_svT_ps")
            pe.wait_ge(s["p_svT"], 1)
            product(ps_m[0:NS, 2, 0:D], sT, wos).then_inc(s["p_svo"], 1)
            pe.wait_ge(s["p_svo_sb"], 1)
            for c in range(NC):
                if c >= 2:
                    pe.wait_ge(s["out_ready"], c - 1)
                for t in range(TT):
                    mm = pe.matmul(ps_m[:, 2 * (c % 2) + t // 2, D * (t % 2):D * (t % 2) + D],
                                   alphaT[:, CT * c + P * t:CT * c + P * t + P], svo, start=True, stop=True)
                mm.then_inc(s["out_psum"], 1)

        @block.vector
        def _(dve):
            dve.wait_ge(s["ld_cond"], 96)
            dve.wait_ge(s["ld_const"], N_CONST)
            scale = E ** -0.5
            dve.tensor_scalar(tau[:, 2:3], tau[:, 0:1], scale, None, ALU.mult)
            dve.tensor_scalar(win_f[:, 2:3], win_f[:, 0:1], -float(W // 2), 0.0, ALU.add, ALU.max)
            dve.tensor_copy(win_f[:, 4:5], win_i[:, 0:1])
            dve.tensor_scalar(rtau[:, 1:2], rtau[:, 0:1], -1.0, None, ALU.mult)
            dve.drain()
            dve.tensor_scalar(qk_bias[:, 0, :], qk_bias[:, 0, :], tau[:, 2:3], None, ALU.mult)
            dve.tensor_scalar(win_f[:, 3:4], win_f[:, 2:3], float(S - W), None, ALU.min)
            dve.tensor_scalar(win_f[:, 5:6], win_f[:, 0:1], -16.0, 0.0, ALU.add, ALU.max)
            dve.tensor_scalar(win_f[:, 6:7], win_f[:, 0:1], 16.0, win_f[:, 4:5], ALU.add, ALU.min)
            dve.tensor_tensor(rtau[:, 0:1], rtau[:, 0:1], rtau[:, 1:2], ALU.max)
            dve.drain()
            dve.tensor_copy(win_i[:, 1:2], win_f[:, 3:4]).then_inc(s["masks_ready"], 1)
            dve.tensor_scalar(rtau[:, 0:1], rtau[:, 0:1], 0.1, None, ALU.add)
            dve.drain()
            dve.tensor_copy(win_f[:, 7:8], win_i[:, 1:2]).then_inc(s["window_start"], 1)
            dve.reciprocal(rtau[:, 1:2], rtau[:, 0:1])
            dve.drain()
            dve.tensor_scalar(iota_w[:], iota_w[:], win_f[:, 7:8], None, ALU.add)
            dve.drain()
            dve.tensor_scalar(keep[:], iota_w[:], win_f[:, 5:6], None, ALU.is_ge)
            dve.tensor_scalar(gauss[:], iota_w[:], win_f[:, 6:7], None, ALU.is_le)
            dve.tensor_scalar(iota_w[:], iota_w[:], win_f[:, 0:1], None, ALU.subtract)
            dve.drain()
            dve.tensor_tensor(keep[:], keep[:], gauss[:], ALU.mult)
            dve.drain()
            dve.tensor_scalar(neg_mask[:], keep[:], -1.0, BIG, ALU.add, ALU.mult)
            dve.tensor_tensor(iota_w[:], iota_w[:], iota_w[:], ALU.mult).then_inc(s["masks_ready"], 1)
            dve.tensor_reduce(slot_mean[:], slotT[:], AX.X, ALU.add)
            dve.drain()
            dve.tensor_scalar(slot_mean[:], slot_mean[:], 1.0 / NS, None, ALU.mult).then_inc(s["mean_ready"], 1)
            dve.wait_ge(s["ld_delta"], 16)
            dve.tensor_scalar(delta_a, delta_a, scale, None, ALU.mult)
            dve.drain()
            dve.tensor_copy(delta3[:, 0, :], delta_a)
            dve.drain()
            dve.tensor_tensor(delta_b, delta_a, delta3[:, 0, :], ALU.subtract)
            dve.drain()
            dve.tensor_copy(delta3[:, 1, :], delta_b)
            dve.drain()
            dve.tensor_tensor(delta3[:, 2, :], delta_b, delta3[:, 1, :], ALU.subtract).then_inc(s["delta_parts"], 1)

            def split(b, m, n):
                dve.wait_ge(s["blk_hi"], b + 1)
                dve.tensor_tensor(rest[:, m, 0:n], q32[:, m, 0:n], parts[:, m, 0, 0:n], ALU.subtract)
                dve.drain()
                dve.tensor_copy(parts[:, m, 1, 0:n], rest[:, m, 0:n])
                dve.drain()
                dve.tensor_tensor(parts[:, m, 2, 0:n], rest[:, m, 0:n], parts[:, m, 1, 0:n], ALU.subtract)\
                   .then_inc(s["blk_parts"], 1)

            for i, (_, n) in enumerate(k_cols):
                for m in range(KT):
                    split(KT * i + m, m, n)
            dve.wait_ge(s["consts_set"], 2)
            for st in range(ST):
                n = rows_of(st)
                dve.wait_ge(s["v_psum"], st + 1)
                dve.tensor_tensor(v_sb[0:n, st, :, 0:E], ps_m[0:n, st % 2, 0:D].rearrange("p (h e) -> p h e", h=H),
                                  bv0[0:n, :].rearrange("p (h e) -> p h e", h=H), ALU.add).then_inc(s["v_taken"], 1)
            dve.wait_ge(s["hb_psum"], 1)
            dve.tensor_tensor(hbias[:], ps_x[:, 0:1], b1[:], ALU.add).then_inc(s["hb_ready"], 1)

            def layernorm(src, n):
                dve.drain()
                for t in range(TT):
                    dve.bn_stats(bst[:, t, :], src(t))
                dve.drain()
                for t in range(TT):
                    last = dve.bn_aggr(mv[:, t, :], bst[:, t, :])
                last.then_inc(s["var_ready"], 1)
                dve.wait_ge(s["rstd_ready"], n)
                for t in range(TT):
                    last = dve.tensor_scalar(xn[:, t, 0:D], src(t), mv[:, t, 0:1], rstd[:, t:t + 1], ALU.subtract, ALU.mult)
                last.then_inc(s["xn_ready"], 1)

            for c in range(NC):
                x_chunk = (xa, xb)[c % 2]
                dve.wait_ge(x_start[c % 2], 16 * (c // 2 + 1))
                layernorm(lambda t: x_chunk[:, t, :], c + 1)
                for m in range(KT):
                    split(KBLK + m + KT * c, m, CT)

            def take_max(u, n1):
                t, h, q = u // (QUARTERS * HG), (u // QUARTERS) % HG, u % QUARTERS
                dve.wait_ge(s["max_ready"], UNITS * n1 + u + 1)
                col = TT * h + t
                dve.tensor_reduce(mx[:, q, col:col + 1], ps_m[:, u % 2, 0:SPLIT], AX.X, ALU.max)\
                   .then_inc(s["max_taken"], 1)

            def max_columns():
                dve.drain()
                dve.tensor_reduce(mxc[:], mx[:].rearrange("p q c -> p c q"), AX.X, ALU.max).then_inc(s["mx_ready"], 1)
                dve.drain()

            def max_out(n1):
                dve.wait_ge(s["mT_ready"], n1 + 1)
                dve.tensor_scalar(mrow[:, 0, :], ps_x[0:HG * TT, 0:P], -1.0, None, ALU.mult)
                dve.drain()
                dve.scalar_tensor_tensor(out=mrow[:, 1, :], in0=ps_x[0:HG * TT, 0:P], scalar=-1.0, in1=mrow[:, 0, :],
                                         op0=ALU.mult, op1=ALU.subtract).then_inc(s["mrow_ready"], 1)

            for v in range(UNITS + LEAD):
                take_max(v % UNITS, v // UNITS)
                if v == UNITS - 1:
                    max_columns()
            max_out(0)

            def invert_z(c, g):
                dve.wait_ge(s["z_cols"], NG * c + g + 1)
                dve.reciprocal(z_inv[:], ps_x[:, 0:TT * HG]).then_inc(s["z_inverted"], 1)

            def normalise(c, g):
                dve.wait_ge(s["z_ready"], NG * c + g + 1)
                dve.tensor_tensor(attc[:, g % NG, :], o_raw[:], ps_x[:], ALU.mult).then_inc(s["att_ready"], 1)

            def stats(src):
                dve.drain()
                for t in range(TT):
                    dve.bn_stats(bst[:, t, :], src[:, t, :])
                dve.drain()
                for t in range(TT):
                    last = dve.bn_aggr(mv[:, t, :], bst[:, t, :])
                last.then_inc(s["var_ready"], 1)

            def take_experts(i, c):
                t, j = i // 4, i % 4
                for e in (2 * j, 2 * j + 1):
                    dve.drain()
                    if e % 2 == 0:
                        wait_filled(dve, f"e{i}", c)
                    last = dve.scalar_tensor_tensor(out=xb[:, t, :], in0=bank(f"e{i}")[:, D * (e % 2):D * (e % 2) + D],
                                                    scalar=hot8[:, t, e:e + 1], in1=(xb if e else xa)[:, t, :],
                                                    op0=ALU.mult, op1=ALU.add)
                taken(last, f"e{i}")

            def behind(c, k):
                if k in (6, 7):
                    i = k - 6
                    dve.wait_ge(s["xres_ready"], c + 1)
                    wait_filled(dve, f"y{i}", c)
                    taken(dve.tensor_tensor(xa[:, 2 * i:2 * i + 2, :], xres[:, 2 * i:2 * i + 2, :],
                                            bank(f"y{i}").rearrange("p (a d) -> p a d", a=2), ALU.add), f"y{i}")
                if k == 7:
                    stats(xa)
                if k == 11:
                    wait_filled(dve, "router", c)
                    taken(dve.tensor_tensor(lg8[:], bank("router")[:, 0:TT * NX].rearrange("p (t e) -> p t e", t=TT),
                                            rb[:].unsqueeze(1).broadcast_to((P, TT, NX)), ALU.add), "router")
                    dve.drain()
                    dve.tensor_reduce(st4[:, 2, :], lg8[:], AX.X, ALU.max)
                    dve.drain()
                    top = st4[:, 2, :].unsqueeze(2).broadcast_to((P, TT, NX))
                    dve.tensor_tensor(hot8[:], lg8[:], top, ALU.is_equal)
                    dve.drain()
                    dve.tensor_tensor(lg8[:], lg8[:], top, ALU.subtract).then_inc(s["lg8_ready"], 1)
                    dve.tensor_tensor(hot8[:], hot8[:], rank[:].unsqueeze(1).broadcast_to((P, TT, NX)), ALU.mult)
                    dve.drain()
                    dve.tensor_reduce(st4[:, 3, :], hot8[:], AX.X, ALU.max)
                    dve.drain()
                    dve.tensor_tensor(hot8[:], hot8[:], st4[:, 3, :].unsqueeze(2).broadcast_to((P, TT, NX)), ALU.is_equal)
                if k == 12:
                    dve.wait_ge(s["ex8_ready"], c + 1)
                    dve.tensor_reduce(st4[:, 4, :], ex8[:], AX.X, ALU.add)
                    dve.drain()
                    dve.reciprocal(st4[:, 5, :], st4[:, 4, :])
                    dve.drain()
                    dve.tensor_tensor(hot8[:], hot8[:], st4[:, 5, :].unsqueeze(2).broadcast_to((P, TT, NX)), ALU.mult)\
                       .then_inc(s["gate_ready"], 1)
                if 12 <= k < 20:
                    take_experts(k - 12, c)
                if k == 20:
                    for i, dst in enumerate((xb[:, 0:2, :], xa[:, 2:4, :])):
                        dve.drain()
                        wait_filled(dve, f"gb{i}", c)
                        taken(dve.tensor_tensor(dst, dst, bank(f"gb{i}").rearrange("p (a d) -> p a d", a=2), ALU.add),
                              f"gb{i}")
                if 21 <= k < 29:
                    take_experts(k - 13, c)
                if k == 28:
                    stats(xb)
                if k == 32:
                    for i in range(2):
                        wait_filled(dve, f"score{i}", c)
                        taken(dve.tensor_tensor(work[:, 2 * i:2 * i + 2, :],
                                                bank(f"score{i}").rearrange("p (a w) -> p a w", a=2),
                                                keep[:].unsqueeze(1).broadcast_to((P, 2, W)), ALU.mult), f"score{i}")
                    dve.drain()
                    dve.tensor_tensor(work[:], work[:], neg_mask[:].unsqueeze(1).broadcast_to((P, TT, W)), ALU.add)
                    dve.drain()
                    dve.tensor_reduce(st4[:, 6, :], work[:], AX.X, ALU.max)
                    dve.drain()
                    dve.tensor_scalar(st4[:, 0, :], st4[:, 6, :], -BIG, -1.0, ALU.max, ALU.mult)\
                       .then_inc(s["negmax_ready"], 1)
                if k == 33:
                    dve.wait_ge(s["rowsum_ready"], c + 1)
                    dve.scalar_tensor_tensor(out=rowsum[:], in0=tail[:], scalar=float(S - W), in1=rowsum[:],
                                             op0=ALU.mult, op1=ALU.add)
                    dve.drain()
                    dve.reciprocal(st4[:, 6, :], rowsum[:])
                    dve.drain()
                    for t in range(TT):
                        last = dve.scalar_tensor_tensor(out=work[:, t, :], in0=work2[:, t, :], scalar=st4[:, 6, t:t + 1],
                                                        in1=gauss[:], op0=ALU.mult, op1=ALU.mult)
                    last.then_inc(s["a_ready"], 1)
                if k == 37:
                    wait_taken(dve, "z0", c)
                    wait_taken(dve, "z1", c)
                    dve.tensor_tensor(xres[:], xb[:], work[:], ALU.add).then_inc(s["x3_ready"], 1)
                    stats(xres)
                if k == 42:
                    wait_filled(dve, "logits", c)
                    taken(dve.tensor_tensor(lg, bank("logits")[:, 0:TT * NS].rearrange("p (t n) -> p t n", t=TT),
                                            b2[:].unsqueeze(1).broadcast_to((P, TT, NS)), ALU.add), "logits")
                    dve.drain()
                    dve.tensor_scalar(lg, lg, rtau[:, 1:2], None, ALU.mult)
                    dve.drain()
                    for t in range(TT):
                        dve.max(top8[:, t, :], lg[:, t, :])
                    dve.drain()
                    dve.tensor_scalar(st4[:, 1, :], top8[:, :, 0], -1.0, None, ALU.mult).then_inc(s["lg_ready"], 1)
                    for t in range(TT):
                        dve.match_replace(lgr[:, t, :], top8[:, t, :], lg[:, t, :], -3.0e38)
                    dve.drain()
                    dve.tensor_tensor(lgr, lg, lgr, ALU.not_equal)
                if k == 43:
                    dve.drain()
                    dve.wait_ge(s["elg_ready"], c + 1)
                    dve.tensor_tensor(elg, elg, lgr, ALU.mult)
                    dve.drain()
                    dve.tensor_reduce(st4[:, 4, :], elg, AX.X, ALU.add)
                    dve.drain()
                    dve.reciprocal(st4[:, 5, :], st4[:, 4, :])
                    dve.drain()
                    dve.tensor_tensor(alpha, elg, st4[:, 5, :].unsqueeze(2).broadcast_to((P, TT, NS)), ALU.mult)\
                       .then_inc(s["alpha_ready"], 1)
                if k == 45:
                    wait_filled(dve, "slots", c)
                    taken(dve.tensor_tensor(slot_acc[:], slot_acc[:], bank("slots")[0:NS, 0:D + 1], ALU.add), "slots")
                    dve.drain()

            def chunk(c, first):
                for k in range(SLOTS):
                    g, st = k // ST, k % ST
                    if st == 3 and (g or not first):
                        invert_z(c, g - 1)
                    if st == 5 and (g or not first):
                        if g == 1 and not first:
                            wait_filled(dve, "y1", c - 1)
                        normalise(c, g - 1)
                    if not first:
                        behind(c - 1, k - SHIFT)
                    for j, u in units_of(k):
                        take_max(u, NG * c + j)
                    if max_end(k - 1) is not None:
                        j = max_end(k - 1)
                        need(dve, m_loaded[(j - 1) % NG], 32 * (c + (j - 1) // NG + 1))
                        max_out(NG * c + j)
                    if max_end(k) is not None:
                        max_columns()

            chunk(0, True)
            with dve.Fori(1, NC) as c:
                chunk(c, False)
            invert_z(NC, -1)
            normalise(NC, -1)
            for k in range(SLOTS):
                behind(NC - 1, k)

            dve.memset(alphaT_raw[NS:NS + 1, :], 1.0)
            dve.wait_ge(s["ld_slot"], 16 * len(slot_loads))
            dve.tensor_scalar(small[:, 0:1], slot_acc[:, D:D + 1], 1e-8, None, ALU.add)
            dve.drain()
            dve.reciprocal(small[:, 1:2], small[:, 0:1])
            dve.drain()
            dve.tensor_scalar(vec, slot_acc[:, 0:D], small[:, 1:2], None, ALU.mult).then_inc(s["p_si"], 1)
            dve.tensor_tensor(b_ih[:, 0:2 * D], b_ih[:, 0:2 * D], b_hh[:, 0:2 * D], ALU.add)

            def copy_T(ready, done):
                dve.wait_ge(s[ready], 1)
                dve.tensor_copy(sT, ps_x[:, 0:KT * NS].rearrange("p (k n) -> p k n", k=KT)).then_inc(s[done], 1)

            copy_T("p_siT_ps", "p_siT")
            dve.wait_ge(s["p_gi"], 1)
            dve.tensor_tensor(rz, ps_m[0:NS, 0, :], b_ih[:, 0:2 * D], ALU.add).then_inc(s["p_rz"], 1)
            dve.tensor_tensor(gate_n, ps_m[0:NS, 1, 0:D], b_ih[:, 2 * D:3 * D], ALU.add)
            dve.tensor_tensor(hid_n, ps_m[0:NS, 2, 0:D], b_hh[:, 2 * D:3 * D], ALU.add)
            dve.wait_ge(s["p_sig"], 1)
            dve.drain()
            dve.tensor_tensor(hid_n, hid_n, rz[:, 0:D], ALU.mult)
            dve.drain()
            dve.tensor_tensor(gate_n, gate_n, hid_n, ALU.add).then_inc(s["p_npre"], 1)
            dve.wait_ge(s["p_n"], 1)
            dve.tensor_tensor(s_new, slot0, gate_n, ALU.subtract)
            dve.drain()
            dve.tensor_tensor(s_new, s_new, rz[:, D:2 * D], ALU.mult)
            dve.drain()
            dve.tensor_tensor(s_new, s_new, gate_n, ALU.add).then_inc(s["p_snew"], 1)
            copy_T("p_snT_ps", "p_snT")
            dve.wait_ge(s["p_qkv"], 1)
            for i in range(2):
                dve.tensor_scalar(qkT[:, i, :], ps_e[i][0:DQ, 0:NS], b_qk[:, i:i + 1], None, ALU.add)
            dve.tensor_tensor(comm, ps_m[0:NS, 3, 0:D], b_v, ALU.add).then_inc(s["p_qkT"], 1)
            dve.wait_ge(s["p_lg"], 1)
            dve.tensor_reduce(small[:, 4:5], ps_x[0:NS, 0:NS], AX.X, ALU.max)
            dve.drain()
            dve.tensor_scalar(small[:, 2:3], small[:, 4:5], -(DQ ** -0.5), None, ALU.mult).then_inc(s["p_nmax"], 1)
            dve.wait_ge(s["p_exp"], 1)
            dve.reciprocal(small[:, 5:6], small[:, 3:4])
            dve.drain()
            dve.tensor_scalar(att_s, att_s, small[:, 5:6], None, ALU.mult).then_inc(s["p_attn"], 1)
            dve.wait_ge(s["p_attT_ps"], 1)
            dve.tensor_copy(att_sT, ps_x[0:NS, P:P + NS]).then_inc(s["p_attT"], 1)
            dve.wait_ge(s["p_comm"], 1)
            dve.tensor_tensor(y_ln, s_new, ps_m[0:NS, 0, 0:D], ALU.add)
            dve.drain()
            dve.bn_stats(bst[0:NS, 0, :], y_ln)
            dve.drain()
            dve.bn_aggr(small[:, 7:9], bst[0:NS, 0, :]).then_inc(s["p_var"], 1)
            dve.wait_ge(s["p_rstd"], 1)
            dve.tensor_scalar(y_ln, y_ln, small[:, 7:8], small[:, 10:11], ALU.subtract, ALU.mult)
            dve.drain()
            dve.tensor_tensor(y_ln, y_ln, ln_g, ALU.mult)
            dve.drain()
            dve.tensor_tensor(y_ln, y_ln, ln_b, ALU.add).then_inc(s["p_y"], 1)
            copy_T("p_yT_ps", "p_yT")
            dve.wait_ge(s["p_sv"], 1)
            dve.tensor_tensor(vec, ps_m[0:NS, 1, 0:D], b_vp, ALU.add).then_inc(s["p_svb"], 1)
            copy_T("p_svT_ps", "p_svT")
            dve.wait_ge(s["p_svo"], 1)
            dve.tensor_copy(svo[0:NS, :], ps_m[0:NS, 2, 0:D]).then_inc(s["p_svo_sb"], 1)
            dve.wait_ge(s["x_end_loaded"], 16)
            for c in range(NC):
                dve.wait_ge(s["out_psum"], c + 1)
                tok = x_end[:, TT * c:TT * c + TT, :].rearrange("p (b a) d -> p b (a d)", b=2)
                dve.tensor_tensor(tok, tok, ps_m[:, 2 * (c % 2):2 * (c % 2) + 2, :], ALU.add).then_inc(s["out_ready"], 1)


def kernel(**inputs):
    import numpy as np
    import concourse.bacc as bacc
    from concourse import mybir as _mybir
    from concourse.bass_utils import run_bass_kernel_spmd

    x = {k: np.asarray(v) for k, v in inputs.items()}
    z_pick = np.zeros((P, HG), np.float32)
    for h in range(HG):
        z_pick[32 * h + E, h] = 1.0
    arrays = {
        "x": x["x"][0], "ctxT": x["ctx_1024"][0].T, "condB_tau": x["condB_tau"], "fside": x["fside_BxS2_0"][0],
        "condB_pt": x["condB_pt"], "lenS2": x["_lenS2"],
        "L0_WqT": x["L0_xcond_Wq"].T, "L0_WkT": x["L0_xcond_Wk"].T, "L0_WvT": x["L0_xcond_Wv"].T,
        "L0_WoT": x["L0_xcond_Wo"].T, "L0_bq": x["L0_xcond_bq"], "L0_bk": x["L0_xcond_bk"],
        "L0_bv": x["L0_xcond_bv"], "L0_bo": x["L0_xcond_bo"],
        "router_wT": x["L0_ffn_router_w"].T, "router_b": x["L0_ffn_router_b"],
        "expert_wT": x["L0_ffn_expert_w"].transpose(2, 0, 1).reshape(KT, P, NX * D), "expert_b": x["L0_ffn_expert_b"],
        "L1_W_aT": x["L1_xcond_W_a"].T, "L1_W_cT": x["L1_xcond_W_c"].T,
        "slot_init": x["L1_ffn_slot_init"], "slot_initT": x["L1_ffn_slot_init"].T,
        "w1": x["L1_ffn_w1"], "b1": x["L1_ffn_b1"], "w2": x["L1_ffn_w2"], "b2": x["L1_ffn_b2"],
        "L1_tau": x["L1_ffn_tau"], "WihT": x["L1_ffn_Wih"].T, "WhhT": x["L1_ffn_Whh"].T,
        "bih": x["L1_ffn_bih"], "bhh": x["L1_ffn_bhh"], "wq": x["L1_ffn_wq"], "bq": x["L1_ffn_bq"],
        "wk": x["L1_ffn_wk"], "bk": x["L1_ffn_bk"], "wv": x["L1_ffn_wv"], "bv": x["L1_ffn_bv"],
        "ln_g": x["L1_ffn_ln_g"], "ln_b": x["L1_ffn_ln_b"], "wvp": x["L1_ffn_wvp"], "bvp": x["L1_ffn_bvp"],
        "wo": x["L1_ffn_wo"], "L1_bo": x["L1_ffn_bo"],
        "c_ident": np.eye(P, dtype=np.float32), "c_zpick": z_pick,
        "c_iota": np.arange(W, dtype=np.float32), "c_rank": np.arange(NX, 0, -1).astype(np.float32),
    }
    arrays = {k: np.ascontiguousarray(a) for k, a in arrays.items()}
    nc = bacc.Bacc("TRN2", target_bir_lowering=False, num_devices=1)
    io = {k: nc.dram_tensor(f"in_{k}", a.shape, _mybir.dt.from_np(a.dtype), kind="ExternalInput").ap() for k, a in arrays.items()}
    io["out"] = nc.dram_tensor("out_0", (T, D), _mybir.dt.float32, kind="ExternalOutput").ap()
    build(nc, io)
    r = run_bass_kernel_spmd(nc, [{f"in_{k}": a for k, a in arrays.items()}], core_ids=[0])
    return r.results[0]["out_0"].reshape(1, T, D)
```

```python
from contextlib import ExitStack

import concourse.bass as bass
from concourse import mybir

F32 = mybir.dt.float32
BF16 = mybir.dt.bfloat16
I32 = mybir.dt.int32
ALU = mybir.AluOpType
ACT = mybir.ActivationFunctionType
AX = mybir.AxisListType

P = 128
T, D = 2048, 256
S = 1601
H, E = 16, 16
KT = D // P
CT = 512
NC = T // CT
TT = CT // P
HG = 4
NG = H // HG
ST = (S + P - 1) // P
LAST = S - (ST - 1) * P
NX = 8
NE = 2 * TT * NX // 4
W = 256
NS, TOPK = 64, 8
DQ, DH = 64, 128
QUARTERS = 4
SPLIT = (S + QUARTERS - 1) // QUARTERS
QUARTER_START = [min(q * SPLIT, S - SPLIT) for q in range(QUARTERS)]
UNITS = TT * HG * QUARTERS
SLOTS = NG * ST
LEAD = 14
SHIFT = 1
BIG = 1.0e9

PART_GROUPS = ((0, 0, 3), (3, 1, 2), (5, 2, 1))
DELTA_ROW = 96
MAX_ROW = 99
ROWS = 101


START = ([("L", 0), ("C", 0), ("K", 0), ("T", 0), ("Q", 0), ("D", 0)] + [("V", i) for i in range(2)] + [("K", 1)]
         + [("V", i) for i in range(2, 4)] + [("K", 2)] + [("V", i) for i in range(4, 6)] + [("K", 3)]
         + [("V", i) for i in range(6, ST)] + [("L", 1), ("M", 0), ("T", 1), ("L", 2), ("Q", 1), ("T", 2), ("W", 0),
            ("L", 3), ("Q", 2), ("T", 3), ("Q", 3)])
LAST_K = ("K", ST // 4)
BLOCKS = [step for step in START if step[0] in "KQ"]

JOBS = (["y0", "y1", "t1a", "t1b", "router"] + [f"e{i}" for i in range(4)] + ["gateT"] + [f"e{i}" for i in range(4, 8)]
        + ["gb0", "gb1"] + [f"e{i}" for i in range(8, 16)]
        + ["t2a", "t2b", "score0", "score1", "aTa", "aTb", "z0", "z1", "t3a", "t3b", "h", "logits", "slots", "alphaT"])
JOB = {name: i for i, name in enumerate(JOBS)}
USES = len(JOBS) // 2
assert len(JOBS) % 2 == 0


def need(eng, sem, value):
    if not (isinstance(value, int) and value <= 0):
        eng.wait_ge(sem, value)


def units_of(k):
    per = NG * UNITS
    return [divmod(UNITS + LEAD + v, UNITS) for v in range(per * k // SLOTS, per * (k + 1) // SLOTS)]


def max_end(k):
    return next((j for j, u in units_of(k % SLOTS) if u == UNITS - 1), None)


def rows_of(st):
    return LAST if st == ST - 1 else P


def build(nc, io):
    with ExitStack() as ctx:
        def sb(name, shape, dt=F32):
            return ctx.enter_context(nc.sbuf_tensor(name, shape, dt))

        def ps(name, shape, dt=F32):
            return ctx.enter_context(nc.psum_tensor(name, shape, dt))

        def sem(name):
            return ctx.enter_context(nc.semaphore(name))

        q_parts = nc.dram_tensor("q_parts", (3, D, T + CT), BF16, kind="Internal").ap()
        k_parts = nc.dram_tensor("k_parts", (3, D, S), BF16, kind="Internal").ap()
        x3_dram = nc.dram_tensor("x3", (T, D), F32, kind="Internal").ap().rearrange("(a p) d -> p a d", p=P)
        x_dram = io["x"].rearrange("(a p) d -> p a d", p=P)

        xres = sb("xres", [P, TT, D])
        kst_raw = sb("k_stack", [P, H * S // 2 + 8])
        kst = kst_raw[:, 0:H * S // 2].bitcast(BF16).rearrange("p (h s) -> p h s", h=H)
        qst = sb("q_stack", [P, NG, HG, CT], BF16)
        v_sb = sb("v_heads", [P, ST, H, 32])
        probs_raw = sb("probs", [P, 2 * HG * CT])
        probs = probs_raw[:].rearrange("p (b h t) -> p b h t", b=2, h=HG)
        ctxT = probs_raw[:, 0:KT * S].rearrange("p (k s) -> p k s", k=KT)
        expert_w = sb("expert_w", [P, KT, NX * D])
        wqkv = expert_w[:].rearrange("p k n -> p (k n)")[:, 0:3 * KT * D]\
            .rearrange("p (w k n) -> p w k n", w=3, k=KT)
        attc_raw = sb("attn_chunk", [P, NG * CT])
        attc = attc_raw[:, 0:2 * CT].rearrange("p (g t) -> p g t", g=2)
        att_odd = attc_raw[:, 2 * CT:3 * CT]
        o_raw = sb("o_unnormed", [P, CT])
        z_sb = sb("z_sb", [P, CT])
        wo_rows = sb("wo_rows", [P, 2, D])
        alphaT_raw = sb("alphaT", [P, T])
        alphaT = alphaT_raw[0:NS + 1, :]
        xa = sb("xa", [P, TT, D])
        attc_flat = attc_raw[:]
        part_bufs = [raw[:, 0:3 * CT].bitcast(BF16).rearrange("p (m a t) -> p m a t", m=2, a=3)
                     for raw in (alphaT_raw, attc_flat)]
        xb = sb("xb", [P, TT, D])
        xn = sb("xn", [P, TT, D + 1])
        xnT = sb("xnT", [P, KT, CT])
        work = sb("work", [P, TT, W])
        work2 = sb("work2", [P, TT, W])
        hT = sb("hT", [P, CT])
        q32 = work[:].rearrange("p t w -> p (t w)").rearrange("p (m n) -> p m n", m=2)
        rest = work2[:].rearrange("p t w -> p (t w)").rearrange("p (m n) -> p m n", m=2)
        ident = sb("ident", [P, P])
        z_pick = sb("z_pick", [P, 2, HG])
        v_cols = sb("v_cols", [P, 2, 32])
        z_inv = sb("z_inv", [P, TT * HG])
        iota_w = z_sb[:, W:2 * W]
        keep = sb("keep", [P, W])
        gauss = sb("gauss", [P, W])
        neg_mask = sb("neg_mask", [P, W])
        win_f = sb("win_f", [P, 8])
        win_i = sb("win_i", [P, 2], I32)
        enc_win = o_raw[:].rearrange("p (k w) -> p k w", k=KT)
        win_k = sb("win_k", [P, KT, W])
        win_v = sb("win_v", [P, KT, D])
        wa = attc_flat[:, 3 * CT:3 * CT + KT * D].rearrange("p (k n) -> p k n", k=KT)
        wc = sb("wc", [P, 2 * KT, D])
        w1 = sb("w1", [P, 2 * KT, DH])
        w2 = sb("w2", [DH, NS])
        rw = sb("router_w", [P, KT, NX])
        rb = sb("router_b", [P, NX])
        rank = sb("rank", [P, NX])
        eb = sb("expert_b_tiles", [TT * NX, TT, D])
        bo0 = sb("bo0", [P, D])
        bv0 = z_sb[:, 0:D]
        b2 = sb("b2", [P, NS])
        b1 = sb("b1", [P, 1])
        hbias = sb("hbias", [P, 1])
        slotT = sb("slotT", [P, KT, NS])
        slot_mean = sb("slot_mean", [P, KT])
        qk_bias = sb("qk_bias", [P, 2, KT])
        tau = sb("tau", [P, 4])
        rtau = sb("rtau", [P, 2])
        q_flat = qst[:].rearrange("p g h t -> p (g h t)")
        delta3 = q_flat[0:H, 0:3 * S].rearrange("p (a s) -> p a s", a=3)
        delta_a = q_flat[0:H, 3 * S + 1:5 * S + 1].bitcast(F32)
        delta_b = expert_w[:].rearrange("p k n -> p (k n)")[0:H, 3 * KT * D:3 * KT * D + S]
        aT = work2[:].rearrange("p (k a) w -> p k (a w)", k=KT)
        ones_sb = xres[:].rearrange("p t d -> p (t d)")[0:H, :].bitcast(BF16)
        mx = sb("mx", [P, QUARTERS, HG * TT])
        mxc = sb("mxc", [P, HG * TT])
        mrow = sb("mrow", [HG * TT, 2, P], BF16)
        bst = sb("bst", [P, TT, 6])
        mv = sb("mv", [P, TT, 2])
        var_e = sb("var_e", [P, TT])
        rstd = sb("rstd", [P, TT])
        neg_half = sb("neg_half", [P, TT])
        eps = sb("eps", [P, TT])
        lg8 = sb("lg8", [P, TT, NX])
        ex8 = sb("ex8", [P, TT, NX])
        hot8 = sb("hot8", [P, TT, NX])
        st4 = sb("st4", [P, 8, TT])
        gateT = sb("gateT", [TT * NX, P])
        rowsum = sb("rowsum", [P, TT])
        tail = sb("tail", [P, TT])
        neg_big = sb("neg_big", [P, 1])
        lg, lgr, elg, alpha = (work[:].rearrange("p t w -> p (t w)")[:, TT * NS * i:TT * NS * (i + 1)]
                               .rearrange("p (t n) -> p t n", t=TT) for i in range(4))
        top8 = sb("top8", [P, TT, TOPK])
        slot_acc = sb("slot_acc", [NS, D + 1])

        at = [0]

        def late(n_rows, *shape):
            n = 1
            for x in shape:
                n *= x
            a = kst_raw[0:n_rows, at[0]:at[0] + n]
            at[0] += n
            assert at[0] <= H * S // 2
            if len(shape) == 2:
                a = a.rearrange("p (a b) -> p a b", a=shape[0])
            return a

        wihT, whhT = late(P, KT, 3 * D), late(P, KT, 3 * D)
        wqs, wks = late(P, KT, DQ), late(P, KT, DQ)
        wvs, wvps, wos = late(P, KT, D), late(P, KT, D), late(P, KT, D)
        b_ih, b_hh = late(NS, 3 * D), late(NS, 3 * D)
        b_v, ln_g, ln_b, b_vp, slot0 = (late(NS, D) for _ in range(5))
        b_qk = late(DQ, 2)
        rz, gate_n, hid_n, s_new, comm, y_ln = late(NS, 2 * D), late(NS, D), late(NS, D), late(NS, D), late(NS, D), late(NS, D)
        vec = late(NS, D)
        sT = late(P, KT, NS)
        qkT = late(DQ, 2, NS)
        att_s = late(NS, NS)
        att_sT = late(NS, NS)
        svo = late(NS + 1, D)
        small = late(NS, 16)
        x_end = probs_raw[:].rearrange("p (a d) -> p a d", d=D)

        ps_e = [ps(f"ps_e{i}", [P, CT]) for i in range(2)]
        ps_m = ps("ps_m", [P, 4, CT])
        ps_o = ps("ps_o", [P, CT])
        ps_x = ps("ps_x", [P, CT])

        names = """ld_const ld_early ld_cond ld_encwin ld_expert ld_delta ld_delta_k ld_ones ld_fill ld_k ld_slot
            x_loaded x3_stored x_end_loaded
            fills_set consts_set v_ones_set q0_copied delta_hi delta_parts window_start masks_ready
            blk_psum blk_hi blk_parts v_psum v_taken
            var_ready rstd_ready xn_ready xnT_psum xnT_ready
            win_psum win_copied hb_psum hb_ready mean_ready
            max_ready max_taken mx_ready mT_ready mrow_ready
            qk_ready exp_done pv_done o_taken z_cols z_inverted z_repeated z_ready att_ready
            xres_ready lg8_ready ex8_ready gate_ready negmax_ready rowsum_ready a_ready x3_ready
            lg_ready elg_ready alpha_ready
            p_si p_siT_ps p_siT p_gi p_rz p_sig p_npre p_n p_snew p_snT_ps p_snT p_qkv p_qkT p_lg
            p_nmax p_exp p_attn p_attT_ps p_attT p_comm p_var p_rstd p_y p_yT_ps p_yT p_sv p_svb p_svT_ps p_svT
            p_svo p_svo_sb out_psum out_ready out_stored""".split()
        s = {n: sem(n) for n in names}
        ctx_loaded = [sem(f"ctx_loaded{i}") for i in range(ST // 3)]
        w_loaded = [sem(f"w_loaded{i}") for i in range(3)]
        parts_stored = [[sem(f"parts_stored{b}_{m}") for m in range(KT)] for b in range(2)]
        q_loaded = [sem(f"q_loaded{g}") for g in range(NG)]
        m_loaded = [sem(f"m_loaded{g}") for g in range(NG)]
        x_start = [sem(f"x_start{i}") for i in range(2)]
        bank_filled = [sem(f"bank_filled{b}") for b in range(2)]
        bank_taken = [sem(f"bank_taken{b}") for b in range(2)]

        def bank(job):
            return ps_m[:, 2 + JOB[job] % 2, :]

        def bank_free(eng, job, c):
            need(eng, bank_taken[JOB[job] % 2], USES * c + JOB[job] // 2)

        def filled(mm, job):
            mm.then_inc(bank_filled[JOB[job] % 2], 1)

        def wait_filled(eng, job, c):
            eng.wait_ge(bank_filled[JOB[job] % 2], USES * c + JOB[job] // 2 + 1)

        def taken(ins, job):
            ins.then_inc(bank_taken[JOB[job] % 2], 1)

        def wait_taken(eng, job, c):
            eng.wait_ge(bank_taken[JOB[job] % 2], USES * c + JOB[job] // 2 + 1)
        block = ctx.enter_context(nc.Block())

        const_loads = [
            (z_pick[:], io["c_zpick"]),
            (iota_w[:], io["c_iota"].partition_broadcast(P)), (rank[:], io["c_rank"].partition_broadcast(P)),
            (wc[:], io["L1_W_cT"].rearrange("(k p) n -> p k n", p=P)),
            (w1[:], io["w1"].rearrange("(k p) n -> p k n", p=P)),
            (w2[:], io["w2"]),
            (rw[:], io["router_wT"].rearrange("(k p) n -> p k n", p=P)),
            (rb[:], io["router_b"].partition_broadcast(P)),
            (bo0[:], io["L0_bo"].partition_broadcast(P)), 
            (b2[:], io["b2"].partition_broadcast(P)),
            (b1[:], io["b1"].rearrange("(p a) -> p a", a=1)),
            (slotT[:], io["slot_initT"].rearrange("(k p) n -> p k n", p=P)),
            (wa, io["L1_W_aT"].rearrange("(k p) n -> p k n", p=P)),
        ]
        wo_loads = [(wo_rows[32 * j + E * odd:32 * j + E * odd + E, :, :],
                     io["L0_WoT"].rearrange("(g o j e) n -> o j e g n", g=2, o=2, j=HG)[odd, j])
                    for j in range(HG) for odd in range(2)]
        eb_loads = [(eb[NX * t:NX * t + NX, t, :], io["expert_b"]) for t in range(TT)]
        slot_loads = [
            (wihT, io["WihT"].rearrange("(k p) n -> p k n", p=P)), (whhT, io["WhhT"].rearrange("(k p) n -> p k n", p=P)),
            (wqs, io["wq"].rearrange("(k p) n -> p k n", p=P)), (wks, io["wk"].rearrange("(k p) n -> p k n", p=P)),
            (wvs, io["wv"].rearrange("(k p) n -> p k n", p=P)), (wvps, io["wvp"].rearrange("(k p) n -> p k n", p=P)),
            (wos, io["wo"].rearrange("(k p) n -> p k n", p=P)),
            (b_ih, io["bih"].partition_broadcast(NS)), (b_hh, io["bhh"].partition_broadcast(NS)),
            (b_v, io["bv"].partition_broadcast(NS)), (ln_g, io["ln_g"].partition_broadcast(NS)),
            (ln_b, io["ln_b"].partition_broadcast(NS)), (b_vp, io["bvp"].partition_broadcast(NS)),
            (slot0, io["slot_init"]), (svo[NS:NS + 1, :], io["L1_bo"].unsqueeze(0)), (b_qk[:, 0:1], io["bq"].rearrange("(p a) -> p a", a=1)),
            (b_qk[:, 1:2], io["bk"].rearrange("(p a) -> p a", a=1)),
        ]
        N_CONST = 16 * len(const_loads)
        N_FILL = 16 * (len(wo_loads) + len(eb_loads))
        k_cols = [(i * CT, min(CT, S - i * CT)) for i in range((S + CT - 1) // CT)]
        N_BLOCKS = len(BLOCKS)

        def block_cols(kind, i):
            return k_cols[i][1] if kind == "K" else CT

        def wait_stored(eng, b, m):
            eng.wait_ge(parts_stored[b % 2][m], 16 * (b // 2 + 1))

        def load_q(eng, g, chunk):
            for j, part, n in PART_GROUPS:
                for i in range(n):
                    src = q_parts[part, HG * E * g:HG * E * (g + 1), bass.ds(chunk * CT, CT)]
                    eng.dma_start(qst[16 * (j + i):16 * (j + i) + 16, g, :, :], src.rearrange("(h e) t -> e h t", h=HG))\
                       .then_inc(q_loaded[g], 16)

        @block.sync
        def _(sp):
            def load_w(i, name):
                sp.dma_start(wqkv[:, i], io[name].rearrange("(k p) n -> p k n", p=P)).then_inc(w_loaded[i], 16)

            def load_ctx(i):
                at_col, n = k_cols[i]
                sp.dma_start(ctxT[:, :, at_col:at_col + n],
                             io["ctxT"].rearrange("(k p) s -> p k s", p=P)[:, :, at_col:at_col + n])\
                  .then_inc(ctx_loaded[i], 16)

            sp.dma_start(xa[:], x_dram[:, 0:TT, :]).then_inc(x_start[0], 16)
            load_w(0, "L0_WkT")
            load_ctx(0)
            load_w(2, "L0_WqT")
            load_ctx(1)
            load_w(1, "L0_WvT")
            sp.dma_start(xb[:], x_dram[:, TT:2 * TT, :]).then_inc(x_start[1], 16)
            load_ctx(2)
            load_ctx(3)
            for dst, src in const_loads:
                sp.dma_start(dst, src).then_inc(s["ld_const"], 16)
            sp.wait_ge(s["consts_set"], 1)
            for r in (MAX_ROW, MAX_ROW + 1):
                sp.dma_start(kst[r:r + 1, :, :], ones_sb[0:H, 0:S]).then_inc(s["ld_k"], 16)
            for g in range(NG):
                sp.dma_start(qst[DELTA_ROW:DELTA_ROW + 3, g, :, :], ones_sb[0:3, :]).then_inc(s["ld_ones"], 16)

            def store(b, kind, i):
                at_col, n = k_cols[i] if kind == "K" else (CT * i, CT)
                dst = k_parts if kind == "K" else q_parts
                for m in range(KT):
                    sp.wait_ge(s["blk_parts"], KT * b + m + 1)
                    sp.dma_start(dst[:, P * m:P * m + P, at_col:at_col + n].rearrange("a p n -> p a n"),
                                 part_bufs[b % 2][:, m, :, 0:n]).then_inc(parts_stored[b % 2][m], 16)

            def gather_k(b, i):
                at_col, n = k_cols[i]
                for m in range(KT):
                    wait_stored(sp, b, m)
                for j, _, copies in PART_GROUPS:
                    for a in range(copies):
                        sp.dma_start(kst[16 * (j + a):16 * (j + a) + 16, :, at_col:at_col + n],
                                     k_parts[a, :, at_col:at_col + n].rearrange("(h e) s -> e h s", h=H))\
                          .then_inc(s["ld_k"], 16)

            for b, (kind, i) in enumerate(BLOCKS):
                store(b, kind, i)
                if b and BLOCKS[b - 1][0] == "K" and BLOCKS[b - 1] != LAST_K:
                    gather_k(b - 1, BLOCKS[b - 1][1])
                if BLOCKS[b] == LAST_K:
                    sp.wait_ge(s["delta_parts"], 1)
                    for a in range(3):
                        sp.dma_start(kst[DELTA_ROW + a:DELTA_ROW + a + 1, :, :], delta3[:, a, :]).then_inc(s["ld_delta_k"], 16)
                    gather_k(b, i)
                    sp.wait_ge(s["ld_delta_k"], 48)
                    for g in range(3):
                        load_q(sp, g, 0)
                    sp.dma_start(q_parts[:, :, T:T + CT], q_parts[:, :, 0:CT]).then_inc(s["q0_copied"], 16)
            sp.wait_ge(s["fills_set"], 1)
            for dst, src in wo_loads + eb_loads:
                sp.dma_start(dst, src).then_inc(s["ld_fill"], 16)
            for b in (N_BLOCKS - 2, N_BLOCKS - 1):
                for m in range(KT):
                    wait_stored(sp, b, m)
            sp.wait_ge(s["q0_copied"], 16)
            sp.wait_ge(s["blk_psum"], KT * N_BLOCKS)
            for k in range(KT):
                sp.dma_start(expert_w[:, k, :], io["expert_wT"][k]).then_inc(s["ld_expert"], 16)
            sp.wait_ge(s["mrow_ready"], 1)

            def load_m(g):
                for a in range(2):
                    sp.dma_start(qst[MAX_ROW + a:MAX_ROW + a + 1, g, :, :], mrow[:, a, :]).then_inc(m_loaded[g], 16)

            def store_x3(c):
                sp.wait_ge(s["x3_ready"], c + 1)
                sp.dma_start(x3_dram[:, bass.ds(c * TT, TT), :], xres[:]).then_inc(s["x3_stored"], 16)

            def chunk_loads(c, behind):
                for g in range(NG):
                    sp.wait_ge(s["mrow_ready"], NG * c + g + 2)
                    load_m((g + 1) % NG)
                    load_q(sp, (g + 3) % NG, c if g == 0 else c + 1)
                    if g == NG - 1:
                        if behind:
                            store_x3(c - 1)
                            sp.wait_ge(s["x3_stored"], 16 * c)
                        sp.dma_start(xres[:], x_dram[:, bass.ds(c * TT, TT), :]).then_inc(s["x_loaded"], 16)

            load_m(0)
            chunk_loads(0, False)
            with sp.Fori(1, NC) as c:
                chunk_loads(c, True)
            store_x3(NC - 1)
            for dst, src in slot_loads:
                sp.dma_start(dst, src).then_inc(s["ld_slot"], 16)
            sp.wait_ge(s["x3_stored"], 16 * NC)
            sp.dma_start(x_end, x3_dram).then_inc(s["x_end_loaded"], 16)
            out = io["out"].rearrange("(a p) d -> p a d", p=P)
            for c in range(NC):
                sp.wait_ge(s["out_ready"], c + 1)
                sp.dma_start(out[:, TT * c:TT * c + TT, :], x_end[:, TT * c:TT * c + TT, :]).then_inc(s["out_stored"], 16)
            for g in range(NG):
                sp.wait_ge(q_loaded[g], 96 * (NC + (g < 3)))
            sp.wait_ge(m_loaded[0], 32 * (NC + 1))
            sp.wait_ge(s["out_stored"], 16 * NC)

        LN_SLOTS = (7, 28, 37)

        @block.gpsimd
        def _(pool):
            pool.memset(neg_half[:], -0.5)
            pool.memset(eps[:], 1e-5)
            for odd in range(2):
                pool.memset(v_cols[:, odd, 0:E], 1.0 - odd)
                pool.memset(v_cols[:, odd, E:32], 1.0 * odd)
            pool.memset(neg_big[:], -BIG)
            pool.memset(xn[:, :, D:D + 1], 1.0)
            pool.memset(slot_acc[:], 0.0)
            v_even_odd = v_sb[:].rearrange("p a (g o j) e -> p o (a g) j e", g=2, o=2)
            pool.memset(v_even_odd[:, 0, :, :, E:32], 1.0)
            pool.memset(v_even_odd[:, 1, :, :, 0:E], 1.0).then_inc(s["v_ones_set"], 1)

            def rsqrt(n):
                pool.wait_ge(s["var_ready"], n)
                pool.tensor_tensor(var_e[:], mv[:, :, 1], eps[:], ALU.add)
                pool.drain()
                pool.tensor_tensor(rstd[:], var_e[:], neg_half[:], ALU.pow).then_inc(s["rstd_ready"], 1)

            pool.drain()
            rsqrt(1)
            pool.memset(ones_sb, 1.0).then_inc(s["consts_set"], 1)
            pool.wait_ge(s["delta_hi"], 1)
            pool.tensor_tensor(delta_b, delta_a, delta3[:, 0, :], ALU.subtract)
            pool.wait_ge(s["window_start"], 1)
            w0 = pool.value_load(win_i[0:1, 1:2], min_val=0, max_val=S - W)
            pool.dma_start(enc_win[:], io["ctxT"].rearrange("(k p) s -> p k s", p=P)[:, :, bass.ds(w0, W)])\
                .then_inc(s["ld_encwin"], 16)
            pool.drain()
            pool.tensor_copy(delta3[:, 1, :], delta_b)
            pool.drain()
            pool.tensor_tensor(delta3[:, 2, :], delta_b, delta3[:, 1, :], ALU.subtract).then_inc(s["delta_parts"], 1)
            rsqrt(2)
            pool.memset(eb[:], 0.0).then_inc(s["fills_set"], 1)
            rsqrt(3)
            rsqrt(4)
            pool.wait_ge(s["ld_const"], N_CONST)

            def repeat_z(c, g):
                pool.wait_ge(s["z_inverted"], NG * c + g + 1)
                z_wide = z_inv[:].unsqueeze(2).broadcast_to((P, TT * HG, 32))
                pool.tensor_tensor(z_sb[:].rearrange("p (a e) -> p a e", e=32), z_wide,
                                   v_cols[:, g % 2, :].unsqueeze(1).broadcast_to((P, TT * HG, 32)), ALU.mult)\
                    .then_inc(s["z_repeated"], 1)

            def behind(c, k):
                if k == 4:
                    pool.wait_ge(s["x_loaded"], 16 * (c + 1))
                    pool.tensor_tensor(xres[:], xres[:], bo0[:].unsqueeze(1).broadcast_to((P, TT, D)), ALU.add)\
                        .then_inc(s["xres_ready"], 1)
                if k in LN_SLOTS:
                    rsqrt(NC + 3 * c + LN_SLOTS.index(k) + 1)

            def chunk(c, first):
                for k in range(SLOTS):
                    g, st = k // ST, k % ST
                    if st == 3 and (g or not first):
                        repeat_z(c, g - 1)
                    if not first:
                        behind(c - 1, k - SHIFT)

            chunk(0, True)
            with pool.Fori(1, NC) as c:
                chunk(c, False)
            repeat_z(NC, -1)
            for k in range(SLOTS):
                behind(NC - 1, k)
            pool.wait_ge(s["p_var"], 1)
            pool.tensor_scalar(small[:, 9:10], small[:, 8:9], 1e-5, None, ALU.add)
            pool.drain()
            pool.tensor_tensor(small[:, 10:11], small[:, 9:10], neg_half[0:NS, 0:1], ALU.pow).then_inc(s["p_rstd"], 1)

        @block.scalar
        def _(act):
            for dst, src in ((ident[:], io["c_ident"]), (bv0[:], io["L0_bv"].partition_broadcast(P))):
                act.dma_start(dst, src).then_inc(s["ld_early"], 16)
            act.dma_start(tau[:, 0:1], io["condB_tau"].partition_broadcast(P)).then_inc(s["ld_cond"], 16)
            act.dma_start(win_f[:, 0:1], io["condB_pt"].partition_broadcast(P)).then_inc(s["ld_cond"], 16)
            act.dma_start(win_i[:, 0:1], io["lenS2"].partition_broadcast(P)).then_inc(s["ld_cond"], 16)
            act.dma_start(rtau[:, 0:1], io["L1_tau"].partition_broadcast(P)).then_inc(s["ld_cond"], 16)
            for i, name in enumerate(("L0_bq", "L0_bk")):
                act.dma_start(qk_bias[:, i, :], io[name].rearrange("(k p) -> p k", p=P),
                              allow_slow_non_contiguous=True).then_inc(s["ld_cond"], 16)
            act.dma_start(delta_a, io["fside"].partition_broadcast(H)).then_inc(s["ld_delta"], 16)

            def block_hi(b, kind, i):
                n = block_cols(kind, i)
                bias, scale = (qk_bias[:, 1, :], 1.0) if kind == "K" else (qk_bias[:, 0, :], tau[:, 2:3])
                for m in range(KT):
                    act.wait_ge(s["blk_psum"], KT * b + m + 1)
                    if b:
                        act.wait_ge(s["blk_parts"], KT * (b - 1) + m + 1)
                    act.activation(q32[:, m, 0:n], ps_e[m][:, 0:n], ACT.Identity, bias=bias[:, m:m + 1], scale=scale)
                    if b >= 2:
                        wait_stored(act, b - 2, m)
                    act.activation(part_bufs[b % 2][:, m, 0, 0:n], ps_e[m][:, 0:n], ACT.Identity,
                                   bias=bias[:, m:m + 1], scale=scale).then_inc(s["blk_hi"], 1)

            act.wait_ge(s["masks_ready"], 1)
            for kind, i in START:
                if kind in "KQ":
                    block_hi(BLOCKS.index((kind, i)), kind, i)
                if kind == "T":
                    act.wait_ge(s["xnT_psum"], i + 1)
                    act.copy(xnT[:], ps_m[:, 2:4, :]).then_inc(s["xnT_ready"], 1)
                if kind == "T" and i + 2 < NC:
                    act.dma_start((xa, xb)[i % 2][:], x_dram[:, TT * (i + 2):TT * (i + 3), :]).then_inc(x_start[i % 2], 16)
                if kind == "D":
                    act.wait_ge(s["ld_delta"], 16)
                    act.activation(delta3[:, 0, :], delta_a, ACT.Identity, scale=E ** -0.5)
                    act.drain()
                    act.activation(delta_a, delta_a, ACT.Identity, scale=E ** -0.5).then_inc(s["delta_hi"], 1)
                if kind == "M":
                    act.wait_ge(s["masks_ready"], 2)
                    act.activation(gauss[:], iota_w[:], ACT.Exp, scale=-1.0 / 128.0)
                if kind == "W":
                    act.wait_ge(s["win_psum"], 1)
                    act.copy(win_k[:], ps_x[:].rearrange("p (k w) -> p k w", k=KT))
                    act.copy(win_v[:], ps_o[:].rearrange("p (k w) -> p k w", k=KT)).then_inc(s["win_copied"], 1)

            def exps(c, k):
                n = rows_of(k % ST)
                need(act, s["pv_done"], SLOTS * c + k - 1)
                for h in range(HG):
                    act.wait_ge(s["qk_ready"], SLOTS * HG * c + HG * k + h + 1)
                    act.activation(probs[0:n, k % 2, h, :], ps_e[h % 2][0:n, :], ACT.Exp).then_inc(s["exp_done"], 1)

            def take_o(c, g):
                act.wait_ge(s["pv_done"], SLOTS * c + ST * (g + 1))
                need(act, s["att_ready"], NG * c + g)
                act.copy(o_raw[:], ps_o[:]).then_inc(s["o_taken"], 1)

            def take_xnT(names, c):
                for k, name in enumerate(names):
                    wait_filled(act, name, c)
                    taken(act.copy(xnT[:, k, :], bank(name)), name)

            def behind(c, k):
                if k == 9:
                    take_xnT(("t1a", "t1b"), c)
                if k == 11:
                    act.wait_ge(s["lg8_ready"], c + 1)
                    act.activation(ex8[:], lg8[:], ACT.Exp).then_inc(s["ex8_ready"], 1)
                if k == 15:
                    wait_filled(act, "gateT", c)
                    taken(act.copy(gateT[:], bank("gateT")[0:TT * NX, 0:P]), "gateT")
                if k == 30:
                    take_xnT(("t2a", "t2b"), c)
                if k == 32:
                    act.wait_ge(s["negmax_ready"], c + 1)
                    act.activation(tail[:], st4[:, 0, :], ACT.Exp, bias=neg_big[:, 0:1])
                    for t in range(TT):
                        last = act.activation(work2[:, t, :], work[:, t, :], ACT.Exp, bias=st4[:, 0, t:t + 1],
                                              accum_out=rowsum[:, t:t + 1])
                    last.then_inc(s["rowsum_ready"], 1)
                if k == 34:
                    for kk, name in enumerate(("aTa", "aTb")):
                        wait_filled(act, name, c)
                        taken(act.copy(aT[:, kk, :], bank(name)), name)
                if k in (35, 36):
                    name = f"z{k - 35}"
                    wait_filled(act, name, c)
                    taken(act.activation(work[:, 2 * (k - 35):2 * (k - 35) + 2, :].rearrange("p a w -> p (a w)"),
                                         bank(name), ACT.Tanh), name)
                if k == 39:
                    take_xnT(("t3a", "t3b"), c)
                if k == 40:
                    wait_filled(act, "h", c)
                    taken(act.activation(hT[:], bank("h"), ACT.Gelu, bias=hbias[:, 0:1]), "h")
                if k == 42:
                    act.wait_ge(s["lg_ready"], c + 1)
                    for t in range(TT):
                        last = act.activation(elg[:, t, :], lg[:, t, :], ACT.Exp, bias=st4[:, 1, t:t + 1])
                    last.then_inc(s["elg_ready"], 1)
                if k == 44:
                    wait_filled(act, "alphaT", c)
                    taken(act.copy(alphaT[0:NS, bass.ds(c * CT, CT)], bank("alphaT")[0:NS, :]), "alphaT")

            def chunk(c, first):
                for k in range(SLOTS):
                    g, st = k // ST, k % ST
                    if st == 1 and (g or not first):
                        take_o(c, g - 1)
                    exps(c, k)
                    if not first:
                        behind(c - 1, k - SHIFT)

            chunk(0, True)
            with act.Fori(1, NC) as c:
                chunk(c, False)
            take_o(NC, -1)
            for k in range(SLOTS):
                behind(NC - 1, k)
            act.wait_ge(s["p_rz"], 1)
            act.activation(rz, rz, ACT.Sigmoid).then_inc(s["p_sig"], 1)
            act.wait_ge(s["p_npre"], 1)
            act.activation(gate_n, gate_n, ACT.Tanh).then_inc(s["p_n"], 1)
            act.wait_ge(s["p_nmax"], 1)
            act.activation(att_s, ps_x[0:NS, 0:NS], ACT.Exp, bias=small[:, 2:3], scale=DQ ** -0.5,
                           accum_out=small[:, 3:4]).then_inc(s["p_exp"], 1)

        @block.tensor
        def _(pe):
            def project(b, kind, i):
                at_col, n = k_cols[i] if kind == "K" else (0, CT)
                src, w = (ctxT, 0) if kind == "K" else (xnT, 2)
                if i == 0:
                    pe.wait_ge(w_loaded[w], 16)
                if kind == "K":
                    pe.wait_ge(ctx_loaded[i], 16)
                else:
                    pe.wait_ge(s["xnT_ready"], i + 1)
                for m in range(KT):
                    if b:
                        pe.wait_ge(s["blk_hi"], KT * (b - 1) + m + 1)
                    for k in range(KT):
                        mm = pe.matmul(ps_e[m][:, 0:n], wqkv[:, w, k, P * m:P * m + P], src[:, k, at_col:at_col + n],
                                       start=(k == 0), stop=(k == KT - 1))
                    mm.then_inc(s["blk_psum"], 1)

            def max_unit(u, c, j, banks=2):
                g, n1 = j % NG, NG * c + j
                t, h, q = u // (QUARTERS * HG), (u // QUARTERS) % HG, u % QUARTERS
                if u == 0:
                    pe.wait_ge(q_loaded[j % NG], 96 * (c + j // NG + 1))
                need(pe, s["max_taken"], UNITS * n1 + u + 1 - banks)
                pe.matmul(ps_m[:, u % 2 if banks == 2 else (UNITS * n1 + u) % banks, 0:SPLIT], qst[0:MAX_ROW, g, h, P * t:P * t + P],
                          kst[0:MAX_ROW, HG * g + h, QUARTER_START[q]:QUARTER_START[q] + SPLIT],
                          start=True, stop=True).then_inc(s["max_ready"], 1)

            def max_rows(n1):
                need(pe, s["att_ready"], n1 - 1)
                pe.wait_ge(s["mx_ready"], n1 + 1)
                pe.transpose(ps_x[0:HG * TT, 0:P], mxc[:], ident[:]).then_inc(s["mT_ready"], 1)

            pe.wait_ge(s["ld_early"], 32)
            for kind, i in START:
                if kind in "KQ":
                    project(BLOCKS.index((kind, i)), kind, i)
                if kind == "T":
                    pe.wait_ge(s["xn_ready"], i + 1)
                    for k in range(KT):
                        for t in range(TT):
                            mm = pe.transpose(ps_m[:, 2 + k, P * t:P * t + P], xn[:, t, P * k:P * k + P], ident[:])
                    mm.then_inc(s["xnT_psum"], 1)
                if kind == "V":
                    n = rows_of(i)
                    if i == 0:
                        pe.wait_ge(w_loaded[1], 16)
                    if i >= 2:
                        pe.wait_ge(s["v_taken"], i - 1)
                    for k in range(KT):
                        mm = pe.matmul(ps_m[0:n, i % 2, 0:D], ctxT[:, k, P * i:P * i + n], wqkv[:, 1, k, :],
                                       start=(k == 0), stop=(k == KT - 1))
                    mm.then_inc(s["v_psum"], 1)
                if kind == "M":
                    pe.wait_ge(s["ld_const"], N_CONST)
                    pe.wait_ge(s["mean_ready"], 1)
                    for k in range(KT):
                        mm = pe.matmul(ps_x[:, 0:1], w1[:, KT + k, :], slot_mean[:, k:k + 1],
                                       start=(k == 0), stop=(k == KT - 1))
                    mm.then_inc(s["hb_psum"], 1)
                if kind == "W":
                    pe.wait_ge(s["ld_encwin"], 16)
                    pe.wait_ge(s["hb_ready"], 1)
                    for m in range(KT):
                        for k in range(KT):
                            pe.matmul(ps_x[:, W * m:W * m + W], wa[:, k, P * m:P * m + P], enc_win[:, k, :],
                                      start=(k == 0), stop=(k == KT - 1))
                    for m in range(KT):
                        for k in range(KT):
                            mm = pe.matmul(ps_o[:, D * m:D * m + D], enc_win[:, k, P * m:P * m + P], wc[:, k, :],
                                           start=(k == 0), stop=(k == KT - 1))
                    mm.then_inc(s["win_psum"], 1)
            pe.wait_ge(s["ld_k"], 16 * (2 + 6 * len(k_cols)))
            pe.wait_ge(s["ld_delta_k"], 48)
            pe.wait_ge(s["ld_ones"], 16 * NG)
            pe.wait_ge(s["v_taken"], ST)
            for v in range(UNITS + LEAD):
                if v == UNITS + 3:
                    pe.wait_ge(s["win_copied"], 1)
                    max_rows(0)
                max_unit(v % UNITS, 0, v // UNITS, banks=4)
            pe.wait_ge(s["blk_hi"], KT * N_BLOCKS)
            pe.wait_ge(s["ld_fill"], N_FILL)
            pe.wait_ge(s["ld_expert"], 32)

            def pv(c, k, half):
                cols = slice(CT // 2 * half, CT // 2 * (half + 1))
                g, st = k // ST % NG, k % ST
                n = rows_of(st)
                if half == 0:
                    if st == 0:
                        need(pe, s["o_taken"], NG * c + g)
                    pe.wait_ge(s["exp_done"], HG * (SLOTS * c + k + 1))
                for h in range(HG):
                    mm = pe.matmul(ps_o[32 * h:32 * h + 32, cols], v_sb[0:n, st, HG * g + h, :],
                                   probs[0:n, k % 2, h, cols], start=(st == 0 and half == 0),
                                   stop=(st == ST - 1 and half == 1))
                if half == 1:
                    mm.then_inc(s["pv_done"], 1)

            def z_columns(c, g):
                pe.wait_ge(s["o_taken"], NG * c + g + 1)
                pe.wait_ge(s["mrow_ready"], NG * c + g + 2)
                for t in range(TT):
                    mm = pe.matmul(ps_x[:, HG * t:HG * t + HG], o_raw[:, P * t:P * t + P], z_pick[:, g % 2, :],
                                   start=True, stop=True)
                mm.then_inc(s["z_cols"], 1)

            def spread_z(c, g):
                pe.wait_ge(s["z_repeated"], NG * c + g + 1)
                for t in range(TT):
                    mm = pe.matmul(ps_x[:, P * t:P * t + P], z_sb[:, P * t:P * t + P], ident[:], start=True, stop=True)
                mm.then_inc(s["z_ready"], 1)

            def to_xnT(names, n, c):
                pe.wait_ge(s["xn_ready"], n)
                for k, name in enumerate(names):
                    bank_free(pe, name, c)
                    for t in range(TT):
                        mm = pe.transpose(bank(name)[:, P * t:P * t + P], xn[:, t, P * k:P * k + P], ident[:])
                    filled(mm, name)

            def xnT_there(names, c):
                for name in names:
                    wait_taken(pe, name, c)

            def experts(i, c):
                name, t, j = f"e{i}", i // 4, i % 4
                bank_free(pe, name, c)
                for k in range(KT):
                    mm = pe.matmul(bank(name), xnT[:, k, P * t:P * t + P], expert_w[:, k, CT * j:CT * j + CT],
                                   start=(k == 0), stop=(k == KT - 1))
                filled(mm, name)

            def behind(c, k):
                if k in (5, 6):
                    name = f"y{k - 5}"
                    pe.wait_ge(s["att_ready"], NG * (c + 1))
                    bank_free(pe, name, c)
                    for t in range(2):
                        tok = P * (2 * (k - 5) + t)
                        for g in range(2):
                            mm = pe.matmul(bank(name)[:, D * t:D * t + D], attc[:, g, tok:tok + P], wo_rows[:, g, :],
                                           start=(g == 0), stop=(g == 1))
                    filled(mm, name)
                if k == 9:
                    to_xnT(("t1a", "t1b"), NC + 3 * c + 1, c)
                if k == 10:
                    xnT_there(("t1a", "t1b"), c)
                    bank_free(pe, "router", c)
                    for t in range(TT):
                        for kk in range(KT):
                            mm = pe.matmul(bank("router")[:, NX * t:NX * t + NX], xnT[:, kk, P * t:P * t + P],
                                           rw[:, kk, :], start=(kk == 0), stop=(kk == KT - 1))
                    filled(mm, "router")
                if k == 15:
                    pe.wait_ge(s["gate_ready"], c + 1)
                    bank_free(pe, "gateT", c)
                    filled(pe.transpose(bank("gateT")[0:TT * NX, 0:P], hot8[:].rearrange("p t e -> p (t e)"), ident[:]),
                           "gateT")
                if 11 <= k < 19:
                    experts(k - 11, c)
                if k == 19:
                    wait_taken(pe, "gateT", c)
                    for i in range(2):
                        bank_free(pe, f"gb{i}", c)
                        for t in range(2):
                            mm = pe.matmul(bank(f"gb{i}")[:, D * t:D * t + D], gateT[:], eb[:, 2 * i + t, :],
                                           start=True, stop=True)
                        filled(mm, f"gb{i}")
                if 20 <= k < 28:
                    experts(k - 12, c)
                if k == 30:
                    to_xnT(("t2a", "t2b"), NC + 3 * c + 2, c)
                if k == 31:
                    xnT_there(("t2a", "t2b"), c)
                    for i in range(2):
                        name = f"score{i}"
                        bank_free(pe, name, c)
                        for t in range(2):
                            for kk in range(KT):
                                tok = P * (2 * i + t)
                                mm = pe.matmul(bank(name)[:, W * t:W * t + W], xnT[:, kk, tok:tok + P], win_k[:, kk, :],
                                               start=(kk == 0), stop=(kk == KT - 1))
                        filled(mm, name)
                if k == 34:
                    pe.wait_ge(s["a_ready"], c + 1)
                    for kk, name in enumerate(("aTa", "aTb")):
                        bank_free(pe, name, c)
                        for t in range(TT):
                            mm = pe.transpose(bank(name)[:, P * t:P * t + P], work[:, t, P * kk:P * kk + P], ident[:])
                        filled(mm, name)
                if k in (35, 36):
                    xnT_there(("aTa", "aTb"), c)
                    name = f"z{k - 35}"
                    bank_free(pe, name, c)
                    for t in range(2):
                        tok = P * (2 * (k - 35) + t)
                        o = bank(name)[:, D * t:D * t + D]
                        for kk in range(KT):
                            pe.matmul(o, aT[:, kk, tok:tok + P], win_v[:, kk, :], start=(kk == 0), stop=False)
                        for kk in range(KT):
                            mm = pe.matmul(o, xnT[:, kk, tok:tok + P], wc[:, KT + kk, :], start=False, stop=(kk == KT - 1))
                    filled(mm, name)
                if k == 39:
                    to_xnT(("t3a", "t3b"), NC + 3 * c + 3, c)
                if k == 40:
                    xnT_there(("t3a", "t3b"), c)
                    bank_free(pe, "h", c)
                    for kk in range(KT):
                        mm = pe.matmul(bank("h"), w1[:, kk, :], xnT[:, kk, :], start=(kk == 0), stop=(kk == KT - 1))
                    filled(mm, "h")
                if k == 41:
                    wait_taken(pe, "h", c)
                    bank_free(pe, "logits", c)
                    for t in range(TT):
                        mm = pe.matmul(bank("logits")[:, NS * t:NS * t + NS], hT[:, P * t:P * t + P], w2[:],
                                       start=True, stop=True)
                    filled(mm, "logits")
                if k == 44:
                    pe.wait_ge(s["alpha_ready"], c + 1)
                    bank_free(pe, "slots", c)
                    bank_free(pe, "alphaT", c)
                    for t in range(TT):
                        mm = pe.matmul(bank("slots")[0:NS, 0:D + 1], alpha[:, t, :], xn[:, t, :],
                                       start=(t == 0), stop=(t == TT - 1))
                    filled(mm, "slots")
                    for t in range(TT):
                        mm = pe.transpose(bank("alphaT")[0:NS, P * t:P * t + P], alpha[:, t, :], ident[:])
                    filled(mm, "alphaT")

            def chunk(c, first):
                for k in range(SLOTS):
                    g, st = k // ST, k % ST
                    n = rows_of(st)
                    if st == 0:
                        pe.wait_ge(m_loaded[g], 32 * (c + 1))
                    units = units_of(k)
                    for h in range(HG):
                        if h == 2:
                            if not first:
                                behind(c - 1, k - SHIFT)
                            if k or not first:
                                pv(c, k - 1, 0)
                        need(pe, s["exp_done"], HG * SLOTS * c + HG * k + h - 1)
                        pe.matmul(ps_e[h % 2][0:n, :], kst[0:ROWS, HG * g + h, P * st:P * st + n],
                                  qst[0:ROWS, g, h, :], start=True, stop=True).then_inc(s["qk_ready"], 1)
                        for j, u in units[h:h + 1]:
                            max_unit(u, c, j)
                    if k or not first:
                        pv(c, k - 1, 1)
                    for j, u in units[HG:]:
                        max_unit(u, c, j)
                    if st == 2 and (g or not first):
                        z_columns(c, g - 1)
                    if st == 4 and (g or not first):
                        spread_z(c, g - 1)
                    if max_end(k - 1) is not None:
                        max_rows(NG * c + max_end(k - 1))

            chunk(0, True)
            with pe.Fori(1, NC) as c:
                chunk(c, False)
            for half in range(2):
                pv(NC, -1, half)
            z_columns(NC, -1)
            spread_z(NC, -1)
            for k in range(SLOTS):
                behind(NC - 1, k)
            for name in ("slots", "alphaT"):
                wait_taken(pe, name, NC - 1)

            def transpose_slots(src, ready, done):
                pe.wait_ge(s[ready], 1)
                for k in range(KT):
                    mm = pe.transpose(ps_x[:, NS * k:NS * k + NS], src[:, P * k:P * k + P], ident[0:NS, 0:NS])
                mm.then_inc(s[done], 1)

            def product(out, lhsT, rhs, first=True, last=True):
                for k in range(KT):
                    mm = pe.matmul(out, lhsT[:, k, :], rhs[:, k, :], start=(first and k == 0), stop=(last and k == KT - 1))
                return mm

            transpose_slots(vec, "p_si", "p_siT_ps")
            pe.wait_ge(s["ld_slot"], 16 * len(slot_loads))
            pe.wait_ge(s["p_siT"], 1)
            product(ps_m[0:NS, 0, :], sT, wihT[:, :, 0:2 * D], last=False)
            product(ps_m[0:NS, 0, :], slotT, whhT[:, :, 0:2 * D], first=False)
            product(ps_m[0:NS, 1, 0:D], sT, wihT[:, :, 2 * D:3 * D])
            product(ps_m[0:NS, 2, 0:D], slotT, whhT[:, :, 2 * D:3 * D]).then_inc(s["p_gi"], 1)
            transpose_slots(s_new, "p_snew", "p_snT_ps")
            pe.wait_ge(s["p_snT"], 1)
            product(ps_e[0][0:DQ, 0:NS], wqs, sT)
            product(ps_e[1][0:DQ, 0:NS], wks, sT)
            product(ps_m[0:NS, 3, 0:D], sT, wvs).then_inc(s["p_qkv"], 1)
            pe.wait_ge(s["p_qkT"], 1)
            pe.matmul(ps_x[0:NS, 0:NS], qkT[:, 0, :], qkT[:, 1, :], start=True, stop=True).then_inc(s["p_lg"], 1)
            pe.wait_ge(s["p_attn"], 1)
            pe.transpose(ps_x[0:NS, P:P + NS], att_s, ident[0:NS, 0:NS]).then_inc(s["p_attT_ps"], 1)
            pe.wait_ge(s["p_attT"], 1)
            pe.matmul(ps_m[0:NS, 0, 0:D], att_sT, comm, start=True, stop=True).then_inc(s["p_comm"], 1)
            transpose_slots(y_ln, "p_y", "p_yT_ps")
            pe.wait_ge(s["p_yT"], 1)
            product(ps_m[0:NS, 1, 0:D], sT, wvps).then_inc(s["p_sv"], 1)
            transpose_slots(vec, "p_svb", "p_svT_ps")
            pe.wait_ge(s["p_svT"], 1)
            product(ps_m[0:NS, 2, 0:D], sT, wos).then_inc(s["p_svo"], 1)
            pe.wait_ge(s["p_svo_sb"], 1)
            for c in range(NC):
                if c >= 2:
                    pe.wait_ge(s["out_ready"], c - 1)
                for t in range(TT):
                    mm = pe.matmul(ps_m[:, 2 * (c % 2) + t // 2, D * (t % 2):D * (t % 2) + D],
                                   alphaT[:, CT * c + P * t:CT * c + P * t + P], svo, start=True, stop=True)
                mm.then_inc(s["out_psum"], 1)

        @block.vector
        def _(dve):
            def split(b, kind, i):
                n = block_cols(kind, i)
                parts = part_bufs[b % 2]
                for m in range(KT):
                    dve.wait_ge(s["blk_hi"], KT * b + m + 1)
                    dve.tensor_tensor(rest[:, m, 0:n], q32[:, m, 0:n], parts[:, m, 0, 0:n], ALU.subtract)
                    dve.drain()
                    dve.tensor_copy(parts[:, m, 1, 0:n], rest[:, m, 0:n])
                    dve.drain()
                    dve.tensor_tensor(parts[:, m, 2, 0:n], rest[:, m, 0:n], parts[:, m, 1, 0:n], ALU.subtract)\
                       .then_inc(s["blk_parts"], 1)

            def condition():
                dve.wait_ge(s["ld_cond"], 96)
                scale = E ** -0.5
                dve.tensor_scalar(tau[:, 2:3], tau[:, 0:1], scale, None, ALU.mult)
                dve.tensor_scalar(win_f[:, 2:3], win_f[:, 0:1], -float(W // 2), 0.0, ALU.add, ALU.max)
                dve.tensor_copy(win_f[:, 4:5], win_i[:, 0:1])
                dve.tensor_scalar(rtau[:, 1:2], rtau[:, 0:1], -1.0, None, ALU.mult)
                dve.drain()
                dve.tensor_scalar(qk_bias[:, 0, :], qk_bias[:, 0, :], tau[:, 2:3], None, ALU.mult)
                dve.tensor_scalar(win_f[:, 3:4], win_f[:, 2:3], float(S - W), None, ALU.min)
                dve.tensor_scalar(win_f[:, 5:6], win_f[:, 0:1], -16.0, 0.0, ALU.add, ALU.max)
                dve.tensor_scalar(win_f[:, 6:7], win_f[:, 0:1], 16.0, win_f[:, 4:5], ALU.add, ALU.min)
                dve.tensor_tensor(rtau[:, 0:1], rtau[:, 0:1], rtau[:, 1:2], ALU.max)
                dve.drain()
                dve.tensor_copy(win_i[:, 1:2], win_f[:, 3:4]).then_inc(s["masks_ready"], 1)
                dve.tensor_scalar(rtau[:, 0:1], rtau[:, 0:1], 0.1, None, ALU.add)
                dve.drain()
                dve.tensor_copy(win_f[:, 7:8], win_i[:, 1:2]).then_inc(s["window_start"], 1)
                dve.reciprocal(rtau[:, 1:2], rtau[:, 0:1])
                dve.drain()

            def take_v(st):
                n = rows_of(st)
                dve.wait_ge(s["v_psum"], st + 1)
                v_in, bias, out = (a.rearrange("p (g o j e) -> p o g j e", g=2, o=2, j=HG) for a in
                                   (ps_m[0:n, st % 2, 0:D], bv0[0:n, :], v_sb[0:n, st, :, :].rearrange("p h e -> p (h e)")))
                for odd in range(2):
                    last = dve.tensor_tensor(out[:, odd, :, :, E * odd:E * odd + E], v_in[:, odd], bias[:, odd], ALU.add)
                last.then_inc(s["v_taken"], 1)

            def masks():
                dve.wait_ge(s["ld_const"], N_CONST)
                dve.tensor_scalar(iota_w[:], iota_w[:], win_f[:, 7:8], None, ALU.add)
                dve.tensor_reduce(slot_mean[:], slotT[:], AX.X, ALU.add)
                dve.drain()
                dve.tensor_scalar(slot_mean[:], slot_mean[:], 1.0 / NS, None, ALU.mult).then_inc(s["mean_ready"], 1)
                dve.tensor_scalar(keep[:], iota_w[:], win_f[:, 5:6], None, ALU.is_ge)
                dve.tensor_scalar(gauss[:], iota_w[:], win_f[:, 6:7], None, ALU.is_le)
                dve.tensor_scalar(iota_w[:], iota_w[:], win_f[:, 0:1], None, ALU.subtract)
                dve.drain()
                dve.tensor_tensor(keep[:], keep[:], gauss[:], ALU.mult)
                dve.drain()
                dve.tensor_scalar(neg_mask[:], keep[:], -1.0, BIG, ALU.add, ALU.mult)
                dve.tensor_tensor(iota_w[:], iota_w[:], iota_w[:], ALU.mult).then_inc(s["masks_ready"], 1)

            def stats(src):
                dve.drain()
                for t in range(TT):
                    dve.bn_stats(bst[:, t, :], src[:, t, :])
                dve.drain()
                for t in range(TT):
                    last = dve.bn_aggr(mv[:, t, :], bst[:, t, :])
                last.then_inc(s["var_ready"], 1)

            def normal(src, n):
                dve.wait_ge(s["rstd_ready"], n)
                for t in range(TT):
                    last = dve.tensor_scalar(xn[:, t, 0:D], src[:, t, :], mv[:, t, 0:1], rstd[:, t:t + 1],
                                             ALU.subtract, ALU.mult)
                last.then_inc(s["xn_ready"], 1)

            def take_max(u, n1, banks=2):
                t, h, q = u // (QUARTERS * HG), (u // QUARTERS) % HG, u % QUARTERS
                dve.wait_ge(s["max_ready"], UNITS * n1 + u + 1)
                col = TT * h + t
                bank_of = u % 2 if banks == 2 else (UNITS * n1 + u) % banks
                dve.tensor_reduce(mx[:, q, col:col + 1], ps_m[:, bank_of, 0:SPLIT], AX.X, ALU.max)\
                   .then_inc(s["max_taken"], 1)

            def max_columns():
                dve.drain()
                dve.tensor_reduce(mxc[:], mx[:].rearrange("p q c -> p c q"), AX.X, ALU.max).then_inc(s["mx_ready"], 1)
                dve.drain()

            def max_out(n1):
                dve.wait_ge(s["mT_ready"], n1 + 1)
                dve.tensor_scalar(mrow[:, 0, :], ps_x[0:HG * TT, 0:P], -1.0, None, ALU.mult)
                dve.drain()
                dve.scalar_tensor_tensor(out=mrow[:, 1, :], in0=ps_x[0:HG * TT, 0:P], scalar=-1.0, in1=mrow[:, 0, :],
                                         op0=ALU.mult, op1=ALU.subtract).then_inc(s["mrow_ready"], 1)


            for kind, i in START:
                if kind in "KQ":
                    split(BLOCKS.index((kind, i)), kind, i)
                if kind == "L":
                    x_chunk = (xa, xb)[i % 2]
                    dve.wait_ge(x_start[i % 2], 16 * (i // 2 + 1))
                    stats(x_chunk)
                    if i:
                        dve.wait_ge(s["xnT_psum"], i)
                    normal(x_chunk, i + 1)
                if kind == "V":
                    if i == 0:
                        dve.wait_ge(s["v_ones_set"], 1)
                        dve.wait_ge(s["ld_early"], 32)
                    take_v(i)
                if kind == "C":
                    condition()
                if kind == "M":
                    masks()
                    dve.wait_ge(s["hb_psum"], 1)
                    dve.tensor_tensor(hbias[:], ps_x[:, 0:1], b1[:], ALU.add).then_inc(s["hb_ready"], 1)

            for v in range(UNITS + LEAD):
                take_max(v % UNITS, v // UNITS, banks=4)
                if v == UNITS - 1:
                    max_columns()
                if v == UNITS + 4:
                    max_out(0)

            def invert_z(c, g):
                dve.wait_ge(s["z_cols"], NG * c + g + 1)
                dve.reciprocal(z_inv[:], ps_x[:, 0:TT * HG]).then_inc(s["z_inverted"], 1)

            def normalise(c, g):
                dve.wait_ge(s["z_ready"], NG * c + g + 1)
                pair, odd = g % NG // 2, g % 2
                last = dve.tensor_tensor(att_odd if odd else attc[:, pair, :], o_raw[:], ps_x[:], ALU.mult)
                if odd:
                    dve.drain()
                    last = dve.tensor_tensor(attc[:, pair, :], attc[:, pair, :], att_odd, ALU.add)
                last.then_inc(s["att_ready"], 1)

            def take_experts(i, c):
                t, j = i // 4, i % 4
                for e in (2 * j, 2 * j + 1):
                    dve.drain()
                    if e % 2 == 0:
                        wait_filled(dve, f"e{i}", c)
                    last = dve.scalar_tensor_tensor(out=xb[:, t, :], in0=bank(f"e{i}")[:, D * (e % 2):D * (e % 2) + D],
                                                    scalar=hot8[:, t, e:e + 1], in1=(xb if e else xa)[:, t, :],
                                                    op0=ALU.mult, op1=ALU.add)
                taken(last, f"e{i}")

            def behind(c, k):
                if k in (6, 7):
                    i = k - 6
                    dve.wait_ge(s["xres_ready"], c + 1)
                    wait_filled(dve, f"y{i}", c)
                    taken(dve.tensor_tensor(xa[:, 2 * i:2 * i + 2, :], xres[:, 2 * i:2 * i + 2, :],
                                            bank(f"y{i}").rearrange("p (a d) -> p a d", a=2), ALU.add), f"y{i}")
                if k == 7:
                    stats(xa)
                if k == 8:
                    normal(xa, NC + 3 * c + 1)
                if k == 11:
                    wait_filled(dve, "router", c)
                    taken(dve.tensor_tensor(lg8[:], bank("router")[:, 0:TT * NX].rearrange("p (t e) -> p t e", t=TT),
                                            rb[:].unsqueeze(1).broadcast_to((P, TT, NX)), ALU.add), "router")
                    dve.drain()
                    dve.tensor_reduce(st4[:, 2, :], lg8[:], AX.X, ALU.max)
                    dve.drain()
                    top = st4[:, 2, :].unsqueeze(2).broadcast_to((P, TT, NX))
                    dve.tensor_tensor(hot8[:], lg8[:], top, ALU.is_equal)
                    dve.drain()
                    dve.tensor_tensor(lg8[:], lg8[:], top, ALU.subtract).then_inc(s["lg8_ready"], 1)
                    dve.tensor_tensor(hot8[:], hot8[:], rank[:].unsqueeze(1).broadcast_to((P, TT, NX)), ALU.mult)
                    dve.drain()
                    dve.tensor_reduce(st4[:, 3, :], hot8[:], AX.X, ALU.max)
                    dve.drain()
                    dve.tensor_tensor(hot8[:], hot8[:], st4[:, 3, :].unsqueeze(2).broadcast_to((P, TT, NX)), ALU.is_equal)
                if k == 12:
                    dve.wait_ge(s["ex8_ready"], c + 1)
                    dve.tensor_reduce(st4[:, 4, :], ex8[:], AX.X, ALU.add)
                    dve.drain()
                    dve.reciprocal(st4[:, 5, :], st4[:, 4, :])
                    dve.drain()
                    dve.tensor_tensor(hot8[:], hot8[:], st4[:, 5, :].unsqueeze(2).broadcast_to((P, TT, NX)), ALU.mult)\
                       .then_inc(s["gate_ready"], 1)
                if 12 <= k < 20:
                    take_experts(k - 12, c)
                if k == 20:
                    for i, dst in enumerate((xb[:, 0:2, :], xa[:, 2:4, :])):
                        dve.drain()
                        wait_filled(dve, f"gb{i}", c)
                        taken(dve.tensor_tensor(dst, dst, bank(f"gb{i}").rearrange("p (a d) -> p a d", a=2), ALU.add),
                              f"gb{i}")
                if 21 <= k < 29:
                    take_experts(k - 13, c)
                if k == 28:
                    stats(xb)
                if k == 29:
                    normal(xb, NC + 3 * c + 2)
                if k == 32:
                    for i in range(2):
                        wait_filled(dve, f"score{i}", c)
                        taken(dve.tensor_tensor(work[:, 2 * i:2 * i + 2, :],
                                                bank(f"score{i}").rearrange("p (a w) -> p a w", a=2),
                                                keep[:].unsqueeze(1).broadcast_to((P, 2, W)), ALU.mult), f"score{i}")
                    dve.drain()
                    dve.tensor_tensor(work[:], work[:], neg_mask[:].unsqueeze(1).broadcast_to((P, TT, W)), ALU.add)
                    dve.drain()
                    dve.tensor_reduce(st4[:, 6, :], work[:], AX.X, ALU.max)
                    dve.drain()
                    dve.tensor_scalar(st4[:, 0, :], st4[:, 6, :], -BIG, -1.0, ALU.max, ALU.mult)\
                       .then_inc(s["negmax_ready"], 1)
                if k == 33:
                    dve.wait_ge(s["rowsum_ready"], c + 1)
                    dve.scalar_tensor_tensor(out=rowsum[:], in0=tail[:], scalar=float(S - W), in1=rowsum[:],
                                             op0=ALU.mult, op1=ALU.add)
                    dve.drain()
                    dve.reciprocal(st4[:, 6, :], rowsum[:])
                    dve.drain()
                    for t in range(TT):
                        last = dve.scalar_tensor_tensor(out=work[:, t, :], in0=work2[:, t, :], scalar=st4[:, 6, t:t + 1],
                                                        in1=gauss[:], op0=ALU.mult, op1=ALU.mult)
                    last.then_inc(s["a_ready"], 1)
                if k == 37:
                    wait_taken(dve, "z0", c)
                    wait_taken(dve, "z1", c)
                    dve.tensor_tensor(xres[:], xb[:], work[:], ALU.add).then_inc(s["x3_ready"], 1)
                    stats(xres)
                if k == 38:
                    normal(xres, NC + 3 * c + 3)
                if k == 42:
                    wait_filled(dve, "logits", c)
                    taken(dve.tensor_tensor(lg, bank("logits")[:, 0:TT * NS].rearrange("p (t n) -> p t n", t=TT),
                                            b2[:].unsqueeze(1).broadcast_to((P, TT, NS)), ALU.add), "logits")
                    dve.drain()
                    dve.tensor_scalar(lg, lg, rtau[:, 1:2], None, ALU.mult)
                    dve.drain()
                    for t in range(TT):
                        dve.max(top8[:, t, :], lg[:, t, :])
                    dve.drain()
                    dve.tensor_scalar(st4[:, 1, :], top8[:, :, 0], -1.0, None, ALU.mult).then_inc(s["lg_ready"], 1)
                    for t in range(TT):
                        dve.match_replace(lgr[:, t, :], top8[:, t, :], lg[:, t, :], -3.0e38)
                    dve.drain()
                    dve.tensor_tensor(lgr, lg, lgr, ALU.not_equal)
                if k == 43:
                    dve.drain()
                    dve.wait_ge(s["elg_ready"], c + 1)
                    dve.tensor_tensor(elg, elg, lgr, ALU.mult)
                    dve.drain()
                    dve.tensor_reduce(st4[:, 4, :], elg, AX.X, ALU.add)
                    dve.drain()
                    dve.reciprocal(st4[:, 5, :], st4[:, 4, :])
                    dve.drain()
                    dve.tensor_tensor(alpha, elg, st4[:, 5, :].unsqueeze(2).broadcast_to((P, TT, NS)), ALU.mult)\
                       .then_inc(s["alpha_ready"], 1)
                if k == 45:
                    wait_filled(dve, "slots", c)
                    taken(dve.tensor_tensor(slot_acc[:], slot_acc[:], bank("slots")[0:NS, 0:D + 1], ALU.add), "slots")
                    dve.drain()

            def chunk(c, first):
                for k in range(SLOTS):
                    g, st = k // ST, k % ST
                    if st == 3 and (g or not first):
                        invert_z(c, g - 1)
                    if st == 5 and (g or not first):
                        if g == 1 and not first:
                            wait_filled(dve, "y1", c - 1)
                        normalise(c, g - 1)
                    if not first:
                        behind(c - 1, k - SHIFT)
                    for j, u in units_of(k):
                        take_max(u, NG * c + j)
                    if max_end(k - 1) is not None:
                        j = max_end(k - 1)
                        need(dve, m_loaded[(j - 1) % NG], 32 * (c + (j - 1) // NG + 1))
                        max_out(NG * c + j)
                    if max_end(k) is not None:
                        max_columns()

            chunk(0, True)
            with dve.Fori(1, NC) as c:
                chunk(c, False)
            invert_z(NC, -1)
            normalise(NC, -1)
            for k in range(SLOTS):
                behind(NC - 1, k)

            dve.memset(alphaT_raw[NS:NS + 1, :], 1.0)
            dve.wait_ge(s["ld_slot"], 16 * len(slot_loads))
            dve.tensor_scalar(small[:, 0:1], slot_acc[:, D:D + 1], 1e-8, None, ALU.add)
            dve.drain()
            dve.reciprocal(small[:, 1:2], small[:, 0:1])
            dve.drain()
            dve.tensor_scalar(vec, slot_acc[:, 0:D], small[:, 1:2], None, ALU.mult).then_inc(s["p_si"], 1)
            dve.tensor_tensor(b_ih[:, 0:2 * D], b_ih[:, 0:2 * D], b_hh[:, 0:2 * D], ALU.add)

            def copy_T(ready, done):
                dve.wait_ge(s[ready], 1)
                dve.tensor_copy(sT, ps_x[:, 0:KT * NS].rearrange("p (k n) -> p k n", k=KT)).then_inc(s[done], 1)

            copy_T("p_siT_ps", "p_siT")
            dve.wait_ge(s["p_gi"], 1)
            dve.tensor_tensor(rz, ps_m[0:NS, 0, :], b_ih[:, 0:2 * D], ALU.add).then_inc(s["p_rz"], 1)
            dve.tensor_tensor(gate_n, ps_m[0:NS, 1, 0:D], b_ih[:, 2 * D:3 * D], ALU.add)
            dve.tensor_tensor(hid_n, ps_m[0:NS, 2, 0:D], b_hh[:, 2 * D:3 * D], ALU.add)
            dve.wait_ge(s["p_sig"], 1)
            dve.drain()
            dve.tensor_tensor(hid_n, hid_n, rz[:, 0:D], ALU.mult)
            dve.drain()
            dve.tensor_tensor(gate_n, gate_n, hid_n, ALU.add).then_inc(s["p_npre"], 1)
            dve.wait_ge(s["p_n"], 1)
            dve.tensor_tensor(s_new, slot0, gate_n, ALU.subtract)
            dve.drain()
            dve.tensor_tensor(s_new, s_new, rz[:, D:2 * D], ALU.mult)
            dve.drain()
            dve.tensor_tensor(s_new, s_new, gate_n, ALU.add).then_inc(s["p_snew"], 1)
            copy_T("p_snT_ps", "p_snT")
            dve.wait_ge(s["p_qkv"], 1)
            for i in range(2):
                dve.tensor_scalar(qkT[:, i, :], ps_e[i][0:DQ, 0:NS], b_qk[:, i:i + 1], None, ALU.add)
            dve.tensor_tensor(comm, ps_m[0:NS, 3, 0:D], b_v, ALU.add).then_inc(s["p_qkT"], 1)
            dve.wait_ge(s["p_lg"], 1)
            dve.tensor_reduce(small[:, 4:5], ps_x[0:NS, 0:NS], AX.X, ALU.max)
            dve.drain()
            dve.tensor_scalar(small[:, 2:3], small[:, 4:5], -(DQ ** -0.5), None, ALU.mult).then_inc(s["p_nmax"], 1)
            dve.wait_ge(s["p_exp"], 1)
            dve.reciprocal(small[:, 5:6], small[:, 3:4])
            dve.drain()
            dve.tensor_scalar(att_s, att_s, small[:, 5:6], None, ALU.mult).then_inc(s["p_attn"], 1)
            dve.wait_ge(s["p_attT_ps"], 1)
            dve.tensor_copy(att_sT, ps_x[0:NS, P:P + NS]).then_inc(s["p_attT"], 1)
            dve.wait_ge(s["p_comm"], 1)
            dve.tensor_tensor(y_ln, s_new, ps_m[0:NS, 0, 0:D], ALU.add)
            dve.drain()
            dve.bn_stats(bst[0:NS, 0, :], y_ln)
            dve.drain()
            dve.bn_aggr(small[:, 7:9], bst[0:NS, 0, :]).then_inc(s["p_var"], 1)
            dve.wait_ge(s["p_rstd"], 1)
            dve.tensor_scalar(y_ln, y_ln, small[:, 7:8], small[:, 10:11], ALU.subtract, ALU.mult)
            dve.drain()
            dve.tensor_tensor(y_ln, y_ln, ln_g, ALU.mult)
            dve.drain()
            dve.tensor_tensor(y_ln, y_ln, ln_b, ALU.add).then_inc(s["p_y"], 1)
            copy_T("p_yT_ps", "p_yT")
            dve.wait_ge(s["p_sv"], 1)
            dve.tensor_tensor(vec, ps_m[0:NS, 1, 0:D], b_vp, ALU.add).then_inc(s["p_svb"], 1)
            copy_T("p_svT_ps", "p_svT")
            dve.wait_ge(s["p_svo"], 1)
            dve.tensor_copy(svo[0:NS, :], ps_m[0:NS, 2, 0:D]).then_inc(s["p_svo_sb"], 1)
            dve.wait_ge(s["x_end_loaded"], 16)
            for c in range(NC):
                dve.wait_ge(s["out_psum"], c + 1)
                tok = x_end[:, TT * c:TT * c + TT, :].rearrange("p (b a) d -> p b (a d)", b=2)
                dve.tensor_tensor(tok, tok, ps_m[:, 2 * (c % 2):2 * (c % 2) + 2, :], ALU.add).then_inc(s["out_ready"], 1)


def kernel(**inputs):
    import numpy as np
    import concourse.bacc as bacc
    from concourse import mybir as _mybir
    from concourse.bass_utils import run_bass_kernel_spmd

    x = {k: np.asarray(v) for k, v in inputs.items()}
    z_pick = np.zeros((P, 2, HG), np.float32)
    for h in range(HG):
        z_pick[32 * h + E, 0, h] = 1.0
        z_pick[32 * h, 1, h] = 1.0
    arrays = {
        "x": x["x"][0], "ctxT": x["ctx_1024"][0].T, "condB_tau": x["condB_tau"], "fside": x["fside_BxS2_0"][0],
        "condB_pt": x["condB_pt"], "lenS2": x["_lenS2"],
        "L0_WqT": x["L0_xcond_Wq"].T, "L0_WkT": x["L0_xcond_Wk"].T, "L0_WvT": x["L0_xcond_Wv"].T,
        "L0_WoT": x["L0_xcond_Wo"].T, "L0_bq": x["L0_xcond_bq"], "L0_bk": x["L0_xcond_bk"],
        "L0_bv": x["L0_xcond_bv"], "L0_bo": x["L0_xcond_bo"],
        "router_wT": x["L0_ffn_router_w"].T, "router_b": x["L0_ffn_router_b"],
        "expert_wT": x["L0_ffn_expert_w"].transpose(2, 0, 1).reshape(KT, P, NX * D), "expert_b": x["L0_ffn_expert_b"],
        "L1_W_aT": x["L1_xcond_W_a"].T, "L1_W_cT": x["L1_xcond_W_c"].T,
        "slot_init": x["L1_ffn_slot_init"], "slot_initT": x["L1_ffn_slot_init"].T,
        "w1": x["L1_ffn_w1"], "b1": x["L1_ffn_b1"], "w2": x["L1_ffn_w2"], "b2": x["L1_ffn_b2"],
        "L1_tau": x["L1_ffn_tau"], "WihT": x["L1_ffn_Wih"].T, "WhhT": x["L1_ffn_Whh"].T,
        "bih": x["L1_ffn_bih"], "bhh": x["L1_ffn_bhh"], "wq": x["L1_ffn_wq"], "bq": x["L1_ffn_bq"],
        "wk": x["L1_ffn_wk"], "bk": x["L1_ffn_bk"], "wv": x["L1_ffn_wv"], "bv": x["L1_ffn_bv"],
        "ln_g": x["L1_ffn_ln_g"], "ln_b": x["L1_ffn_ln_b"], "wvp": x["L1_ffn_wvp"], "bvp": x["L1_ffn_bvp"],
        "wo": x["L1_ffn_wo"], "L1_bo": x["L1_ffn_bo"],
        "c_ident": np.eye(P, dtype=np.float32), "c_zpick": z_pick,
        "c_iota": np.arange(W, dtype=np.float32), "c_rank": np.arange(NX, 0, -1).astype(np.float32),
    }
    arrays = {k: np.ascontiguousarray(a) for k, a in arrays.items()}
    nc = bacc.Bacc("TRN2", target_bir_lowering=False, num_devices=1)
    io = {k: nc.dram_tensor(f"in_{k}", a.shape, _mybir.dt.from_np(a.dtype), kind="ExternalInput").ap() for k, a in arrays.items()}
    io["out"] = nc.dram_tensor("out_0", (T, D), _mybir.dt.float32, kind="ExternalOutput").ap()
    build(nc, io)
    r = run_bass_kernel_spmd(nc, [{f"in_{k}": a for k, a in arrays.items()}], core_ids=[0])
    return r.results[0]["out_0"].reshape(1, T, D)
```
